# Optimizing a Trainium2 kernel written in Bass

```python
import numpy as np
import jax
import jax.numpy as jnp

def _softmax(x, axis=-1):
    return jax.nn.softmax(x, axis=axis)

def _gelu(x):
    return jax.nn.gelu(x, approximate=True)

def _silu(x):
    return jax.nn.silu(x)

def _sigmoid(x):
    return jax.nn.sigmoid(x)

def _layernorm(x, axis=-1, eps=1e-05):
    m = jnp.mean(x, axis=axis, keepdims=True)
    v = jnp.var(x, axis=axis, keepdims=True)
    return (x - m) / jnp.sqrt(v + eps)

def _scatter_add(tgt, idx, src, axis=0):
    return tgt.at[idx].add(src)

def _segment_sum(src, seg, n):
    return jax.ops.segment_sum(src, seg, n)
kernel_name = 'mk_vit_tower_postln_d2_tok_img2048_r4_498b98'

def setup_inputs(seed: int=0):
    np.random.seed(seed)
    _w = jnp.asarray

    def _rec_inputs():
        import jax
        import jax.numpy as jnp
        _rk = jax.random.key(seed)
        x = -0.00178296 + 0.498989 * jax.random.normal(jax.random.fold_in(_rk, 1), (16, 256, 64, 2), jnp.float32)
        return x
    x = _rec_inputs()

    def _L0_tok_setup():
        import jax, jax.numpy as jnp
        import numpy as np
        H, N, CCH, LLEN = (256, 64, 1, 512)
        key = jax.random.key(seed)
        k1, k2 = jax.random.split(key, 2)
        log_dt = jax.random.uniform(k1, (H,), jnp.float32, float(np.log(0.001)), float(np.log(0.1)))
        C = 0.5 * jax.random.normal(k2, (CCH, H, N, 2), jnp.float32)
        log_w_real = jnp.full((H, N), float(np.log(0.5)), jnp.float32)
        w_imag = jnp.broadcast_to(np.pi * jnp.arange(N, dtype=jnp.float32), (H, N)) + jnp.zeros((H, N), jnp.float32)
        return {'C': C, 'log_dt': log_dt, 'log_w_real': log_w_real, 'w_imag': w_imag, 'L': LLEN}
    _L0_tok_all = _L0_tok_setup()
    _L0_tok_in = {k: v for k, v in _L0_tok_all.items() if k in ('log_dt', 'log_w_real', 'w_imag')}
    del _L0_tok_all

    def _L0_attn_setup():
        import jax, jax.numpy as jnp
        import numpy as np
        B, S, HID = (1, 512, 512)
        NH, NKV, HD = (16, 4, 128)
        WIN = 256
        THETA = 10000.0

        def _rotate_half(x):
            h = x.shape[-1] // 2
            return jnp.concatenate((-x[..., h:], x[..., :h]), axis=-1)

        def _rope_cos_sin(seq_len, dtype):
            inv_freq = 1.0 / THETA ** (jnp.arange(0, HD, 2, dtype=jnp.float32) / HD)
            t = jnp.arange(seq_len, dtype=jnp.float32)
            freqs = jnp.outer(t, inv_freq)
            emb = jnp.concatenate((freqs, freqs), axis=-1)
            return (jnp.cos(emb).astype(dtype)[None, None], jnp.sin(emb).astype(dtype)[None, None])
        key = jax.random.key(seed)
        ks = jax.random.split(key, 5)
        return {'hidden_states': jax.random.normal(ks[0], (B, S, HID), dtype=jnp.float32), 'w_q': jax.random.normal(ks[1], (HID, NH * HD), dtype=jnp.float32) * 0.02, 'w_k': jax.random.normal(ks[2], (HID, NKV * HD), dtype=jnp.float32) * 0.02, 'w_v': jax.random.normal(ks[3], (HID, NKV * HD), dtype=jnp.float32) * 0.02, 'w_o': jax.random.normal(ks[4], (NH * HD, HID), dtype=jnp.float32) * 0.02}
    _L0_attn_all = _L0_attn_setup()
    _L0_attn_in = {k: v for k, v in _L0_attn_all.items() if k in ('w_q', 'w_k', 'w_v', 'w_o')}
    del _L0_attn_all

    def _L0_ffn_setup():
        import jax, jax.numpy as jnp
        import numpy as np
        EPS = 1e-05

        def _ternary_weight(w, eps=EPS):
            alpha = jnp.maximum(jnp.mean(jnp.abs(w)), eps)
            return jnp.clip(jnp.round(w / alpha), -1.0, 1.0) * alpha

        def _absmax_act(x, eps=EPS):
            scale = jnp.maximum(jnp.max(jnp.abs(x), axis=-1, keepdims=True), eps) / 127.0
            return jnp.clip(jnp.round(x / scale), -128.0, 127.0) * scale
        key = jax.random.key(seed)
        k1, k2, k3 = jax.random.split(key, 3)
        B, S, D_IN, D_OUT = (4, 2048, 512, 512)
        x = jax.random.normal(k1, (B, S, D_IN), dtype=jnp.float32)
        bound_w = 1.0 / np.sqrt(D_IN)
        weight = jax.random.uniform(k2, (D_OUT, D_IN), dtype=jnp.float32, minval=-bound_w, maxval=bound_w)
        bias = jax.random.uniform(k3, (D_OUT,), dtype=jnp.float32, minval=-bound_w, maxval=bound_w)
        return {'x': x, 'weight': weight, 'bias': bias}
    _L0_ffn_all = _L0_ffn_setup()
    _L0_ffn_in = {k: v for k, v in _L0_ffn_all.items() if k in ('weight', 'bias')}
    del _L0_ffn_all

    def _L1_attn_setup():
        import jax, jax.numpy as jnp
        import numpy as np
        B, T, HID = (2, 512, 512)
        H, HKV = (16, 4)
        D = HID // H
        G = H // HKV
        ROPE_BASE = 1000000.0
        DTYPE = jnp.bfloat16

        def rotate_half(x):
            half = x.shape[-1] // 2
            return jnp.concatenate([-x[..., half:], x[..., :half]], axis=-1)
        key = jax.random.key(seed)
        ks = jax.random.split(key, 8)
        s = 0.02
        return {'x': jax.random.normal(ks[0], (B, T, HID), dtype=DTYPE), 'Wq': (jax.random.normal(ks[1], (HID, H * D), dtype=jnp.float32) * s).astype(DTYPE), 'bq': jnp.zeros((H * D,), dtype=DTYPE), 'Wk': (jax.random.normal(ks[2], (HID, HKV * D), dtype=jnp.float32) * s).astype(DTYPE), 'bk': jnp.zeros((HKV * D,), dtype=DTYPE), 'Wv': (jax.random.normal(ks[3], (HID, HKV * D), dtype=jnp.float32) * s).astype(DTYPE), 'bv': jnp.zeros((HKV * D,), dtype=DTYPE), 'Wo': (jax.random.normal(ks[4], (H * D, HID), dtype=jnp.float32) * s).astype(DTYPE)}
    _L1_attn_all = _L1_attn_setup()
    _L1_attn_in = {k: v for k, v in _L1_attn_all.items() if k in ('Wq', 'bq', 'Wk', 'bk', 'Wv', 'bv', 'Wo')}
    del _L1_attn_all

    def _L1_ffn_setup():
        import jax, jax.numpy as jnp
        import numpy as np
        B, S, D = (4, 512, 512)
        E, F, K = (8, 256, 2)
        SF = 256
        EPS = 1e-06

        def _rmsnorm(x, w, eps=EPS):
            var = jnp.mean(x * x, axis=-1, keepdims=True)
            return x * jax.lax.rsqrt(var + eps) * w
        key = jax.random.key(seed)
        ks = jax.random.split(key, 9)
        g = lambda k, shape, scale: jax.random.normal(k, shape, jnp.float32) * scale
        return {'x': g(ks[0], (B, S, D), 1.0), 'rms_weight': jnp.ones((D,), jnp.float32), 'router_w': g(ks[1], (D, E), 0.02), 'w_gate': g(ks[2], (E, D, F), 0.02), 'w_up': g(ks[3], (E, D, F), 0.02), 'w_down': g(ks[4], (E, F, D), 0.02), 'sw_gate': g(ks[5], (D, SF), 0.02), 'sw_up': g(ks[6], (D, SF), 0.02), 'sw_down': g(ks[7], (SF, D), 0.02)}
    _L1_ffn_all = _L1_ffn_setup()
    _L1_ffn_in = {k: v for k, v in _L1_ffn_all.items() if k in ('rms_weight', 'router_w', 'w_gate', 'w_up', 'w_down', 'sw_gate', 'sw_up', 'sw_down')}
    del _L1_ffn_all
    return {'x': x, 'L0_tok_log_dt': _L0_tok_in['log_dt'], 'L0_tok_log_w_real': _L0_tok_in['log_w_real'], 'L0_tok_w_imag': _L0_tok_in['w_imag'], 'L0_attn_w_q': _L0_attn_in['w_q'], 'L0_attn_w_k': _L0_attn_in['w_k'], 'L0_attn_w_v': _L0_attn_in['w_v'], 'L0_attn_w_o': _L0_attn_in['w_o'], 'L0_ffn_weight': _L0_ffn_in['weight'], 'L0_ffn_bias': _L0_ffn_in['bias'], 'L1_attn_Wq': _L1_attn_in['Wq'], 'L1_attn_bq': _L1_attn_in['bq'], 'L1_attn_Wk': _L1_attn_in['Wk'], 'L1_attn_bk': _L1_attn_in['bk'], 'L1_attn_Wv': _L1_attn_in['Wv'], 'L1_attn_bv': _L1_attn_in['bv'], 'L1_attn_Wo': _L1_attn_in['Wo'], 'L1_ffn_rms_weight': _L1_ffn_in['rms_weight'], 'L1_ffn_router_w': _L1_ffn_in['router_w'], 'L1_ffn_w_gate': _L1_ffn_in['w_gate'], 'L1_ffn_w_up': _L1_ffn_in['w_up'], 'L1_ffn_w_down': _L1_ffn_in['w_down'], 'L1_ffn_sw_gate': _L1_ffn_in['sw_gate'], 'L1_ffn_sw_up': _L1_ffn_in['sw_up'], 'L1_ffn_sw_down': _L1_ffn_in['sw_down']}

def reference(x, L0_tok_log_dt, L0_tok_log_w_real, L0_tok_w_imag, L0_attn_w_q, L0_attn_w_k, L0_attn_w_v, L0_attn_w_o, L0_ffn_weight, L0_ffn_bias, L1_attn_Wq, L1_attn_bq, L1_attn_Wk, L1_attn_bk, L1_attn_Wv, L1_attn_bv, L1_attn_Wo, L1_ffn_rms_weight, L1_ffn_router_w, L1_ffn_w_gate, L1_ffn_w_up, L1_ffn_w_down, L1_ffn_sw_gate, L1_ffn_sw_up, L1_ffn_sw_down):
    import jax
    import jax.numpy as jnp

    def _L0_tok_ref(C, log_dt, log_w_real, w_imag, L):
        import jax, jax.numpy as jnp
        import numpy as np
        H, N, CCH, LLEN = (256, 64, 1, 512)
        dt = jnp.exp(log_dt)
        Cc = C[..., 0] + 1j * C[..., 1]
        w = -jnp.exp(log_w_real) + 1j * w_imag
        dtA = w * dt[:, None]
        K = dtA[:, :, None] * jnp.arange(L)
        Cm = Cc * (jnp.exp(dtA) - 1.0) / w
        K = jnp.einsum('chn,hnl->chl', Cm, jnp.exp(K))
        return 2 * K.real

    def _L0_attn_ref(hidden_states, w_q, w_k, w_v, w_o):
        import jax, jax.numpy as jnp
        import numpy as np
        B, S, HID = (1, 512, 512)
        NH, NKV, HD = (16, 4, 128)
        WIN = 256
        THETA = 10000.0

        def _rotate_half(x):
            h = x.shape[-1] // 2
            return jnp.concatenate((-x[..., h:], x[..., :h]), axis=-1)

        def _rope_cos_sin(seq_len, dtype):
            inv_freq = 1.0 / THETA ** (jnp.arange(0, HD, 2, dtype=jnp.float32) / HD)
            t = jnp.arange(seq_len, dtype=jnp.float32)
            freqs = jnp.outer(t, inv_freq)
            emb = jnp.concatenate((freqs, freqs), axis=-1)
            return (jnp.cos(emb).astype(dtype)[None, None], jnp.sin(emb).astype(dtype)[None, None])
        b, s, _ = hidden_states.shape
        dt = hidden_states.dtype
        q = (hidden_states @ w_q).reshape(b, s, NH, HD).transpose(0, 2, 1, 3)
        k = (hidden_states @ w_k).reshape(b, s, NKV, HD).transpose(0, 2, 1, 3)
        v = (hidden_states @ w_v).reshape(b, s, NKV, HD).transpose(0, 2, 1, 3)
        cos, sin = _rope_cos_sin(s, dt)
        q = q * cos + _rotate_half(q) * sin
        k = k * cos + _rotate_half(k) * sin
        rep = NH // NKV
        k = jnp.repeat(k, rep, axis=1)
        v = jnp.repeat(v, rep, axis=1)
        qpos = jnp.arange(s) + (s - s)
        kpos = jnp.arange(s)
        dist = qpos[:, None] - kpos[None, :]
        bad = (dist < 0) | (dist > WIN)
        bias = jnp.where(bad, jnp.finfo(dt).min, jnp.zeros((), dt))[None, None]
        scores = jnp.einsum('bhqd,bhkd->bhqk', q, k) / jnp.sqrt(jnp.asarray(HD, dt))
        probs = jax.nn.softmax(scores + bias, axis=-1)
        out = jnp.einsum('bhqk,bhkd->bhqd', probs, v)
        out = out.transpose(0, 2, 1, 3).reshape(b, s, NH * HD)
        return out @ w_o

    def _L0_ffn_ref(x, weight, bias):
        import jax, jax.numpy as jnp
        import numpy as np
        EPS = 1e-05

        def _ternary_weight(w, eps=EPS):
            alpha = jnp.maximum(jnp.mean(jnp.abs(w)), eps)
            return jnp.clip(jnp.round(w / alpha), -1.0, 1.0) * alpha

        def _absmax_act(x, eps=EPS):
            scale = jnp.maximum(jnp.max(jnp.abs(x), axis=-1, keepdims=True), eps) / 127.0
            return jnp.clip(jnp.round(x / scale), -128.0, 127.0) * scale
        q_w = _ternary_weight(weight).astype(x.dtype)
        q_x = _absmax_act(x)
        return jnp.einsum('bsi,oi->bso', q_x, q_w) + bias.astype(x.dtype)

    def _L1_attn_ref(x, Wq, bq, Wk, bk, Wv, bv, Wo):
        import jax, jax.numpy as jnp
        import numpy as np
        B, T, HID = (2, 512, 512)
        H, HKV = (16, 4)
        D = HID // H
        G = H // HKV
        ROPE_BASE = 1000000.0
        DTYPE = jnp.bfloat16

        def rotate_half(x):
            half = x.shape[-1] // 2
            return jnp.concatenate([-x[..., half:], x[..., :half]], axis=-1)
        b, t, _ = x.shape
        dt = x.dtype
        half = D // 2
        inv_freq = 1.0 / ROPE_BASE ** (jnp.arange(half, dtype=jnp.float32) / half)
        ang = jnp.outer(jnp.arange(t, dtype=jnp.float32), inv_freq)
        cos = jnp.concatenate([jnp.cos(ang), jnp.cos(ang)], axis=-1).astype(dt)[None, :, None, :]
        sin = jnp.concatenate([jnp.sin(ang), jnp.sin(ang)], axis=-1).astype(dt)[None, :, None, :]
        q = (x @ Wq + bq).reshape(b, t, H, D)
        k = (x @ Wk + bk).reshape(b, t, HKV, D)
        v = (x @ Wv + bv).reshape(b, t, HKV, D)
        q = q * cos + rotate_half(q) * sin
        k = k * cos + rotate_half(k) * sin
        qg = q.reshape(b, t, HKV, G, D)
        scale = D ** (-0.5)
        attn = jnp.einsum('bikgd,bjkd->bkgij', qg, k) * scale
        causal = jnp.tril(jnp.ones((t, t), dtype=bool))
        attn = jnp.where(causal, attn, jnp.finfo(dt).min)
        p = jax.nn.softmax(attn.astype(jnp.float32), axis=-1).astype(dt)
        out = jnp.einsum('bkgij,bjkd->bikgd', p, v).reshape(b, t, H * D)
        return out @ Wo

    def _L1_ffn_ref(x, rms_weight, router_w, w_gate, w_up, w_down, sw_gate, sw_up, sw_down):
        import jax, jax.numpy as jnp
        import numpy as np
        B, S, D = (4, 512, 512)
        E, F, K = (8, 256, 2)
        SF = 256
        EPS = 1e-06

        def _rmsnorm(x, w, eps=EPS):
            var = jnp.mean(x * x, axis=-1, keepdims=True)
            return x * jax.lax.rsqrt(var + eps) * w
        b, s, d = x.shape
        e = router_w.shape[1]
        h = _rmsnorm(x, rms_weight)
        ht = h.reshape(-1, d)
        t = ht.shape[0]
        logits = ht @ router_w
        probs = jax.nn.softmax(logits, axis=-1)
        topv, topi = jax.lax.top_k(probs, K)
        topv = topv / jnp.sum(topv, axis=-1, keepdims=True)
        w_dense = jnp.zeros((t, e), ht.dtype).at[jnp.arange(t)[:, None], topi].set(topv)
        g = jnp.einsum('td,edf->tef', ht, w_gate)
        u = jnp.einsum('td,edf->tef', ht, w_up)
        eo = jnp.einsum('tef,efd->ted', jax.nn.silu(g) * u, w_down)
        moe = jnp.einsum('te,ted->td', w_dense, eo)
        sh = jax.nn.silu(ht @ sw_gate) * (ht @ sw_up) @ sw_down
        return (moe + sh).reshape(b, s, d)
    h = _L0_tok_ref(x, L0_tok_log_dt, L0_tok_log_w_real, L0_tok_w_imag, 512)
    h = _layernorm(h + _L0_attn_ref(h, L0_attn_w_q, L0_attn_w_k, L0_attn_w_v, L0_attn_w_o), axis=-1)
    h = _layernorm(h + _L0_ffn_ref(h, L0_ffn_weight, L0_ffn_bias), axis=-1)
    h = _layernorm(h + _L1_attn_ref(h, L1_attn_Wq, L1_attn_bq, L1_attn_Wk, L1_attn_bk, L1_attn_Wv, L1_attn_bv, L1_attn_Wo), axis=-1)
    h = _layernorm(h + _L1_ffn_ref(h, L1_ffn_rms_weight, L1_ffn_router_w, L1_ffn_w_gate, L1_ffn_w_up, L1_ffn_w_down, L1_ffn_sw_gate, L1_ffn_sw_up, L1_ffn_sw_down), axis=-1)
    return h

_drawn_inputs = setup_inputs


def setup_inputs(seed=0):
    import zlib

    import numpy as np

    out = dict(_drawn_inputs(seed))
    spreads = {'L0_tok_log_w_real': (-0.6931471824645996, 0.2),
     'L1_attn_bq': (0.0, 0.8),
     'L1_attn_bk': (0.0, 0.8),
     'L1_attn_bv': (0.0, 0.1),
     'L1_ffn_rms_weight': (1.0, 0.6)}
    factors = {'L0_attn_w_q': 64.0, 'L0_attn_w_k': 64.0, 'L1_attn_Wq': 8.0, 'L1_attn_Wk': 8.0}
    for name, (base, spread) in spreads.items():
        noise = np.random.default_rng([zlib.crc32(name.encode()), seed]).standard_normal(out[name].shape)
        drawn = base * np.exp(spread * noise) if base else spread * noise
        out[name] = jnp.asarray(drawn.astype(out[name].dtype))
    for name, factor in factors.items():
        out[name] = (out[name] * factor).astype(out[name].dtype)
    return out
```

```python
from contextlib import ExitStack

import concourse.bass as bass
from concourse import mybir

ALU = mybir.AluOpType
ACT = mybir.ActivationFunctionType
AX_X = mybir.AxisListType.X
F32 = mybir.dt.float32
F32R = mybir.dt.float32r
BF16 = mybir.dt.bfloat16
I32 = mybir.dt.int32

P = 128
B, S, D = 16, 256, 512
NST = 64
CD = D // P
ST = S // P
ROUND = 12582912.0
PI = 3.141592653589793
LN_EPS = 1e-5


class Memory:

    def __init__(self, nc, ctx):
        self.nc, self.ctx = nc, ctx

    def sb(self, name, shape, dt=F32):
        return self.ctx.enter_context(self.nc.sbuf_tensor(name, shape, dt))

    def ps(self, name, shape, dt=F32):
        return self.ctx.enter_context(self.nc.psum_tensor(name, shape, dt))

    def sem(self, name):
        return self.ctx.enter_context(self.nc.semaphore(name))


class Chain:

    def __init__(self, eng, sem, base=0):
        self.eng, self.sem, self.base, self.n = eng, sem, base, 0

    def __call__(self, ins):
        self.n += 1
        ins.then_inc(self.sem, 1)
        self.eng.wait_ge(self.sem, self.base + self.n)


def carry_wait(eng, passed):
    eng.sem_inc(passed, 1)


HC = 8
HS = 2 * HC
STEPS = S // HS
NA, NM = 8, 64
NM1 = 8
TWO_PI_1 = 6.28125
TWO_PI_2 = 0.0019350051879882812
TWO_PI_3 = 3.0199161274e-07
LN2_1 = 0.693359375
LN2_2 = -2.12194440e-4


def token_mixer(nc, dyn_in, c_in, mult_in, half_in, h0):
    with ExitStack() as ctx:
        m = Memory(nc, ctx)
        dyn = m.sb("dyn", [P, 3, S])
        mult = m.sb("mult", [P, 3, NM1])
        half = m.sb("half", [P, 8])
        ex = m.sb("ex", [P, 2, S])
        ek = m.sb("ek", [P, 2, S])
        ep = m.sb("ep", [P, 2, S])
        ei = m.sb("ei", [P, 2, S], I32)
        wr = m.sb("wr", [P, S])
        al = m.sb("al", [P, S])
        th = m.sb("th", [P, S])
        g = [m.sb(f"g{n}", [P, S]) for n in range(7)]
        qq = m.sb("qq", [P, 3, S])
        craw = m.sb("craw", [P, 2, HS, 2, B])
        cm = m.sb("cm", [P, 2, HS, B])
        cm2 = m.sb("cm2", [P, 2, HS, B])
        ang = m.sb("ang", [P, 3, HS, NM1])
        turn = m.sb("turn", [P, 3, HS, NM1])
        ra = m.sb("ra", [P, 3, HS, NM1])
        rb = m.sb("rb", [P, 3, HS, NM1])
        mag = m.sb("mag", [P, 3, HS, NM1])
        tr = m.sb("tr", [P, 2, 3, HS, NM1])
        vv = [m.sb(f"vv{n}", [P, HC, NM]) for n in range(2)]
        v2 = m.sb("v2", [P, HC, NM])
        s1 = [m.sb(f"s1{n}", [P, HC, NA, B]) for n in range(2)]
        s2 = [m.sb(f"s2{n}", [P, HC, NA, B]) for n in range(2)]
        kout = m.sb("kout", [P, HS, NM])
        kps = [m.ps(f"kps{n}", [P, HC, NM]) for n in range(2)]

        ld = m.sem("ld")
        c_landed = [m.sem(f"c_landed{n}") for n in range(2)]
        c_free = m.sem("c_free")
        dve_chain = m.sem("dve_chain")
        exps = m.sem("exps")
        alpha_ready = m.sem("alpha_ready")
        pre_act = m.sem("pre_act")
        q_ready = m.sem("q_ready")
        cm_chain = m.sem("cm_chain")
        cm_ready = m.sem("cm_ready")
        angles_ready = m.sem("angles_ready")
        trig_ready = m.sem("trig_ready")
        tables_ready = m.sem("tables_ready")
        tables_free = m.sem("tables_free")
        vs_ready = m.sem("vs_ready")
        s2_ready = m.sem("s2_ready")
        k_ready = m.sem("k_ready")
        kout_ready = m.sem("kout_ready")
        k_stored = m.sem("k_stored")

        block = ctx.enter_context(nc.Block())

        @block.sync
        def _(sp):
            sp.dma_start(dyn[:, :, :], dyn_in).then_inc(ld, 16)
            sp.dma_start(mult[:, :, :], mult_in).then_inc(ld, 16)
            sp.dma_start(half[:, :], half_in).then_inc(ld, 16)
            with sp.Fori(0, STEPS) as i:
                sp.wait_ge(c_free, i + 1)
                sp.dma_start(craw[:, 0], c_in[:, bass.ds(i * HS, HS), :, :]).then_inc(c_landed[0], 16)
                sp.wait_ge(kout_ready, 2 * i + 2)
                sp.dma_start(h0[:, bass.ds(i * HS, HS), :], kout[:, :, :]).then_inc(k_stored, 16)
            sp.wait_ge(k_stored, 16 * STEPS)

        @block.gpsimd
        def _(pool):
            pool.sem_inc(c_free, 1)
            pool.wait_ge(q_ready, 1)
            with pool.Fori(0, STEPS) as i:
                chain = Chain(pool, cm_chain, i * 2)
                hs = bass.ds(i * HS, HS)
                pool.wait_ge(c_landed[0], 16 * i + 16)
                pool.wait_ge(s2_ready, 2 * i)
                pool.wait_ge(vs_ready, 2 * i)
                cr = craw[:, 0, :, 0, :].unsqueeze(1).broadcast_to([P, 2, HS, B])
                ci = craw[:, 0, :, 1, :].unsqueeze(1).broadcast_to([P, 2, HS, B])
                pool.tensor_tensor(cm2[:, :, :, :], ci, qq[:, 1:3, hs].unsqueeze(3).broadcast_to([P, 2, HS, B]),
                                   ALU.mult)
                chain(pool.tensor_tensor(cm[:, :, :, :], cr,
                                         qq[:, 0:2, hs].unsqueeze(3).broadcast_to([P, 2, HS, B]), ALU.mult))
                chain(pool.tensor_tensor(cm[:, :, :, :], cm[:, :, :, :], cm2[:, :, :, :], ALU.add))
                pool.sem_inc(cm_ready, 1)
                pool.sem_inc(c_free, 1)
                for j in range(2):
                    if j == 0:
                        pool.wait_ge(tables_ready, i + 1)
                    pool.wait_ge(k_ready, 2 * i + 1 + j)
                    js = slice(j * HC, (j + 1) * HC)
                    pool.tensor_tensor(s2[j][:, :, :, :],
                                       cm[:, 1, js, :].unsqueeze(2).broadcast_to([P, HC, NA, B]),
                                       tr[:, 1, 2, js, :].unsqueeze(3).broadcast_to([P, HC, NA, B]),
                                       ALU.mult).then_inc(s2_ready, 1)

        @block.vector
        def _(dve):
            c = Chain(dve, dve_chain)
            dve.wait_ge(ld, 48)
            c(dve.tensor_scalar(ex[:, :, :], dyn[:, 0:2, :], -87.0, 88.0, ALU.max, ALU.min))
            c(dve.tensor_scalar(ek[:, :, :], ex[:, :, :], 1.4426950408889634, ROUND, ALU.mult, ALU.add))
            c(dve.tensor_scalar(ek[:, :, :], ek[:, :, :], ROUND, None, ALU.subtract))
            c(dve.scalar_tensor_tensor(ex[:, :, :], ek[:, :, :], -LN2_1, ex[:, :, :], ALU.mult, ALU.add))
            c(dve.scalar_tensor_tensor(ex[:, :, :], ek[:, :, :], -LN2_2, ex[:, :, :], ALU.mult, ALU.add))
            c(dve.tensor_scalar(ep[:, :, :], ex[:, :, :], 1.0 / 5040, None, ALU.mult))
            for f in (720.0, 120.0, 24.0, 6.0, 2.0, 1.0):
                c(dve.scalar_tensor_tensor(ep[:, :, :], ep[:, :, :], 1.0 / f, ex[:, :, :], ALU.add, ALU.mult))
            c(dve.tensor_scalar(ei[:, :, :], ek[:, :, :], 127.0, None, ALU.add))
            c(dve.tensor_scalar(ei[:, :, :], ei[:, :, :], 23, None, ALU.logical_shift_left))
            c(dve.scalar_tensor_tensor(ep[:, :, :], ep[:, :, :], 1.0, ei[:, :, :].bitcast(F32), ALU.add, ALU.mult))
            dt, wabs, wi = ep[:, 0, :], ep[:, 1, :], dyn[:, 2, :]
            c(dve.tensor_scalar(wr[:, :], wabs, -1.0, None, ALU.mult))
            c(dve.tensor_tensor(al[:, :], wr[:, :], dt, ALU.mult))
            c(dve.tensor_tensor(th[:, :], wi, dt, ALU.mult))
            k, r, a = g[0], g[1], g[2]
            c(dve.tensor_scalar(k[:, :], th[:, :], 1.0 / (2 * PI), ROUND, ALU.mult, ALU.add))
            c(dve.tensor_scalar(k[:, :], k[:, :], ROUND, None, ALU.subtract))
            c(dve.scalar_tensor_tensor(r[:, :], k[:, :], -TWO_PI_1, th[:, :], ALU.mult, ALU.add))
            c(dve.scalar_tensor_tensor(r[:, :], k[:, :], -TWO_PI_2, r[:, :], ALU.mult, ALU.add))
            c(dve.scalar_tensor_tensor(r[:, :], k[:, :], -TWO_PI_3, r[:, :], ALU.mult, ALU.add))
            c(dve.tensor_scalar(r[:, :], r[:, :], PI, -PI, ALU.min, ALU.max))
            dve.scalar_tensor_tensor(a[:, :], r[:, :], -1.0, r[:, :], ALU.mult, ALU.max).then_inc(alpha_ready, 1)
            sn, cs, t = g[3], g[4], g[5]
            em1, nr, ni, den = g[0], g[1], g[2], g[6]
            dve.wait_ge(pre_act, 3)
            c(dve.tensor_scalar(den[:, :], t[:, :], -1.0, 1.0, ALU.mult, ALU.add))
            c(dve.reciprocal(den[:, :], den[:, :]))
            c(dve.scalar_tensor_tensor(em1[:, :], t[:, :], 2.0, den[:, :], ALU.mult, ALU.mult))
            c(dve.tensor_tensor(cs[:, :], cs[:, :], sn[:, :], ALU.mult))
            c(dve.scalar_tensor_tensor(sn[:, :], sn[:, :], -2.0, sn[:, :], ALU.mult, ALU.mult))
            c(dve.tensor_scalar(t[:, :], em1[:, :], 1.0, None, ALU.add))
            c(dve.tensor_tensor(nr[:, :], sn[:, :], t[:, :], ALU.mult))
            c(dve.tensor_tensor(nr[:, :], nr[:, :], em1[:, :], ALU.add))
            c(dve.scalar_tensor_tensor(ni[:, :], cs[:, :], 2.0, t[:, :], ALU.mult, ALU.mult))
            c(dve.tensor_tensor(sn[:, :], wr[:, :], wr[:, :], ALU.mult))
            c(dve.tensor_tensor(cs[:, :], wi, wi, ALU.mult))
            c(dve.tensor_tensor(den[:, :], sn[:, :], cs[:, :], ALU.add))
            c(dve.reciprocal(den[:, :], den[:, :]))
            c(dve.tensor_tensor(sn[:, :], nr[:, :], wr[:, :], ALU.mult))
            c(dve.tensor_tensor(cs[:, :], ni[:, :], wi, ALU.mult))
            c(dve.tensor_tensor(sn[:, :], sn[:, :], cs[:, :], ALU.add))
            c(dve.tensor_tensor(qq[:, 0, :], sn[:, :], den[:, :], ALU.mult))
            c(dve.tensor_tensor(sn[:, :], nr[:, :], wi, ALU.mult))
            c(dve.tensor_tensor(cs[:, :], ni[:, :], wr[:, :], ALU.mult))
            c(dve.tensor_tensor(sn[:, :], sn[:, :], cs[:, :], ALU.subtract))
            c(dve.tensor_tensor(qq[:, 1, :], sn[:, :], den[:, :], ALU.mult))
            dve.tensor_scalar(qq[:, 2, :], qq[:, 0, :], -1.0, None, ALU.mult).then_inc(q_ready, 1)

            used = c.n
            with dve.Fori(0, STEPS) as i:
                per = 13
                c = Chain(dve, dve_chain, i * per + used)
                hs = bass.ds(i * HS, HS)
                full = [P, 3, HS, NM1]
                mt = mult[:, :, :].unsqueeze(2).broadcast_to(full)
                dve.wait_ge(trig_ready, i)
                dve.tensor_tensor(mag[:, :, :, :], al[:, hs].unsqueeze(1).unsqueeze(3).broadcast_to(full), mt, ALU.mult)
                c(dve.tensor_tensor(ang[:, :, :, :], th[:, hs].unsqueeze(1).unsqueeze(3).broadcast_to(full), mt,
                                    ALU.mult))
                c(dve.tensor_scalar(turn[:, :, :, :], ang[:, :, :, :], 1.0 / (2 * PI), ROUND, ALU.mult, ALU.add))
                c(dve.tensor_scalar(turn[:, :, :, :], turn[:, :, :, :], ROUND, None, ALU.subtract))
                for part in (TWO_PI_1, TWO_PI_2, TWO_PI_3):
                    c(dve.scalar_tensor_tensor(ang[:, :, :, :], turn[:, :, :, :], -part, ang[:, :, :, :], ALU.mult,
                                               ALU.add))
                c(dve.tensor_scalar(ang[:, :, :, :], ang[:, :, :, :], PI, -PI, ALU.min, ALU.max))
                c(dve.scalar_tensor_tensor(ra[:, :, :, :], ang[:, :, :, :], half[:, 0:1], ang[:, :, :, :], ALU.mult,
                                           ALU.max))
                dve.scalar_tensor_tensor(rb[:, :, :, :], ang[:, :, :, :], half[:, 1:2], ang[:, :, :, :], ALU.mult,
                                         ALU.max).then_inc(angles_ready, 1)
                dve.wait_ge(trig_ready, i + 1)
                c(dve.tensor_tensor(tr[:, :, :, :, :].rearrange("p t g h m -> p t (g h m)"),
                                    tr[:, :, :, :, :].rearrange("p t g h m -> p t (g h m)"),
                                    mag[:, :, :, :].rearrange("p g h m -> p (g h m)").unsqueeze(1).broadcast_to(
                                        [P, 2, 3 * HS * NM1]), ALU.mult))
                dve.sem_inc(tables_ready, 1)
                dve.wait_ge(cm_ready, i + 1)
                for j in range(2):
                    js = slice(j * HC, (j + 1) * HC)
                    out4 = [P, HC, NM1, NM1]
                    dve.wait_ge(k_ready, 2 * i + 1 + j)
                    dve.tensor_tensor(v2[:, :, :].rearrange("p h (a b) -> p h a b", b=NM1),
                                      tr[:, 1, 1, js, :].unsqueeze(3).broadcast_to(out4),
                                      tr[:, 1, 0, js, :].unsqueeze(2).broadcast_to(out4), ALU.mult)
                    c(dve.tensor_tensor(vv[j][:, :, :].rearrange("p h (a b) -> p h a b", b=NM1),
                                        tr[:, 0, 1, js, :].unsqueeze(3).broadcast_to(out4),
                                        tr[:, 0, 0, js, :].unsqueeze(2).broadcast_to(out4), ALU.mult))
                    c(dve.tensor_tensor(vv[j][:, :, :], vv[j][:, :, :], v2[:, :, :], ALU.add))
                    dve.tensor_tensor(s1[j][:, :, :, :],
                                      cm[:, 0, js, :].unsqueeze(2).broadcast_to([P, HC, NA, B]),
                                      tr[:, 0, 2, js, :].unsqueeze(3).broadcast_to([P, HC, NA, B]),
                                      ALU.mult).then_inc(vs_ready, 1)
                assert c.n == per, c.n

        @block.scalar
        def _(act):
            act.wait_ge(alpha_ready, 1)
            act.activation(g[3][:, :], g[1][:, :], ACT.Sin, scale=0.5).then_inc(pre_act, 1)
            act.activation(g[4][:, :], g[2][:, :], ACT.Sin, bias=half[:, 6:7], scale=-0.5).then_inc(pre_act, 1)
            act.activation(g[5][:, :], al[:, :], ACT.Tanh, scale=0.5).then_inc(pre_act, 1)
            with act.Fori(0, STEPS) as i:
                act.wait_ge(angles_ready, i + 1)
                act.wait_ge(vs_ready, 2 * i)
                act.wait_ge(s2_ready, 2 * i)
                sin = ACT.Sin
                act.activation(tr[0:64, 0, 0], ra[0:64, 0], sin, bias=half[0:64, 6:7], scale=-1.0)
                act.activation(tr[64:128, 0, 0], rb[64:128, 0], sin, bias=half[64:128, 6:7], scale=-1.0)
                act.activation(tr[0:64, 1, 0], rb[0:64, 0], sin)
                act.activation(tr[64:128, 1, 0], ra[64:128, 0], sin)
                act.activation(tr[:, 0, 1], ra[:, 1], sin, bias=half[:, 2:3], scale=half[:, 0:1])
                act.activation(tr[:, 1, 1], rb[:, 1], sin, bias=half[:, 3:4], scale=-1.0)
                act.activation(tr[:, 0, 2], ra[:, 2], sin, bias=half[:, 2:3], scale=-1.0)
                act.activation(tr[:, 1, 2], rb[:, 2], sin, bias=half[:, 3:4], scale=half[:, 1:2])
                act.activation(mag[:, :, :, :], mag[:, :, :, :], ACT.Exp).then_inc(trig_ready, 1)
                for j in range(2):
                    act.wait_ge(k_ready, 2 * i + j + 3)
                    if j == 0:
                        act.wait_ge(k_stored, 16 * i)
                    act.activation(kout[:, j * HC:(j + 1) * HC, :], kps[j][:, :, :], ACT.Copy,
                                   scale=2.0).then_inc(kout_ready, 1)

        @block.tensor
        def _(pe):
            pe.sem_inc(k_ready, 2)
            with pe.Fori(0, STEPS) as i:
                for j in range(2):
                    pe.wait_ge(vs_ready, 2 * i + j + 1)
                    pe.wait_ge(s2_ready, 2 * i + j + 1)
                    pe.wait_ge(kout_ready, 2 * i)
                    for h in range(HC):
                        pe.matmul(kps[j][:, h, :], s1[j][:, h], vv[j][:, h, :], start=True, stop=False)
                        mm = pe.matmul(kps[j][:, h, :], s2[j][:, h], vv[j][:, h, :], start=False, stop=True)
                    mm.then_inc(k_ready, 1)




def mm3(pe, out, lhs, rhs, start, stop):
    pe.matmul(out, lhs[0], rhs[0], start=start, stop=False)
    pe.matmul(out, lhs[0], rhs[1], start=False, stop=False)
    return pe.matmul(out, lhs[1], rhs[0], start=False, stop=stop)


def split_weights(nc, parts):
    with ExitStack() as ctx:
        m = Memory(nc, ctx)
        width = 2048
        tiles = []
        for dram, hi, lo in parts:
            n = dram.shape[1]
            for a in range(0, n, width):
                b = min(a + width, n)
                tiles.append((dram[:, a:b], hi[:, a:b], lo[:, a:b], b - a))
        bufs = 4
        raw = [m.sb(f"wraw{n}", [P, width]) for n in range(bufs)]
        landed = [m.sem(f"w_landed{n}") for n in range(bufs)]
        hi_done = m.sem("w_hi_done")
        lo_done = m.sem("w_lo_done")
        block = ctx.enter_context(nc.Block())

        @block.sync
        def _(sp):
            for t, (dram, _, _, w) in enumerate(tiles):
                if t >= bufs:
                    sp.wait_ge(lo_done, t - bufs + 1)
                sp.dma_start(raw[t % bufs][:, 0:w], dram).then_inc(landed[t % bufs], 16)

        @block.scalar
        def _(act):
            for t, (_, hi, _, w) in enumerate(tiles):
                act.wait_ge(landed[t % bufs], 16 * (t // bufs + 1))
                act.activation(hi, raw[t % bufs][:, 0:w], ACT.Copy).then_inc(hi_done, 1)

        @block.vector
        def _(dve):
            for t, (_, hi, lo, w) in enumerate(tiles):
                dve.wait_ge(hi_done, t + 1)
                dve.tensor_tensor(lo, raw[t % bufs][:, 0:w], hi.bitcast(F32), ALU.subtract).then_inc(lo_done, 1)


NH, NKV, HD = 16, 4, 128
REP = NH // NKV
NEG = -1e37
BIG = 3e38


def attention0(nc, wq_in, wk_in, wv_in, wo_in, rope_in, mask_in, ident_in, h0, h1):
    with ExitStack() as wctx:
        w = Memory(nc, wctx)
        wq = [w.sb(f"wq{p}", [P, CD, NH * HD], F32R) for p in ("h", "l")]
        wk = [w.sb(f"wk{p}", [P, CD, NKV * HD], F32R) for p in ("h", "l")]
        wv = [w.sb(f"wv{p}", [P, CD, NKV * HD], F32R) for p in ("h", "l")]
        wo = [w.sb(f"wo{p}", [P, NH, D], F32R) for p in ("h", "l")]
        flat = lambda t: t[:, :, :].rearrange("p a n -> p (a n)")
        for c in range(1):
            split_weights(nc, [(wk_in, flat(wk[0]), flat(wk[1])), (wv_in, flat(wv[0]), flat(wv[1])),
                               (wq_in, flat(wq[0]), flat(wq[1])), (wo_in, flat(wo[0]), flat(wo[1]))])
        with ExitStack() as ctx:
            attention0_loop(nc, Memory(nc, ctx), wq, wk, wv, wo, rope_in, mask_in, ident_in, h0, h1)


def attention0_loop(nc, m, wq, wk, wv, wo, rope_in, mask_in, ident_in, h0, h1):
    UNITS, ROPES = 2 + NKV + ST + NH, NKV + NH
    SCALE = float(HD) ** -0.5
    ident = m.sb("ident", [P, P])
    cos = m.sb("cos", [P, S])
    sin = m.sb("sin", [P, S])
    mask = m.sb("mask", [P, 2 * P])
    xs = m.sb("xs", [P, D])
    res = m.sb("res", [P, ST, D])
    xT = [m.sb(f"xT{p}", [P, CD, S], F32R) for p in "hl"]
    kT = [m.sb(f"kT{p}", [P, NKV, S], F32R) for p in "hl"]
    v = [m.sb(f"v{p}", [P, ST, NKV * HD], F32R) for p in "hl"]
    t1 = m.sb("t1", [P, S])
    t2 = m.sb("t2", [P, S])
    q = [[m.sb(f"q{p}{n}", [P, S], F32R) for p in "hl"] for n in range(2)]
    prob = [m.sb(f"prob{n}", [P, 3 * P]) for n in range(2)]
    pT = [m.sb(f"pT{p}", [P, 3 * P], F32R) for p in "hl"]
    oT = [m.sb(f"oT{p}", [P, S], F32R) for p in "hl"]
    mx = m.sb("mx", [P, 2, ST])
    sums = m.sb("sums", [P, 2, ST])
    inv = m.sb("inv", [P, 2, ST])
    st = m.sb("st", [P, ST, 6])
    mv = m.sb("mv", [P, ST, 2])
    nhalf = m.sb("nhalf", [P, ST])
    proj = [m.ps(f"proj{n}", [P, 512]) for n in range(3)]
    sc = m.ps("sc", [P, 512])
    pTp = m.ps("pTp", [P, 512])
    oTp = m.ps("oTp", [P, 512])
    acc = [m.ps(f"acc{t}", [P, D]) for t in range(ST)]

    consts = m.sem("consts")
    dve_passed = m.sem("a_dve_passed")
    x_landed = m.sem("x_landed")
    res_landed = m.sem("res_landed")
    proj_ready = m.sem("proj_ready")
    proj_used = m.sem("proj_used")
    split_hi = m.sem("split_hi")
    rope_sum = m.sem("rope_sum")
    rope_hi = m.sem("rope_hi")
    rope_lo = m.sem("rope_lo")
    sc_ready = m.sem("sc_ready")
    mx_ready = m.sem("mx_ready")
    ex_ready = m.sem("ex_ready")
    inv_ready = m.sem("inv_ready")
    p_ready = m.sem("p_ready")
    pt_ready = m.sem("pt_ready")
    pt_hi = m.sem("pt_hi")
    pt_lo = m.sem("pt_lo")
    pv_ready = m.sem("pv_ready")
    ot_hi = m.sem("ot_hi")
    ot_lo = m.sem("ot_lo")
    o_done = m.sem("o_done")
    ln_chain = m.sem("ln_chain")
    ln_var = m.sem("ln_var")
    ln_rstd = m.sem("ln_rstd")
    ln_done = m.sem("ln_done")
    stored = m.sem("stored")

    head = lambda h: 0 <= h < NH
    LN_STEPS = 3
    block = m.ctx.enter_context(nc.Block())

    @block.sync
    def _(sp):
        sp.dma_start(ident[:, :], ident_in).then_inc(consts, 16)
        sp.dma_start(cos[:, :], rope_in[:, 0, :]).then_inc(consts, 16)
        sp.dma_start(sin[:, :], rope_in[:, 1, :]).then_inc(consts, 16)
        sp.dma_start(mask[:, :], mask_in).then_inc(consts, 16)
        h0_v = h0.rearrange("(a b) s m -> b s a m", b=B)
        h1_v = h1.rearrange("b (t p) d -> b p t d", p=P)
        with sp.Fori(0, B) as i:
            for t in range(ST):
                sp.wait_ge(proj_ready, i * UNITS + t) if t else sp.wait_ge(proj_ready, i * UNITS)
                src = h0_v[bass.ds(i, 1), t * P:(t + 1) * P, :, :].rearrange("o s a m -> (o s) a m")
                sp.dma_start(xs[:, :].rearrange("p (a m) -> p a m", m=NM), src).then_inc(x_landed, 16)
            sp.wait_ge(stored, 16 * i)
            for t in range(ST):
                src = h0_v[bass.ds(i, 1), t * P:(t + 1) * P, :, :].rearrange("o s a m -> (o s) a m")
                sp.dma_start(res[:, t, :].rearrange("p (a m) -> p a m", m=NM), src).then_inc(res_landed, 16)
            sp.wait_ge(ln_done, i + 1)
            sp.dma_start(h1_v[bass.ds(i, 1), :, :, :].rearrange("o p t d -> (o p) t d"), res[:, :, :])\
              .then_inc(stored, 16)
        sp.wait_ge(stored, 16 * B)

    @block.tensor
    def _(pe):
        pe.sem_inc(sc_ready, 2)
        pe.sem_inc(pt_ready, 2)
        pe.wait_ge(consts, 64)
        with pe.Fori(0, B) as i:
            n, u0, r0 = i * NH, i * UNITS, i * ROPES
            u = 0

            def bank():
                nonlocal u
                pe.wait_ge(proj_used, u0 + (u + 1))
                u += 1
                return proj[(u - 1) % 3]

            for t in range(ST):
                pe.wait_ge(x_landed, i * (16 * ST) + 16 * (t + 1))
                b = bank()
                for c in range(CD):
                    mm = pe.transpose(b[:, c * P:(c + 1) * P], xs[:, c * P:(c + 1) * P], ident[:, :])
                mm.then_inc(proj_ready, 1)
            for g in range(NKV):
                b = bank()
                if g == 0:
                    pe.wait_ge(proj_used, u0 + (3 + ST))
                for c in range(CD):
                    mm = mm3(pe, b[:, 0:S], [x[:, c, g * HD:(g + 1) * HD] for x in wk], [x[:, c, :] for x in xT],
                             c == 0, c == CD - 1)
                mm.then_inc(proj_ready, 1)
            for t in range(ST):
                b = bank()
                for c in range(CD):
                    mm = mm3(pe, b[:, :], [x[:, c, t * P:(t + 1) * P] for x in xT], [x[:, c, :] for x in wv],
                             c == 0, c == CD - 1)
                mm.then_inc(proj_ready, 1)
            for s in range(-2, NH + 2):
                if head(s):
                    h, g = s, s // REP
                    pe.wait_ge(rope_lo, r0 + (NKV + h + 1))
                    pe.wait_ge(mx_ready, n + h)
                    qh = q[h % 2]
                    mm3(pe, sc[:, 0:P], [x[:, 0:P] for x in qh], [x[:, g, 0:P] for x in kT], True, True)
                    mm3(pe, sc[:, P:3 * P], [x[:, P:S] for x in qh], [x[:, g, :] for x in kT], True, True)\
                        .then_inc(sc_ready, 1)
                if head(s - 2):
                    h, g = s - 2, (s - 2) // REP
                    pe.wait_ge(pt_lo, n + (h + 1))
                    pe.wait_ge(ot_lo, n + h)
                    if h == 0:
                        pe.wait_ge(proj_used, u0 + (3 + 2 + NKV + ST))
                    mm3(pe, oTp[:, 0:S], [x[:, 0, g * HD:(g + 1) * HD] for x in v], [x[:, 0:S] for x in pT], True,
                        False)
                    mm3(pe, oTp[:, P:S], [x[:, 1, g * HD:(g + 1) * HD] for x in v], [x[:, S:3 * P] for x in pT],
                        False, True).then_inc(pv_ready, 1)
                if head(s + 2):
                    h = s + 2
                    b = bank()
                    for c in range(CD):
                        mm = mm3(pe, b[:, 0:S], [x[:, c, h * HD:(h + 1) * HD] for x in wq],
                                 [x[:, c, :] for x in xT], c == 0, c == CD - 1)
                    mm.then_inc(proj_ready, 1)
                if head(s - 1):
                    h = s - 1
                    pe.wait_ge(p_ready, n + (h + 1))
                    pe.wait_ge(pt_lo, n + h)
                    pr = prob[h % 2]
                    pe.transpose(pTp[:, 0:P], pr[:, 0:P], ident[:, :])
                    pe.transpose(pTp[:, P:2 * P], pr[:, P:2 * P], ident[:, :])
                    pe.transpose(pTp[:, 2 * P:3 * P], pr[:, 2 * P:3 * P], ident[:, :]).then_inc(pt_ready, 1)
                if head(s - 2):
                    h = s - 2
                    pe.wait_ge(ot_lo, n + (h + 1))
                    if h == 0:
                        pe.wait_ge(ln_var, i)
                    for t in range(ST):
                        mm = mm3(pe, acc[t][:, :], [x[:, t * P:(t + 1) * P] for x in oT], [x[:, h, :] for x in wo],
                                 h == 0, h == NH - 1)
                    mm.then_inc(o_done, 1)

    @block.scalar
    def _(act):
        with act.Fori(0, B) as i:
            n, u0, r0 = i * NH, i * UNITS, i * ROPES
            for t in range(ST):
                act.wait_ge(proj_ready, u0 + (t + 1))
                act.activation(xT[0][:, :, t * P:(t + 1) * P], proj[t][:, :].rearrange("p (c s) -> p c s", c=CD),
                               ACT.Copy).then_inc(split_hi, 1)
            for g in range(NKV):
                act.wait_ge(rope_sum, r0 + (g + 1))
                if g == 0:
                    act.wait_ge(sc_ready, n + 2)
                act.activation(kT[0][:, g, :], t1[:, :], ACT.Copy).then_inc(rope_hi, 1)
            for t in range(ST):
                u = 2 + NKV + t
                act.wait_ge(proj_ready, u0 + (u + 1))
                if t == 0:
                    act.wait_ge(pv_ready, n)
                act.activation(v[0][:, t, :], proj[u % 3][:, :], ACT.Copy).then_inc(split_hi, 1)
            for s in range(-2, NH + 2):
                if head(s + 1):
                    h = s + 1
                    act.wait_ge(rope_sum, r0 + (NKV + h + 1))
                    act.wait_ge(sc_ready, n + (h + 1))
                    act.activation(q[h % 2][0][:, :], t1[:, :], ACT.Copy).then_inc(rope_hi, 1)
                if head(s - 2):
                    h = s - 2
                    act.wait_ge(pv_ready, n + (h + 1))
                    act.wait_ge(o_done, n + h)
                    act.activation(oT[0][:, :], oTp[:, 0:S], ACT.Copy).then_inc(ot_hi, 1)
                if head(s):
                    h = s
                    act.wait_ge(mx_ready, n + (h + 1))
                    for t, (a, b) in enumerate(((0, P), (P, 3 * P))):
                        ins = act.activation(prob[h % 2][:, a:b], prob[h % 2][:, a:b], ACT.Exp,
                                             bias=mx[:, h % 2, t:t + 1], scale=-1.0,
                                             accum_out=sums[:, h % 2, t:t + 1])
                    ins.then_inc(ex_ready, 1)
                if head(s - 1):
                    h = s - 1
                    act.wait_ge(pt_ready, n + (h + 3))
                    act.wait_ge(pv_ready, n + h)
                    act.activation(pT[0][:, :], pTp[:, 0:3 * P], ACT.Copy).then_inc(pt_hi, 1)

    @block.gpsimd
    def _(pool):
        pool.memset(nhalf[:, :], -0.5)
        with pool.Fori(0, B) as i:
            n, u0, r0 = i * NH, i * UNITS, i * ROPES
            for r in range(ROPES):
                u = 2 + r if r < NKV else 2 + ST + r
                pool.wait_ge(proj_used, u0 + (3 + u + 1))
                pool.tensor_tensor(t1[:, :], t1[:, :], t2[:, :], ALU.add).then_inc(rope_sum, 1)
                pool.wait_ge(rope_hi, r0 + (r + 1))
                hi, lo = (kT[0][:, r, :], kT[1][:, r, :]) if r < NKV else (q[r % 2][0][:, :], q[r % 2][1][:, :])
                pool.tensor_tensor(lo, t1[:, :], hi.bitcast(F32), ALU.subtract).then_inc(rope_lo, 1)
            pool.wait_ge(ln_var, i + 1)
            pool.tensor_tensor(mv[:, :, 1], mv[:, :, 1], nhalf[:, :], ALU.pow).then_inc(ln_rstd, 1)

    @block.vector
    def _(dve):
        dve.sem_inc(proj_used, 3)
        dve.wait_ge(consts, 64)
        with dve.Fori(0, B) as i:
            n, u0, r0 = i * NH, i * UNITS, i * ROPES

            def rope(u, r):
                b = proj[u % 3]
                dve.wait_ge(proj_ready, u0 + (u + 1))
                dve.wait_ge(rope_lo, r0 + r)
                dve.tensor_tensor(t2[0:64, :], b[64:P, 0:S], sin[0:64, :], ALU.mult)
                dve.tensor_tensor(t2[64:P, :], b[0:64, 0:S], sin[64:P, :], ALU.mult)
                dve.tensor_tensor(t1[:, :], b[:, 0:S], cos[:, :], ALU.mult).then_inc(proj_used, 1)

            for t in range(ST):
                dve.wait_ge(split_hi, i * (2 * ST) + (t + 1))
                sl = slice(t * P, (t + 1) * P)
                dve.tensor_tensor(xT[1][:, :, sl], proj[t][:, :].rearrange("p (c s) -> p c s", c=CD),
                                  xT[0][:, :, sl].bitcast(F32), ALU.subtract).then_inc(proj_used, 1)
            for g in range(NKV):
                rope(2 + g, g)
            for t in range(ST):
                dve.wait_ge(split_hi, i * (2 * ST) + (ST + t + 1))
                dve.tensor_tensor(v[1][:, t, :], proj[(2 + NKV + t) % 3][:, :], v[0][:, t, :].bitcast(F32),
                                  ALU.subtract).then_inc(proj_used, 1)
            for s in range(-2, NH + 2):
                if head(s):
                    h = s
                    dve.wait_ge(sc_ready, n + (h + 3))
                    dve.wait_ge(pt_ready, n + (h + 1))
                    carry_wait(dve, dve_passed)
                    for t, (a, b) in enumerate(((0, P), (P, 3 * P))):
                        ins = dve.tensor_tensor_reduce(out=prob[h % 2][:, a:b], in0=sc[:, a:b],
                                                       in1=mask[:, 2 * P - (b - a):2 * P], scale=-SCALE, scalar=BIG,
                                                       op0=ALU.add, op1=ALU.min, accum_out=mx[:, h % 2, t:t + 1])
                    ins.then_inc(mx_ready, 1)
                if head(s - 2):
                    h = s - 2
                    dve.wait_ge(ot_hi, n + (h + 1))
                    dve.tensor_tensor(oT[1][:, :], oTp[:, 0:S], oT[0][:, :].bitcast(F32), ALU.subtract)\
                       .then_inc(ot_lo, 1)
                if head(s):
                    h = s
                    dve.wait_ge(ex_ready, n + (h + 1))
                    dve.reciprocal(inv[:, h % 2, :], sums[:, h % 2, :]).then_inc(inv_ready, 1)
                    dve.wait_ge(inv_ready, n + (h + 1))
                    for t, (a, b) in enumerate(((0, P), (P, 3 * P))):
                        ins = dve.tensor_scalar(prob[h % 2][:, a:b], prob[h % 2][:, a:b], inv[:, h % 2, t:t + 1],
                                                None, ALU.mult)
                    ins.then_inc(p_ready, 1)
                if head(s + 2):
                    rope(2 + NKV + ST + s + 2, NKV + s + 2)
                if head(s - 1):
                    h = s - 1
                    dve.wait_ge(pt_hi, n + (h + 1))
                    dve.tensor_tensor(pT[1][:, :], pTp[:, 0:3 * P], pT[0][:, :].bitcast(F32), ALU.subtract)\
                       .then_inc(pt_lo, 1)
            ch = Chain(dve, ln_chain, i * LN_STEPS)
            dve.wait_ge(o_done, n + NH)
            dve.wait_ge(res_landed, (i + 1) * (16 * ST))
            for t in range(ST):
                ins = dve.tensor_tensor(res[:, t, :], res[:, t, :], acc[t][:, :], ALU.add)
            ch(ins)
            for t in range(ST):
                ins = dve.bn_stats(st[:, t, :], res[:, t, :])
            ch(ins)
            carry_wait(dve, dve_passed)
            for t in range(ST):
                ins = dve.bn_aggr(mv[:, t, :], st[:, t, :])
            ch(ins)
            dve.tensor_scalar(mv[:, :, 1], mv[:, :, 1], LN_EPS, None, ALU.add).then_inc(ln_var, 1)
            dve.wait_ge(ln_rstd, i + 1)
            for t in range(ST):
                ins = dve.tensor_scalar(res[:, t, :], res[:, t, :], mv[:, t, 0:1], mv[:, t, 1:2], ALU.subtract,
                                        ALU.mult)
            ins.then_inc(ln_done, 1)


NH1, HD1 = 16, 32
G1 = 4
QEPS = 1e-5
F_UNITS = ["qT0", "qT1", "ffn0", "ffn1", "x0", "x1", "q0", "kv0", "q1", "kv1", "tq0", "tk0", "tq1", "tk1"]
ALL_UNITS = ["oT0", "oT1", "qT0", "qT1", "out0", "out1"] + F_UNITS[2:]
G_UNITS = ["oT0", "oT1", "out0", "out1"]
F_HIS = ["x0", "x1", "v0", "v1", "tq0", "tk0", "tq1", "tk1"]
G_HIS = ["oT0", "oT1"]
BETWEEN = {0: ["g_norm"], 1: ["f_quant"], 2: ["g_oT"], 3: ["f_qT"], 4: ["g_out"], 6: ["f_ffn"], 9: ["f_xT"],
           11: ["f_proj0"], 12: ["f_proj1"], 14: ["f_hT0"], 15: ["f_hT1"]}


class Segment:

    def __init__(self, b, kind, parity):
        self.b, self.kind, self.parity = b, kind, parity
        self.units = {"front": F_UNITS, "all": ALL_UNITS, "back": G_UNITS}[kind]
        self.his = {"front": F_HIS, "all": G_HIS + F_HIS, "back": G_HIS}[kind]
        if kind == "front":
            self.unit0, self.hi0 = len(F_UNITS) * (b + 1), len(F_HIS) * (b + 1)
            self.mod = self.unit0 % 3
        elif kind == "all" or b == B - 1:
            self.unit0 = b * len(ALL_UNITS) + (2 * len(F_UNITS) - len(ALL_UNITS))
            self.hi0 = b * (len(F_HIS) + 2) + (2 * len(F_HIS) - len(F_HIS) - 2)
            self.mod = (2 * len(F_UNITS) - len(ALL_UNITS)) % 3
        else:
            self.unit0 = (B - 1) * len(ALL_UNITS) + (2 * len(F_UNITS) - len(ALL_UNITS)) + len(G_UNITS)
            self.hi0 = (B - 1) * (len(F_HIS) + 2) + (2 * len(F_HIS) - len(F_HIS) - 2) + 2
            self.mod = self.unit0 % 3

    def unit(self, name):
        return self.unit0 + (self.units.index(name) + 1)

    def bank(self, name):
        return (self.mod + self.units.index(name)) % 3

    def hi(self, name):
        return self.hi0 + (self.his.index(name) + 1)


def run_segment(seg, h):
    heads = 0 <= seg.b < B if isinstance(seg.b, int) else True
    for s in range(NH1 + 2):
        for name, k in (("sc", s), ("mx", s), ("ex", s), ("pt", s - 1), ("pv", s - 2)):
            if heads and name in h and 0 <= k < NH1:
                h[name](seg, k)
        for name in BETWEEN.get(s, []):
            if name[0] == "g" and seg.kind == "front" or name[0] == "f" and seg.kind == "back":
                continue
            stage = name.rstrip("01")
            if stage in h:
                h[stage](seg) if stage == name else h[stage](seg, int(name[-1]))


def all_segments(eng, h):
    run_segment(Segment(-1, "front", 1), h)
    run_segment(Segment(0, "front", 0), h)
    with eng.Fori(0, (B - 2) // 2) as i:
        run_segment(Segment(i * 2 + 1, "all", 1), h)
        run_segment(Segment(i * 2 + 2, "all", 0), h)
    run_segment(Segment(B - 1, "back", 1), h)
    run_segment(Segment(B, "back", 0), h)


def block01(nc, fw_in, fb_in, wq_in, wkv_in, wo_in, bias_in, rope_in, mask_in, ident_in, identb_in, h1, h3):
    SCALE = float(HD1) ** -0.5
    with ExitStack() as ctx:
        m = Memory(nc, ctx)
        ident = m.sb("b_ident", [P, P])
        identb = m.sb("b_identb", [P, P], BF16)
        rope = m.sb("b_rope", [P, 2, ST, HD1])
        mask = m.sb("b_mask", [P, 2 * P])
        fraw = m.sb("b_fraw", [P, CD * D])
        ftmp = m.sb("b_ftmp", [P, CD * D])
        fw = m.sb("b_fw", [P, CD, D], BF16)
        fbias = m.sb("b_fbias", [P, D])
        asum = m.sb("b_asum", [P, 1])
        alpha = m.sb("b_alpha", [P, 2])
        ones = m.sb("b_ones", [P, P])
        onesr = m.sb("b_onesr", [1, P], F32R)
        wraw = m.sb("b_wraw", [P, CD, D + 2 * P + D], BF16)
        wq = m.sb("b_wq", [P, CD, D], F32R)
        wkv = m.sb("b_wkv", [P, CD, 2 * P], F32R)
        wo = m.sb("b_wo", [P, CD, D], F32R)
        braw = m.sb("b_braw", [1, D + 2 * P], BF16)
        bqkv = m.sb("b_bqkv", [1, D + 2 * P], F32R)
        x1 = m.sb("b_x1", [P, ST, D])
        am = m.sb("b_am", [P, ST])
        rs = m.sb("b_rs", [P, ST])
        sa = m.sb("b_sa", [P, ST])
        qf = m.sb("b_qf", [P, ST, D])
        qb = m.sb("b_qb", [P, ST, D], BF16)
        xb = m.sb("b_xb", [P, ST, D])
        qTb = m.sb("b_qTb", [P, ST, CD, P], BF16)
        x2 = [m.sb(f"b_x2{n}", [P, ST, D]) for n in range(2)]
        xT = [m.sb(f"b_xT{p}", [P, CD, S], F32R) for p in "hl"]
        tq = [m.sb(f"b_tq{n}", [P, D]) for n in range(2)]
        tk = [m.sb(f"b_tk{n}", [P, P]) for n in range(2)]
        qr = m.sb("b_qr", [P, ST, D])
        kr = m.sb("b_kr", [P, ST, D])
        qT = [[m.sb(f"b_qT{p}{n}", [P, G1, S], F32R) for p in "hl"] for n in range(2)]
        kT = [[m.sb(f"b_kT{p}{n}", [P, G1, S], F32R) for p in "hl"] for n in range(2)]
        v = [[m.sb(f"b_v{p}{n}", [P, ST, P], F32R) for p in "hl"] for n in range(2)]
        prob = [m.sb(f"b_prob{n}", [P, 3 * P]) for n in range(2)]
        pT = [[m.sb(f"b_pT{p}{n}", [P, 3 * P], F32R) for p in "hl"] for n in range(2)]
        mx = m.sb("b_mx", [P, 2, ST])
        sums = m.sb("b_sums", [P, 2, ST, NH1])
        inv = m.sb("b_inv", [P, ST, NH1])
        on = m.sb("b_on", [P, ST, D])
        oT = [m.sb(f"b_oT{p}", [P, CD, S], F32R) for p in "hl"]
        y = m.sb("b_y", [P, ST, D])
        st = m.sb("b_st", [P, 2, ST, 6])
        mv = m.sb("b_mv", [P, 2, ST, 2])
        nhalf = m.sb("b_nhalf", [P, ST])
        misc = [m.ps(f"b_misc{n}", [P, D]) for n in range(3)]
        sc = [m.ps(f"b_sc{n}", [P, 512]) for n in range(2)]
        pTp = m.ps("b_pTp", [P, 512])
        o = [m.ps(f"b_o{t}", [P, NH1, HD1]) for t in range(ST)]

        consts = m.sem("b_consts")
        dve_passed = m.sem("b_dve_passed")
        prep_act = m.sem("b_prep_act")
        prep_dve = m.sem("b_prep_dve")
        prep_pe = m.sem("b_prep_pe")
        x1_landed = m.sem("b_x1_landed")
        xb_done = m.sem("b_xb_done")
        fq_chain = m.sem("b_fq_chain")
        q_done = m.sem("b_q_done")
        misc_ready = m.sem("b_misc_ready")
        misc_used = m.sem("b_misc_used")
        hi_done = m.sem("b_hi_done")
        ln_chain = [m.sem(f"b_ln_chain{n}") for n in range(2)]
        ln_var = [m.sem(f"b_ln_var{n}") for n in range(2)]
        ln_rstd = [m.sem(f"b_ln_rstd{n}") for n in range(2)]
        x2_done = m.sem("b_x2_done")
        rope_done = m.sem("b_rope_done")
        sc_ready = m.sem("b_sc_ready")
        mx_ready = m.sem("b_mx_ready")
        ex_ready = m.sem("b_ex_ready")
        pt_ready = m.sem("b_pt_ready")
        pt_hi = m.sem("b_pt_hi")
        pt_lo = m.sem("b_pt_lo")
        pv_ready = m.sem("b_pv_ready")
        inv_ready = m.sem("b_inv_ready")
        on_done = m.sem("b_on_done")
        y_done = m.sem("b_y_done")
        stored = m.sem("b_stored")
        NLN, NFQ = 2, 4
        block = ctx.enter_context(nc.Block())

        @block.sync
        def _(sp):
            for dst, src in ((fraw[:, :], fw_in), (fbias[:, :], fb_in), (wraw[:, :, 0:D], wq_in),
                             (wraw[:, :, D:D + 2 * P], wkv_in), (wraw[:, :, D + 2 * P:], wo_in), (braw[:, :], bias_in),
                             (rope[:, :, :, :], rope_in), (mask[:, :], mask_in), (ident[:, :], ident_in),
                             (identb[:, :], identb_in)):
                sp.dma_start(dst, src).then_inc(consts, 16)
            h1_v = h1.rearrange("b (t p) d -> b p t d", p=P)
            h3_v = h3.rearrange("b (t p) d -> b p t d", p=P)

            def load(b):
                sp.wait_ge(q_done, b)
                sp.wait_ge(xb_done, b)
                sp.dma_start(x1[:, :, :], h1_v[bass.ds(b, 1)].rearrange("o p t d -> (o p) t d"))\
                  .then_inc(x1_landed, 16)

            def store(b):
                sp.wait_ge(y_done, b + 1)
                sp.dma_start(h3_v[bass.ds(b, 1)].rearrange("o p t d -> (o p) t d"), y[:, :, :]).then_inc(stored, 16)

            for b in range(3):
                load(b)
            with sp.Fori(0, B - 3) as i:
                store(i)
                load(i + 3)
            for b in range(B - 3, B):
                store(b)
            sp.wait_ge(stored, 16 * B)

        @block.tensor
        def _(pe):
            pe.sem_inc(pt_ready, 2)
            pe.sem_inc(pv_ready, 1)
            pe.wait_ge(prep_act, 7)
            pe.wait_ge(prep_dve, 1)
            pe.matmul(misc[0][:, 0:1], ones[:, :], asum[:, :], start=True, stop=True).then_inc(prep_pe, 1)
            pe.wait_ge(prep_dve, 6)

            def bank(seg, name):
                pe.wait_ge(misc_used, seg.unit(name))
                return misc[seg.bank(name)]

            def f_qT(seg):
                pe.wait_ge(q_done, seg.b + 2)
                for t in range(ST):
                    b = bank(seg, f"qT{t}")[:, :].bitcast(BF16)
                    for c in range(CD):
                        mm = pe.transpose(b[:, c * P:(c + 1) * P], qb[:, t, c * P:(c + 1) * P], identb[:, :])
                    mm.then_inc(misc_ready, 1)

            def f_ffn(seg):
                for t in range(ST):
                    b = bank(seg, f"ffn{t}")
                    pe.wait_ge(misc_used, seg.unit(f"qT{t}") + 3)
                    for c in range(CD):
                        mm = pe.matmul(b[:, :], qTb[:, t, c, :], fw[:, c, :], start=c == 0, stop=c == CD - 1)
                    mm.then_inc(misc_ready, 1)

            def f_xT(seg):
                pe.wait_ge(x2_done, seg.b + 2)
                for t in range(ST):
                    b = bank(seg, f"x{t}")
                    for c in range(CD):
                        mm = pe.transpose(b[:, c * P:(c + 1) * P], x2[1 - seg.parity][:, t, c * P:(c + 1) * P],
                                          ident[:, :])
                    mm.then_inc(misc_ready, 1)

            def f_proj(seg, t):
                for name, w, a, n in (("q", wq, 0, D), ("kv", wkv, D, 2 * P)):
                    b = bank(seg, f"{name}{t}")
                    pe.wait_ge(misc_used, seg.unit("x1") + 3)
                    pe.matmul(b[:, 0:n], onesr[:, :], bqkv[:, a:a + n], start=True, stop=False)
                    for c in range(CD):
                        for x in xT:
                            mm = pe.matmul(b[:, 0:n], x[:, c, t * P:(t + 1) * P], w[:, c, :], start=False,
                                           stop=c == CD - 1 and x is xT[1])
                    mm.then_inc(misc_ready, 1)

            def f_hT(seg, t):
                pe.wait_ge(rope_done, seg.b * ST + (ST + t + 1))
                for name, src in (("tq", qr), ("tk", kr)):
                    b = bank(seg, f"{name}{t}")
                    for c in range(CD):
                        mm = pe.transpose(b[:, c * P:(c + 1) * P], src[:, t, c * P:(c + 1) * P], ident[:, :])
                    mm.then_inc(misc_ready, 1)

            def score(seg, s):
                if s == 0:
                    pe.wait_ge(misc_used, seg.unit0 + 3)
                pe.wait_ge(mx_ready, seg.b * NH1 + (s + 1))
                g, r = s // 4, slice(32 * (s % 4), 32 * (s % 4) + 32)
                qs, ks = qT[seg.parity], kT[seg.parity]
                mm3(pe, sc[s % 2][:, 0:P], [x[r, g, 0:P] for x in qs], [x[r, g, 0:P] for x in ks], True, True)
                mm3(pe, sc[s % 2][:, P:3 * P], [x[r, g, P:S] for x in qs], [x[r, g, :] for x in ks], True, True)\
                    .then_inc(sc_ready, 1)

            def pt(seg, s):
                pe.wait_ge(ex_ready, seg.b * NH1 + (s + 1))
                pe.wait_ge(pt_lo, seg.b * NH1 + s)
                for c in range(3):
                    mm = pe.transpose(pTp[:, c * P:(c + 1) * P], prob[s % 2][:, c * P:(c + 1) * P], ident[:, :])
                mm.then_inc(pt_ready, 1)

            def pv(seg, s):
                pe.wait_ge(pt_lo, seg.b * NH1 + (s + 1))
                if s == 0:
                    pe.wait_ge(on_done, seg.b)
                p, vs, g = pT[s % 2], v[seg.parity], slice(s // 4 * HD1, s // 4 * HD1 + HD1)
                mm3(pe, o[0][:, s, :], [x[:, 0:P] for x in p], [x[:, 0, g] for x in vs], True, True)
                mm3(pe, o[1][:, s, :], [x[:, P:2 * P] for x in p], [x[:, 0, g] for x in vs], True, False)
                mm3(pe, o[1][:, s, :], [x[:, 2 * P:3 * P] for x in p], [x[:, 1, g] for x in vs], False, True)\
                    .then_inc(pv_ready, 1)

            def g_oT(seg):
                pe.wait_ge(on_done, seg.b)
                for t in range(ST):
                    b = bank(seg, f"oT{t}")
                    for c in range(CD):
                        mm = pe.transpose(b[:, c * P:(c + 1) * P], on[:, t, c * P:(c + 1) * P], ident[:, :])
                    mm.then_inc(misc_ready, 1)

            def g_out(seg):
                for t in range(ST):
                    b = bank(seg, f"out{t}")
                    pe.wait_ge(misc_used, seg.unit(f"oT{t}") + 3)
                    for c in range(CD):
                        for x in oT:
                            mm = pe.matmul(b[:, :], x[:, c, t * P:(t + 1) * P], wo[:, c, :],
                                           start=c == 0 and x is oT[0], stop=c == CD - 1 and x is oT[1])
                    mm.then_inc(misc_ready, 1)

            all_segments(pe, {"f_qT": f_qT, "f_ffn": f_ffn, "f_xT": f_xT, "f_proj": f_proj, "f_hT": f_hT,
                              "sc": score, "pt": pt, "pv": pv, "g_oT": g_oT, "g_out": g_out})

        @block.scalar
        def _(act):
            act.wait_ge(consts, 160)
            act.activation(ftmp[:, :], fraw[:, :], ACT.Abs, accum_out=asum[:, :]).then_inc(prep_act, 1)
            act.activation(wq[:, :, :], wraw[:, :, 0:D], ACT.Copy).then_inc(prep_act, 1)
            act.activation(wkv[:, :, :], wraw[:, :, D:D + 2 * P], ACT.Copy).then_inc(prep_act, 1)
            act.activation(wo[:, :, :], wraw[:, :, D + 2 * P:], ACT.Copy).then_inc(prep_act, 1)
            act.activation(bqkv[:, :], braw[:, :], ACT.Copy).then_inc(prep_act, 1)
            act.wait_ge(prep_dve, 1)
            act.activation(onesr[:, :], ones[0:1, :], ACT.Copy).then_inc(prep_act, 2)

            def f_xT(seg):
                for t in range(ST):
                    act.wait_ge(misc_ready, seg.unit(f"x{t}"))
                    act.activation(xT[0][:, :, t * P:(t + 1) * P],
                                   misc[seg.bank(f"x{t}")][:, :].rearrange("p (c s) -> p c s", c=CD),
                                   ACT.Copy).then_inc(hi_done, 1)

            def f_proj(seg, t):
                act.wait_ge(misc_ready, seg.unit(f"kv{t}"))
                act.activation(v[1 - seg.parity][0][:, t, :], misc[seg.bank(f"kv{t}")][:, P:2 * P],
                               ACT.Copy).then_inc(hi_done, 1)

            def f_hT(seg, t):
                for name, dst in (("tq", qT), ("tk", kT)):
                    act.wait_ge(misc_ready, seg.unit(f"{name}{t}"))
                    act.activation(dst[1 - seg.parity][0][:, :, t * P:(t + 1) * P],
                                   misc[seg.bank(f"{name}{t}")][:, :].rearrange("p (c s) -> p c s", c=G1),
                                   ACT.Copy).then_inc(hi_done, 1)

            def ex(seg, s):
                act.wait_ge(mx_ready, seg.b * NH1 + (s + 3))
                for t, (a, b) in enumerate(((0, P), (P, 3 * P))):
                    ins = act.activation(prob[s % 2][:, a:b], prob[s % 2][:, a:b], ACT.Exp,
                                         bias=mx[:, s % 2, t:t + 1], scale=-1.0,
                                         accum_out=sums[:, seg.parity, t, s:s + 1])
                ins.then_inc(ex_ready, 1)

            def pt(seg, s):
                act.wait_ge(pt_ready, seg.b * NH1 + (s + 3))
                act.wait_ge(pv_ready, seg.b * NH1 + s)
                act.activation(pT[s % 2][0][:, :], pTp[:, 0:3 * P], ACT.Copy).then_inc(pt_hi, 1)

            def g_oT(seg):
                for t in range(ST):
                    act.wait_ge(misc_ready, seg.unit(f"oT{t}"))
                    act.activation(oT[0][:, :, t * P:(t + 1) * P],
                                   misc[seg.bank(f"oT{t}")][:, :].rearrange("p (c s) -> p c s", c=CD),
                                   ACT.Copy).then_inc(hi_done, 1)

            all_segments(act, {"f_xT": f_xT, "f_proj": f_proj, "f_hT": f_hT, "ex": ex, "pt": pt, "g_oT": g_oT})

        @block.gpsimd
        def _(pool):
            pool.memset(nhalf[:, :], -0.5)
            pool.wait_ge(consts, 160)

            def f_quant(seg):
                pool.wait_ge(x1_landed, seg.b * 16 + 32)
                pool.wait_ge(x2_done, seg.b + 1)
                pool.tensor_tensor(xb[:, :, :], x1[:, :, :], fbias[:, :].unsqueeze(1).broadcast_to([P, ST, D]),
                                   ALU.add).then_inc(xb_done, 1)

            def rstd(n, images):
                pool.wait_ge(ln_var[n], images)
                pool.tensor_tensor(mv[:, n, :, 1], mv[:, n, :, 1], nhalf[:, :], ALU.pow).then_inc(ln_rstd[n], 1)

            def f_proj(seg, t):
                pool.wait_ge(misc_used, seg.unit(f"q{t}") + 3)
                pool.tensor_tensor(qr[:, t, :], tq[0][:, :], tq[1][:, :], ALU.add)
                pool.wait_ge(misc_used, seg.unit(f"kv{t}") + 3)
                shape = [P, G1, 4, HD1]
                a, b = [x[:, :].rearrange("p (g d) -> p g d", g=G1).unsqueeze(2).broadcast_to(shape) for x in tk]
                pool.tensor_tensor(kr[:, t, :].rearrange("p (g r d) -> p g r d", g=G1, r=4), a, b,
                                   ALU.add).then_inc(rope_done, 1)

            all_segments(pool, {"f_quant": f_quant, "f_ffn": lambda seg: rstd(0, seg.b + 2), "f_proj": f_proj,
                                "g_out": lambda seg: rstd(1, seg.b)})

        @block.vector
        def _(dve):
            dve.sem_inc(misc_used, 3)
            dve.sem_inc(mx_ready, 2)
            dve.memset(ones[:, :], 1.0).then_inc(prep_dve, 1)
            dve.wait_ge(prep_pe, 1)
            c = Chain(dve, prep_dve, 1)
            c(dve.tensor_scalar(alpha[:, 0:1], misc[0][:, 0:1], 1.0 / (D * D), QEPS, ALU.mult, ALU.max))
            c(dve.reciprocal(alpha[:, 1:2], alpha[:, 0:1]))
            c(dve.tensor_scalar(ftmp[:, :], fraw[:, :], alpha[:, 1:2], ROUND, ALU.mult, ALU.add))
            c(dve.tensor_scalar(ftmp[:, :], ftmp[:, :], ROUND, 1.0, ALU.subtract, ALU.min))
            c(dve.tensor_scalar(fw[:, :, :].rearrange("p c n -> p (c n)"), ftmp[:, :], -1.0, None, ALU.max))

            def f_quant(seg):
                c = Chain(dve, fq_chain, seg.b * NFQ + NFQ)
                dve.wait_ge(x1_landed, seg.b * 16 + 32)
                c(dve.tensor_reduce(am[:, :], x1[:, :, :], AX_X, ALU.max, apply_absolute_value=True))
                c(dve.tensor_scalar(am[:, :], am[:, :], QEPS, 1.0 / 127.0, ALU.max, ALU.mult))
                c(dve.reciprocal(rs[:, :], am[:, :]))
                dve.tensor_scalar(sa[:, :], am[:, :], alpha[:, 0:1], None, ALU.mult)
                for t in range(ST):
                    ins = dve.tensor_scalar(qf[:, t, :], x1[:, t, :], rs[:, t:t + 1], ROUND, ALU.mult, ALU.add)
                c(ins)
                dve.tensor_scalar(qb[:, :, :], qf[:, :, :], ROUND, 127.0, ALU.subtract, ALU.min).then_inc(q_done, 1)

            def f_qT(seg):
                for t in range(ST):
                    dve.wait_ge(misc_ready, seg.unit(f"qT{t}"))
                    dve.tensor_copy(qTb[:, t, :, :].rearrange("p c s -> p (c s)"),
                                    misc[seg.bank(f"qT{t}")][:, :].bitcast(BF16)[:, 0:D]).then_inc(misc_used, 1)

            def norm(n, images, out, done):
                c = Chain(dve, ln_chain[n], images * NLN - NLN)
                for t in range(ST):
                    ins = dve.bn_stats(st[:, n, t, :], out[:, t, :])
                c(ins)
                carry_wait(dve, dve_passed)
                for t in range(ST):
                    ins = dve.bn_aggr(mv[:, n, t, :], st[:, n, t, :])
                c(ins)
                dve.tensor_scalar(mv[:, n, :, 1], mv[:, n, :, 1], LN_EPS, None, ALU.add).then_inc(ln_var[n], 1)
                dve.wait_ge(ln_rstd[n], images)
                for t in range(ST):
                    ins = dve.tensor_scalar(out[:, t, :], out[:, t, :], mv[:, n, t, 0:1], mv[:, n, t, 1:2],
                                            ALU.subtract, ALU.mult)
                ins.then_inc(done, 1)

            def f_ffn(seg):
                x = x2[1 - seg.parity]
                dve.wait_ge(xb_done, seg.b + 2)
                for t in range(ST):
                    dve.wait_ge(misc_ready, seg.unit(f"ffn{t}"))
                    dve.scalar_tensor_tensor(x[:, t, :], misc[seg.bank(f"ffn{t}")][:, :], sa[:, t:t + 1],
                                             xb[:, t, :], ALU.mult, ALU.add).then_inc(misc_used, 1)
                dve.wait_ge(misc_used, seg.unit("ffn1") + 3)
                norm(0, seg.b + 2, x, x2_done)

            def lo(seg, name, hi_name, out, hi, a=0, n=D):
                dve.wait_ge(hi_done, seg.hi(hi_name))
                b = misc[seg.bank(name)][:, a:a + n]
                if len(out.shape) == 3:
                    b = b.rearrange("p (c s) -> p c s", c=CD)
                dve.tensor_tensor(out, b, hi.bitcast(F32), ALU.subtract).then_inc(misc_used, 1)

            def f_xT(seg):
                for t in range(ST):
                    sl = slice(t * P, (t + 1) * P)
                    lo(seg, f"x{t}", f"x{t}", xT[1][:, :, sl], xT[0][:, :, sl])

            def turn(b, t, out, heads):
                x = b.rearrange("p (h two d) -> p h two d", two=2, d=HD1 // 2)
                t1, t2 = out
                r1 = t1[:, :].rearrange("p (h d) -> p h d", d=HD1)
                r2 = t2[:, :].rearrange("p (h two d) -> p h two d", two=2, d=HD1 // 2)
                cs = rope[:, 0, t, :].unsqueeze(1).broadcast_to([P, heads, HD1])
                half = [P, heads, HD1 // 2]
                dve.tensor_tensor(r2[:, :, 0, :], x[:, :, 1, :],
                                  rope[:, 1, t, 0:HD1 // 2].unsqueeze(1).broadcast_to(half), ALU.mult)
                dve.tensor_tensor(r2[:, :, 1, :], x[:, :, 0, :],
                                  rope[:, 1, t, HD1 // 2:].unsqueeze(1).broadcast_to(half), ALU.mult)
                return dve.tensor_tensor(r1, b.rearrange("p (h d) -> p h d", d=HD1), cs, ALU.mult)

            def f_proj(seg, t):
                dve.wait_ge(rope_done, seg.b * ST + (ST + t))
                dve.wait_ge(misc_ready, seg.unit(f"q{t}"))
                turn(misc[seg.bank(f"q{t}")][:, :], t, tq, NH1).then_inc(misc_used, 1)
                dve.wait_ge(hi_done, seg.hi(f"v{t}"))
                turn(misc[seg.bank(f"kv{t}")][:, 0:P], t, tk, G1)
                vv = v[1 - seg.parity]
                lo(seg, f"kv{t}", f"v{t}", vv[1][:, t, :], vv[0][:, t, :], P, P)

            def f_hT(seg, t):
                sl = slice(t * P, (t + 1) * P)
                for name, dst in (("tq", qT), ("tk", kT)):
                    d = dst[1 - seg.parity]
                    lo(seg, f"{name}{t}", f"{name}{t}", d[1][:, :, sl], d[0][:, :, sl])

            def maxima(seg, s):
                dve.wait_ge(sc_ready, seg.b * NH1 + (s + 1))
                dve.wait_ge(pt_ready, seg.b * NH1 + (s + 1))
                carry_wait(dve, dve_passed)
                for t, (a, b) in enumerate(((0, P), (P, 3 * P))):
                    ins = dve.tensor_tensor_reduce(out=prob[s % 2][:, a:b], in0=sc[s % 2][:, a:b],
                                                   in1=mask[:, 2 * P - (b - a):2 * P], scale=-SCALE, scalar=BIG,
                                                   op0=ALU.add, op1=ALU.min, accum_out=mx[:, s % 2, t:t + 1])
                ins.then_inc(mx_ready, 1)

            def pt(seg, s):
                dve.wait_ge(pt_hi, seg.b * NH1 + (s + 1))
                dve.tensor_tensor(pT[s % 2][1][:, :], pTp[:, 0:3 * P], pT[s % 2][0][:, :].bitcast(F32),
                                  ALU.subtract).then_inc(pt_lo, 1)

            def g_norm(seg):
                dve.wait_ge(pv_ready, seg.b * NH1 + 1)
                dve.wait_ge(ex_ready, seg.b * NH1)
                dve.reciprocal(inv[:, :, :], sums[:, 1 - seg.parity, :, :]).then_inc(inv_ready, 1)
                dve.wait_ge(inv_ready, seg.b)
                for t in range(ST):
                    ins = dve.tensor_tensor(on[:, t, :].rearrange("p (h d) -> p h d", h=NH1), o[t][:, :, :],
                                            inv[:, t, :].unsqueeze(2).broadcast_to([P, NH1, HD1]), ALU.mult)
                ins.then_inc(on_done, 1)

            def g_oT(seg):
                for t in range(ST):
                    sl = slice(t * P, (t + 1) * P)
                    lo(seg, f"oT{t}", f"oT{t}", oT[1][:, :, sl], oT[0][:, :, sl])

            def g_out(seg):
                dve.wait_ge(stored, seg.b * 16 - 16)
                for t in range(ST):
                    dve.wait_ge(misc_ready, seg.unit(f"out{t}"))
                    dve.tensor_tensor(y[:, t, :], misc[seg.bank(f"out{t}")][:, :], x2[1 - seg.parity][:, t, :],
                                      ALU.add).then_inc(misc_used, 1)
                dve.wait_ge(misc_used, seg.unit("out1") + 3)
                norm(1, seg.b, y, y_done)

            all_segments(dve, {"f_quant": f_quant, "f_qT": f_qT, "f_ffn": f_ffn, "f_xT": f_xT, "f_proj": f_proj,
                               "f_hT": f_hT, "mx": maxima, "pt": pt, "g_norm": g_norm, "g_oT": g_oT,
                               "g_out": g_out})


E, F, TOPK = 8, 256, 2
CF = F // P
T = B * S
TT = T // P
ROWS = 4
CHUNK = ROWS * P
SHARED = T // CHUNK
SLOTS = (TOPK * T + E * (CHUNK - 1)) // CHUNK
ITEMS = SHARED + SLOTS
NL = SLOTS * ROWS
WCOLS = 2 * CD * F + CF * D
W_PARTS = ((0, CD * F), (CD * F, 2 * CD * F), (2 * CD * F, WCOLS))
RMS_EPS = 1e-6


def experts(nc, w_in, rms_in, router_in, tri_in, small_in, tok_in, ident_in, h3, ht, token_list, ys, out):
    with ExitStack() as octx:
        om = Memory(nc, octx)
        res = om.sb("e_res", [P, TT, D])
        place = om.sb("e_place", [P, 2, TT], mybir.dt.uint32)
        share = om.sb("e_share", [P, 2, TT])
        with ExitStack() as ctx:
            expert_items(nc, Memory(nc, ctx), res, place, share, w_in, rms_in, router_in, tri_in, small_in, tok_in,
                         ident_in, h3, ht, token_list, ys)
        with ExitStack() as ctx:
            combine(nc, Memory(nc, ctx), res, place, share, ys, out)


class Item:

    def __init__(self, n, slot, parity, n_static=None):
        self.n, self.slot, self.parity = n, slot, parity
        self.j = n - (SHARED - 1) if slot else 0
        self.wbuf = (parity + 1) % 2 if slot else 0


def item_segments(eng, h):

    def call(name, *args):
        if name in h:
            h[name](*args)

    def segment(n, parity, slot, slot_before, slot_next, first=False, last=False):
        it = Item(n, slot, parity)
        call("gu", it, 0)
        if not last:
            call("inputs", Item(n + 1, slot_next, 1 - parity))
        if not first:
            call("down", Item(n - 1, slot_before, 1 - parity))
        if not last and slot_next:
            call("weights", Item(n + 1, True, 1 - parity))
        call("gu", it, 1)

    call("weights", Item(0, False, 0))
    call("inputs", Item(0, False, 0))
    segment(0, 0, False, False, False, first=True)
    segment(1, 1, False, False, False)
    with eng.Fori(0, (SHARED - 4) // 2) as i:
        segment(i * 2 + 2, 0, False, False, False)
        segment(i * 2 + 3, 1, False, False, False)
    segment(SHARED - 2, 0, False, False, False)
    segment(SHARED - 1, 1, False, False, True)
    segment(SHARED, 0, True, False, True)
    segment(SHARED + 1, 1, True, True, True)
    pairs = (SLOTS - 2 - 2) // 2
    with eng.Fori(0, pairs) as i:
        segment(i * 2 + (SHARED + 2), 0, True, True, True)
        segment(i * 2 + (SHARED + 3), 1, True, True, True)
    for n in range(SHARED + 2 + 2 * pairs, ITEMS):
        segment(n, n % 2, True, True, True, last=n == ITEMS - 1)
    call("down", Item(ITEMS - 1, True, (ITEMS - 1) % 2))


def expert_items(nc, m, res, place, share, w_in, rms_in, router_in, tri_in, small_in, tok_in, ident_in, h3, ht,
                 token_list, ys):
    U32 = mybir.dt.uint32
    ident = m.sb("e_ident", [P, P])
    rms = m.sb("e_rms", [P, D])
    rraw = m.sb("e_rraw", [P, CD, E])
    router = [m.sb(f"e_router{p}", [P, CD, E], F32R) for p in "hl"]
    tri = m.sb("e_tri", [P, 2, P])
    small = m.sb("e_small", [P, E + SLOTS + 1])
    tok = m.sb("e_tok", [P, TT], U32)
    xin = m.sb("e_xin", [P, ROWS, D])
    ss = m.sb("e_ss", [P, ROWS])
    xT = [[m.sb(f"e_xT{p}{n}", [P, CD, CHUNK], F32R) for p in "hl"] for n in range(2)]
    aT = [[m.sb(f"e_aT{p}{n}", [P, CF, CHUNK], F32R) for p in "hl"] for n in range(2)]
    sg = [m.sb(f"e_sg{f}", [P, CHUNK]) for f in range(CF)]
    wraw = m.sb("e_wraw", [P, WCOLS])
    wb = [[m.sb(f"e_w{p}{n}", [P, WCOLS], F32R) for p in "hl"] for n in range(2)]
    yb = m.sb("e_yb", [P, ROWS, D])
    lg = m.sb("e_lg", [P, TT, E])
    top = m.sb("e_top", [P, TT, 8])
    topi = m.sb("e_topi", [P, TT, 8], U32)
    oh = m.sb("e_oh", [P, 2, TT, E])
    mm_ = m.sb("e_mm", [P, TT, E])
    cum = m.sb("e_cum", [P, E, TT])
    tot = m.sb("e_tot", [P, E, TT])
    blk = m.sb("e_blk", [P, 4, E])
    fl = m.sb("e_fl", [P, 2, TT])
    fj = m.sb("e_fj", [P, 2, TT])
    addr = m.sb("e_addr", [P, 2, TT], U32)
    own = m.sb("e_own", [1, SLOTS, E])
    ownf = m.sb("e_ownf", [1, SLOTS])
    owner = m.sb("e_owner", [1, SLOTS], I32)
    idx = m.sb("e_idx", [P, NL], U32)
    idx4 = m.sb("e_idx4", [P, ROWS], U32)
    tp = [m.ps(f"e_tp{n}", [P, D]) for n in range(2)]
    gu = [m.ps(f"e_gu{n}", [P, CHUNK]) for n in range(4)]
    dn = [m.ps(f"e_dn{n}", [P, D]) for n in range(2)]

    consts = m.sem("e_consts")
    pool_passed = m.sem("e_pool_passed")
    res_landed = [m.sem(f"e_res_landed{n}") for n in range(2)]
    ss_done = m.sem("e_ss_done")
    ms_done = m.sem("e_ms_done")
    rs_done = m.sem("e_rs_done")
    ht_done = m.sem("e_ht_done")
    ht_stored = m.sem("e_ht_stored")
    r_prep = m.sem("e_r_prep")
    c_t = m.sem("e_c_t")
    c_hi = m.sem("e_c_hi")
    c_lo = m.sem("e_c_lo")
    c_lg = m.sem("e_c_lg")
    c_lgd = m.sem("e_c_lgd")
    rt = m.sem("e_rt")
    rt_mm = m.sem("e_rt_mm")
    rt_pe = m.sem("e_rt_pe")
    rt_exp = m.sem("e_rt_exp")
    rt_done = m.sem("e_rt_done")
    zeroed = m.sem("e_zeroed")
    listed = m.sem("e_listed")
    idx_landed = m.sem("e_idx_landed")
    idx_copied = m.sem("e_idx_copied")
    x_landed = m.sem("e_x_landed")
    g_landed = m.sem("e_g_landed")
    t_ready = m.sem("e_t_ready")
    x_hi = m.sem("e_x_hi")
    x_lo = m.sem("e_x_lo")
    gu_ready = m.sem("e_gu_ready")
    silu_done = m.sem("e_silu_done")
    mul_done = m.sem("e_mul_done")
    a_hi = m.sem("e_a_hi")
    a_lo = m.sem("e_a_lo")
    d_ready = m.sem("e_d_ready")
    d_used = m.sem("e_d_used")
    y_stored = m.sem("e_y_stored")
    raw_landed = m.sem("e_raw_landed")
    w_hi = m.sem("e_w_hi")
    w_lo = m.sem("e_w_lo")
    block = m.ctx.enter_context(nc.Block())

    def gate(w, c, f):
        return w[:, c * F + f * P:c * F + f * P + P]

    def up(w, c, f):
        return w[:, CD * F + c * F + f * P:CD * F + c * F + f * P + P]

    def down_w(w, f):
        return w[:, 2 * CD * F + f * D:2 * CD * F + (f + 1) * D]

    @block.sync
    def _(sp):
        for dst, src in ((ident[:, :], ident_in), (rms[:, :], rms_in), (rraw[:, :, :], router_in),
                         (tri[:, :, :], tri_in), (small[:, :], small_in), (tok[:, :], tok_in)):
            sp.dma_start(dst, src).then_inc(consts, 16)
        h3_v = h3.rearrange("b (t p) d -> p (b t) d", p=P)
        ht_v = ht.rearrange("(t p) d -> p t d", p=P)

        def load_res(k, par):
            sp.dma_start(res[:, bass.ds(k * ROWS, ROWS), :], h3_v[:, bass.ds(k * ROWS, ROWS), :])\
              .then_inc(res_landed[par], 16)

        def store_ht(k):
            sp.wait_ge(ht_done, k + 1)
            sp.dma_start(ht_v[:, bass.ds(k * ROWS, ROWS), :], xin[:, :, :]).then_inc(ht_stored, 16)

        load_res(0, 0)
        load_res(1, 1)
        sp.dma_start(wraw[:, :], w_in[E]).then_inc(raw_landed, 16)
        with sp.Fori(0, SHARED // 2 - 1) as i:
            for par in range(2):
                sp.wait_ge(ss_done, i * 2 + (par + 1))
                load_res(i * 2 + (par + 2), par)
                store_ht(i * 2 + par)
        store_ht(SHARED - 2)
        store_ht(SHARED - 1)
        sp.wait_ge(ht_stored, 16 * SHARED)

        def load_x(n):
            sp.dma_start(xin[:, :, :], ht_v[:, bass.ds(n * ROWS, ROWS), :]).then_inc(x_landed, 16)

        sp.wait_ge(c_t, 4 * SHARED + 2)
        load_x(0)

        def load_w(j, s):
            sp.wait_ge(w_lo, j * 3)
            e = sp.value_load(owner[0:1, bass.ds(s, 1)], min_val=0, max_val=E - 1)
            sp.dma_start(wraw[:, :], w_in[bass.ds(e, 1)].rearrange("o p n -> (o p) n")).then_inc(raw_landed, 16)

        def after_inputs(it):
            if not it.slot and not (isinstance(it.n, int) and it.n >= SHARED - 1):
                sp.wait_ge(t_ready, it.n * 4 + 4)
                load_x(it.n + 1)

        def after_down(it):
            if it.slot:
                sp.wait_ge(d_used, it.n * 4 + 6)
                s = it.n - SHARED
                sp.dma_start(ys[bass.ds(s, 1)].rearrange("o p r d -> (o p) r d"), yb[:, :, :]).then_inc(y_stored, 16)

        def after_weights(it):
            if isinstance(it.n, int) and (it.n == 0 or it.n == ITEMS - 1):
                if it.n == 0:
                    sp.wait_ge(rt_done, 1)
                    load_w(1, 0)
                return
            load_w(it.j + 1, it.n + 1 - SHARED)

        item_segments(sp, {"inputs": after_inputs, "down": after_down, "weights": after_weights})
        sp.wait_ge(y_stored, 16 * SLOTS)

    @block.tensor
    def _(pe):
        pe.sem_inc(c_t, 2)
        pe.wait_ge(consts, 96)
        pe.wait_ge(r_prep, 2)
        with pe.Fori(0, SHARED // 2) as i:
            for par in range(2):
                k = i * 2 + par
                pe.wait_ge(ht_done, k + 1)
                for t in range(ROWS):
                    pe.wait_ge(c_lo, k * ROWS + t)
                    for c in range(CD):
                        mm = pe.transpose(tp[t % 2][:, c * P:(c + 1) * P], xin[:, t, c * P:(c + 1) * P], ident[:, :])
                    mm.then_inc(c_t, 1)
                pe.wait_ge(c_lo, k * ROWS + (ROWS + 1))
                pe.wait_ge(c_lgd, k)
                for t in range(ROWS):
                    for c in range(CD):
                        mm = mm3(pe, dn[0][:, t * E:(t + 1) * E], [x[:, c, t * P:(t + 1) * P] for x in xT[par]],
                                 [x[:, c, :] for x in router], c == 0, c == CD - 1)
                mm.then_inc(c_lg, 1)
        pe.wait_ge(rt_mm, 1)
        flat = mm_[:, :, :].rearrange("p t e -> p (t e)")
        pe.matmul(dn[0][:, 0:TT * E], tri[:, 0, :], flat, start=True, stop=True)
        pe.matmul(dn[1][:, 0:TT * E], tri[:, 1, :], flat, start=True, stop=True).then_inc(rt_pe, 1)

        def inputs(it):
            if it.slot:
                pe.wait_ge(g_landed, it.n * (16 * ROWS) - (SHARED - 1) * (16 * ROWS))
            else:
                pe.wait_ge(x_landed, it.n * 16 + 16)
            for t in range(ROWS):
                pe.wait_ge(x_lo, it.n * 4 + (t + 1))
                for c in range(CD):
                    mm = pe.transpose(tp[t % 2][:, c * P:(c + 1) * P], xin[:, t, c * P:(c + 1) * P], ident[:, :])
                mm.then_inc(t_ready, 1)

        def gate_up(it, f):
            if f == 0:
                pe.wait_ge(x_lo, it.n * 4 + 6)
                pe.wait_ge(w_lo, it.j * 3 + 2)
            pe.wait_ge(mul_done, it.n * 2 + (f + 1))
            x, w = xT[it.parity], wb[it.wbuf]
            for k, part in enumerate((gate, up)):
                for c in range(CD):
                    mm = mm3(pe, gu[2 * f + k][:, :], [part(y, c, f) for y in w], [y[:, c, :] for y in x], c == 0,
                             c == CD - 1)
                mm.then_inc(gu_ready, 1)

        def down(it):
            pe.wait_ge(a_lo, it.n * 2 + 2)
            pe.wait_ge(w_lo, it.j * 3 + 3)
            a, w = aT[it.parity], wb[it.wbuf]
            for t in range(ROWS):
                pe.wait_ge(d_used, it.n * 4 + (t + 1))
                for f in range(CF):
                    mm = mm3(pe, dn[t % 2][:, :], [y[:, f, t * P:(t + 1) * P] for y in a], [down_w(y, f) for y in w],
                             f == 0, f == CF - 1)
                mm.then_inc(d_ready, 1)

        pe.wait_ge(rt_done, 1)
        item_segments(pe, {"inputs": inputs, "gu": gate_up, "down": down})

    @block.scalar
    def _(act):
        act.wait_ge(consts, 96)
        act.activation(router[0][:, :, :], rraw[:, :, :], ACT.Copy).then_inc(r_prep, 1)
        with act.Fori(0, SHARED // 2) as i:
            for par in range(2):
                k = i * 2 + par
                act.wait_ge(res_landed[par], i * 16 + 16)
                act.wait_ge(ht_done, k)
                for t in range(ROWS):
                    ins = act.activation(yb[:, t, :], res[:, bass.ds(k * ROWS + t, 1), :].rearrange(
                        "p o d -> p (o d)"), ACT.Square, accum_out=ss[:, t:t + 1])
                ins.then_inc(ss_done, 1)
                for t in range(ROWS):
                    act.wait_ge(c_t, k * ROWS + (t + 3))
                    act.activation(xT[par][0][:, :, t * P:(t + 1) * P],
                                   tp[t % 2][:, :].rearrange("p (c s) -> p c s", c=CD), ACT.Copy).then_inc(c_hi, 1)
        act.wait_ge(rt, 2)
        act.activation(share[:, 1, :], fl[:, 0, :], ACT.Exp).then_inc(rt_exp, 1)

        def inputs(it):
            for t in range(ROWS):
                act.wait_ge(t_ready, it.n * 4 + (t + 1))
                if t == 0 and not (isinstance(it.n, int) and it.n < 1):
                    act.wait_ge(gu_ready, it.n * 4 - 4)
                act.activation(xT[it.parity][0][:, :, t * P:(t + 1) * P],
                               tp[t % 2][:, :].rearrange("p (c s) -> p c s", c=CD), ACT.Copy).then_inc(x_hi, 1)

        def gate_up(it, f):
            act.wait_ge(gu_ready, it.n * 4 + (2 * f + 1))
            if not (isinstance(it.n, int) and it.n < 1):
                act.wait_ge(a_lo, it.n * 2 + (f - 1))
            act.activation(sg[f][:, :], gu[2 * f][:, :], ACT.Silu).then_inc(silu_done, 1)
            act.wait_ge(mul_done, it.n * 2 + (f + 3))
            if f == 0 and not (isinstance(it.n, int) and it.n < 1):
                act.wait_ge(d_ready, it.n * 4 - 4)
            act.activation(aT[it.parity][0][:, f, :], sg[f][:, :], ACT.Copy).then_inc(a_hi, 1)

        def weights(it):
            act.wait_ge(raw_landed, it.j * 16 + 16)
            if it.slot:
                act.wait_ge(d_ready, it.n * 4 - 4)
            for a, b in W_PARTS:
                act.activation(wb[it.wbuf][0][:, a:b], wraw[:, a:b], ACT.Copy).then_inc(w_hi, 1)

        item_segments(act, {"inputs": inputs, "gu": gate_up, "weights": weights})

    @block.gpsimd
    def _(pool):
        pool.wait_ge(consts, 96)
        pool.memset(idx[:, :], 0)  .then_inc(zeroed, 1)
        pool.wait_ge(zeroed, 1)
        list_v = token_list.rearrange("(p n) o -> p (n o)", p=P)
        pool.dma_start(list_v, idx[:, :]).then_inc(listed, 16)
        nh = small[:, E + SLOTS:E + SLOTS + 1].broadcast_to([P, ROWS])
        with pool.Fori(0, SHARED) as k:
            pool.wait_ge(ss_done, k + 1)
            pool.wait_ge(ht_done, k)
            carry_wait(pool, pool_passed)
            pool.tensor_scalar(ss[:, :], ss[:, :], 1.0 / D, RMS_EPS, ALU.mult, ALU.add).then_inc(ms_done, 1)
            pool.wait_ge(ms_done, k + 1)
            pool.tensor_tensor(ss[:, :], ss[:, :], nh, ALU.pow).then_inc(rs_done, 1)
        pool.wait_ge(rt_done, 1)
        pool.wait_ge(listed, 16)
        for t in range(TT):
            for k in range(2):
                pool.indirect_dma_start(token_list, bass.IndirectOffsetOnAxis(addr[:, k, t:t + 1], 0),
                                        tok[:, t:t + 1], None).then_inc(listed, 16)
        pool.wait_ge(listed, 16 + 16 * 2 * TT)
        pool.dma_start(idx[:, :], list_v).then_inc(idx_landed, 16)
        pool.wait_ge(idx_landed, 16)

        def gather(n):
            s = n - SHARED
            pool.tensor_copy(idx4[:, :], idx[:, bass.ds(s * ROWS, ROWS)]).then_inc(idx_copied, 1)
            pool.wait_ge(idx_copied, s + 1)
            carry_wait(pool, pool_passed)
            for r in range(ROWS):
                pool.indirect_dma_start(xin[:, r, :], None, ht, bass.IndirectOffsetOnAxis(idx4[:, r:r + 1], 0))\
                    .then_inc(g_landed, 16)

        def after_inputs(it):
            if isinstance(it.n, int) and (it.n < SHARED - 1 or it.n == ITEMS - 1) or not it.slot and not isinstance(
                    it.n, int):
                return
            pool.wait_ge(t_ready, it.n * 4 + 4)
            gather(it.n + 1)

        item_segments(pool, {"inputs": after_inputs})

    @block.vector
    def _(dve):
        dve.sem_inc(c_lo, 1)
        dve.sem_inc(x_lo, 2)
        dve.sem_inc(mul_done, 2)
        dve.sem_inc(d_used, 2)
        dve.wait_ge(consts, 96)
        dve.wait_ge(r_prep, 1)
        dve.tensor_tensor(router[1][:, :, :], rraw[:, :, :], router[0][:, :, :].bitcast(F32), ALU.subtract)\
           .then_inc(r_prep, 1)
        with dve.Fori(0, SHARED // 2) as i:
            for par in range(2):
                k = i * 2 + par
                dve.wait_ge(rs_done, k + 1)
                dve.wait_ge(c_t, k * ROWS + 2)
                dve.wait_ge(ht_stored, k * 16)
                for t in range(ROWS):
                    ins = dve.scalar_tensor_tensor(xin[:, t, :], res[:, bass.ds(k * ROWS + t, 1), :].rearrange(
                        "p o d -> p (o d)"), ss[:, t:t + 1], rms[:, :], ALU.mult, ALU.mult)
                ins.then_inc(ht_done, 1)
                for t in range(ROWS):
                    sl = slice(t * P, (t + 1) * P)
                    dve.wait_ge(c_hi, k * ROWS + (t + 1))
                    dve.tensor_tensor(xT[par][1][:, :, sl], tp[t % 2][:, :].rearrange("p (c s) -> p c s", c=CD),
                                      xT[par][0][:, :, sl].bitcast(F32), ALU.subtract).then_inc(c_lo, 1)
                dve.wait_ge(c_lg, k + 1)
                dve.tensor_copy(lg[:, bass.ds(k * ROWS, ROWS), :],
                                dn[0][:, 0:ROWS * E].rearrange("p (t e) -> p t e", e=E)).then_inc(c_lgd, 1)
        dve.wait_ge(c_lgd, SHARED)
        for t in range(TT):
            ins = dve.max(top[:, t, :], lg[:, t, :])
        c = Chain(dve, rt)
        c(ins)
        for t in range(TT):
            dve.max_index(topi[:, t, :], top[:, t, :], lg[:, t, :])
        c(dve.tensor_tensor(fl[:, 0, :], top[:, :, 1], top[:, :, 0], ALU.subtract))
        iota = small[:, 0:E].unsqueeze(1).broadcast_to([P, TT, E])
        for k in range(2):
            ins = dve.tensor_copy(fj[:, k, :], topi[:, :, k])
        c(ins)
        for k in range(2):
            ins = dve.tensor_tensor(oh[:, k, :, :], fj[:, k, :].unsqueeze(2).broadcast_to([P, TT, E]), iota,
                                    ALU.is_equal)
        c(ins)
        dve.tensor_tensor(mm_[:, :, :], oh[:, 0, :, :], oh[:, 1, :, :], ALU.add).then_inc(rt_mm, 1)
        dve.wait_ge(rt_exp, 1)
        c(dve.tensor_scalar(share[:, 0, :], share[:, 1, :], 1.0, None, ALU.add))
        c(dve.reciprocal(share[:, 0, :], share[:, 0, :]))
        c(dve.tensor_tensor(share[:, 1, :], share[:, 1, :], share[:, 0, :], ALU.mult))
        dve.wait_ge(rt_pe, 1)
        c(dve.tensor_copy(tot[:, :, :], dn[1][:, 0:TT * E].rearrange("p (t e) -> p e t", e=E)))
        for e in range(E):
            ins = dve.tensor_tensor_scan(cum[:, e, :], tri[:, 1, 0:TT], tot[:, e, :], 0.0, ALU.mult, ALU.add)
        c(ins)
        c(dve.tensor_copy(blk[:, 0, :], cum[:, :, TT - 1]))
        c(dve.tensor_tensor(cum[:, :, :], cum[:, :, :], tot[:, :, :], ALU.subtract))
        c(dve.tensor_scalar(blk[:, 1, :], blk[:, 0, :], 1.0 / CHUNK, (CHUNK - 1.0) / (2 * CHUNK), ALU.mult, ALU.add))
        c(dve.tensor_scalar(blk[:, 1, :], blk[:, 1, :], ROUND, None, ALU.add))
        c(dve.tensor_scalar(blk[:, 1, :], blk[:, 1, :], ROUND, None, ALU.subtract))
        c(dve.tensor_tensor_scan(blk[:, 2, :], tri[:, 1, 0:E], blk[:, 1, :], 0.0, ALU.mult, ALU.add))
        c(dve.tensor_tensor(blk[:, 3, :], blk[:, 2, :], blk[:, 1, :], ALU.subtract))
        c(dve.tensor_scalar(blk[:, 3, :], blk[:, 3, :], float(CHUNK), None, ALU.mult))
        pos = lg
        c(dve.tensor_tensor(pos[:, :, :], dn[0][:, 0:TT * E].rearrange("p (t e) -> p t e", e=E),
                            cum[:, :, :].rearrange("p e t -> p t e"), ALU.add))
        c(dve.tensor_tensor(pos[:, :, :], pos[:, :, :], blk[:, 3, :].unsqueeze(1).broadcast_to([P, TT, E]), ALU.add))
        for k in range(2):
            ins = dve.tensor_tensor(oh[:, k, :, :], oh[:, k, :, :], pos[:, :, :], ALU.mult)
        c(ins)
        c(dve.tensor_reduce(fl[:, :, :], oh[:, :, :, :], AX_X, ALU.add))
        c(dve.tensor_scalar(fj[:, :, :], fl[:, :, :], 1.0 / P, -(P - 1.0) / (2 * P), ALU.mult, ALU.add))
        c(dve.tensor_scalar(fj[:, :, :], fj[:, :, :], ROUND, None, ALU.add))
        c(dve.tensor_scalar(fj[:, :, :], fj[:, :, :], ROUND, None, ALU.subtract))
        fk = tot[:, 0:2, :]
        c(dve.scalar_tensor_tensor(fk, fj[:, :, :], -float(P), fl[:, :, :], ALU.mult, ALU.add))
        c(dve.scalar_tensor_tensor(addr[:, :, :], fk, float(NL), fj[:, :, :], ALU.mult, ALU.add))
        fs = tot[:, 2:4, :]
        c(dve.tensor_scalar(fs, fj[:, :, :], 1.0 / ROWS, -(ROWS - 1.0) / (2 * ROWS), ALU.mult, ALU.add))
        c(dve.tensor_scalar(fs, fs, ROUND, None, ALU.add))
        c(dve.tensor_scalar(fs, fs, ROUND, None, ALU.subtract))
        c(dve.scalar_tensor_tensor(fj[:, :, :], fs, float(P * ROWS - ROWS), fj[:, :, :], ALU.mult, ALU.add))
        c(dve.scalar_tensor_tensor(place[:, :, :], fk, float(ROWS), fj[:, :, :], ALU.mult, ALU.add))
        sl = small[0:1, E:E + SLOTS].unsqueeze(2).broadcast_to([1, SLOTS, E])
        c(dve.tensor_tensor(own[:, :, :], blk[0:1, 2, :].unsqueeze(1).broadcast_to([1, SLOTS, E]), sl, ALU.is_le))
        c(dve.tensor_reduce(ownf[:, :], own[:, :, :], AX_X, ALU.add))
        dve.tensor_scalar(owner[:, :], ownf[:, :], E - 1.0, None, ALU.min).then_inc(rt_done, 1)

        def inputs(it):
            for t in range(ROWS):
                sl = slice(t * P, (t + 1) * P)
                dve.wait_ge(x_hi, it.n * 4 + (t + 1))
                x = xT[it.parity]
                dve.tensor_tensor(x[1][:, :, sl], tp[t % 2][:, :].rearrange("p (c s) -> p c s", c=CD),
                                  x[0][:, :, sl].bitcast(F32), ALU.subtract).then_inc(x_lo, 1)

        def gate_up(it, f):
            dve.wait_ge(silu_done, it.n * 2 + (f + 1))
            dve.wait_ge(gu_ready, it.n * 4 + (2 * f + 2))
            dve.tensor_tensor(sg[f][:, :], sg[f][:, :], gu[2 * f + 1][:, :], ALU.mult).then_inc(mul_done, 1)
            dve.wait_ge(a_hi, it.n * 2 + (f + 1))
            a = aT[it.parity]
            dve.tensor_tensor(a[1][:, f, :], sg[f][:, :], a[0][:, f, :].bitcast(F32), ALU.subtract).then_inc(a_lo, 1)

        def down(it):
            if it.slot:
                dve.wait_ge(y_stored, it.n * 16 - 16 * SHARED)
            for t in range(ROWS):
                dve.wait_ge(d_ready, it.n * 4 + (t + 1))
                if it.slot:
                    dve.tensor_copy(yb[:, t, :], dn[t % 2][:, :]).then_inc(d_used, 1)
                else:
                    r = res[:, bass.ds(it.n * ROWS + t, 1), :].rearrange("p o d -> p (o d)")
                    dve.tensor_tensor(r, r, dn[t % 2][:, :], ALU.add).then_inc(d_used, 1)

        def weights(it):
            for k, (a, b) in enumerate(W_PARTS):
                dve.wait_ge(w_hi, it.j * 3 + (k + 1))
                w = wb[it.wbuf]
                dve.tensor_tensor(w[1][:, a:b], wraw[:, a:b], w[0][:, a:b].bitcast(F32), ALU.subtract)\
                   .then_inc(w_lo, 1)

        item_segments(dve, {"inputs": inputs, "gu": gate_up, "down": down, "weights": weights})


def combine(nc, m, res, place, share, ys, out):
    NB = 4
    g = [[m.sb(f"f_g{k}{n}", [P, D]) for k in range(2)] for n in range(NB)]
    pl = [m.sb(f"f_pl{n}", [P, 2], mybir.dt.uint32) for n in range(NB)]
    st = m.sb("f_st", [P, NB, 6])
    mv = m.sb("f_mv", [P, NB, 2])
    nhalf = m.sb("f_nhalf", [P, 1])
    nmr = m.sb("f_nmr", [P, NB])
    o = [m.sb(f"f_o{n}", [P, D]) for n in range(NB)]
    copied = m.sem("f_copied")
    dve_passed = m.sem("f_dve_passed")
    pool_passed = m.sem("f_pool_passed")
    landed = [m.sem(f"f_landed{n}") for n in range(NB)]
    chain = m.sem("f_chain")
    var = m.sem("f_var")
    rstd = m.sem("f_rstd")
    shift = m.sem("f_shift")
    normed = m.sem("f_normed")
    stored = [m.sem(f"f_stored{n}") for n in range(NB)]
    rows = ys.rearrange("s p r d -> (s p r) d")
    out_v = out.rearrange("b (t p) d -> p (b t) d", p=P)
    block = m.ctx.enter_context(nc.Block())

    def tiles(eng, body):
        with eng.Fori(0, TT // NB - 1) as i:
            for b in range(NB):
                body(i * NB + b, b, i, True)
        for b in range(NB):
            body(TT - NB + b, b, TT // NB - 1, False)

    @block.gpsimd
    def _(pool):
        pool.memset(nhalf[:, :], -0.5).then_inc(copied, 1)
        pool.wait_ge(copied, 1)

        def gather(t, b):
            pool.tensor_copy(pl[b][:, :], place[:, :, bass.ds(t, 1)].rearrange("p k o -> p (k o)")).then_inc(copied, 1)
            pool.wait_ge(copied, t + 2)
            carry_wait(pool, pool_passed)
            for k in range(2):
                pool.indirect_dma_start(g[b][k][:, :], None, rows, bass.IndirectOffsetOnAxis(pl[b][:, k:k + 1], 0))\
                    .then_inc(landed[b], 16)

        def body(t, b, i, more):
            pool.wait_ge(var, t + 1)
            pool.tensor_tensor(mv[:, b, 1:2], mv[:, b, 1:2], nhalf[:, :], ALU.pow).then_inc(rstd, 1)
            pool.wait_ge(rstd, t + 1)
            carry_wait(pool, pool_passed)
            pool.tensor_scalar(nmr[:, b:b + 1], mv[:, b, 0:1], -1.0, mv[:, b, 1:2], ALU.mult, ALU.mult)\
                .then_inc(shift, 1)
            if more:
                gather(t + NB, b)

        for b in range(NB):
            gather(b, b)
        tiles(pool, body)

    @block.vector
    def _(dve):
        def body(t, b, i, more):
            c = Chain(dve, chain, t * 4)
            dve.wait_ge(landed[b], i * 32 + 32)
            c(dve.scalar_tensor_tensor(g[b][0][:, :], g[b][0][:, :], share[:, 0, bass.ds(t, 1)],
                                       res[:, bass.ds(t, 1), :].rearrange("p o d -> p (o d)"), ALU.mult, ALU.add))
            dve.wait_ge(stored[b], i * 16)
            c(dve.scalar_tensor_tensor(o[b][:, :], g[b][1][:, :], share[:, 1, bass.ds(t, 1)], g[b][0][:, :],
                                       ALU.mult, ALU.add))
            c(dve.bn_stats(st[:, b, :], o[b][:, :]))
            carry_wait(dve, dve_passed)
            c(dve.bn_aggr(mv[:, b, :], st[:, b, :]))
            dve.tensor_scalar(mv[:, b, 1:2], mv[:, b, 1:2], LN_EPS, None, ALU.add).then_inc(var, 1)

        tiles(dve, body)

    @block.scalar
    def _(act):
        def body(t, b, i, more):
            act.wait_ge(shift, t + 1)
            act.activation(o[b][:, :], o[b][:, :], ACT.Identity, bias=nmr[:, b:b + 1], scale=mv[:, b, 1:2])\
               .then_inc(normed, 1)

        tiles(act, body)

    @block.sync
    def _(sp):
        def body(t, b, i, more):
            sp.wait_ge(normed, t + 1)
            sp.dma_start(out_v[:, bass.ds(t, 1), :].rearrange("p o d -> p (o d)"), o[b][:, :]).then_inc(stored[b], 16)

        tiles(sp, body)
        for b in range(NB):
            sp.wait_ge(stored[b], 16 * (TT // NB))


def host_tok(x, log_dt, log_w_real, w_imag):
    import numpy as np
    dyn = np.stack([np.broadcast_to(log_dt[None, :], (NST, S)), log_w_real.T, w_imag.T], 1)
    dyn = np.ascontiguousarray(np.concatenate([dyn, dyn], 0))
    c = x.transpose(2, 1, 3, 0)
    c = np.ascontiguousarray(np.concatenate([c, c], 0))
    return dyn, c


def host_experts(w_gate, w_up, w_down, sw_gate, sw_up, sw_down):
    import numpy as np
    one = lambda a, b, c: np.concatenate([rows_on_partitions(a), rows_on_partitions(b), rows_on_partitions(c)], 1)
    parts = [one(w_gate[e], w_up[e], w_down[e]) for e in range(E)] + [one(sw_gate, sw_up, sw_down)]
    return np.ascontiguousarray(np.stack(parts))


def constants():
    import numpy as np
    mult = np.broadcast_to(np.arange(NM1, dtype=np.float32) * np.array([[1], [NM1], [NM]], np.float32), (P, 3, NM1))
    half = np.zeros((P, 8), np.float32)
    half[:64, 0], half[64:, 0] = -1, 1
    half[:64, 1], half[64:, 1] = 1, -1
    half[:64, 2] = PI / 2
    half[64:, 3] = PI / 2
    half[:, 6] = PI / 2
    inv_freq = 1.0 / 10000.0 ** (np.arange(0, HD, 2, dtype=np.float32) / np.float32(HD))
    ang = np.outer(np.arange(S, dtype=np.float32), inv_freq.astype(np.float32)).astype(np.float32)
    c, sn = np.cos(ang).T.astype(np.float32), np.sin(ang).T.astype(np.float32)
    rope0 = np.stack([np.concatenate([c, c], 0), np.concatenate([-sn, sn], 0)], 1)
    mask = np.zeros((P, 2 * P), np.float32)
    mask[:, P:] = np.triu(np.full((P, P), NEG, np.float32), 1)
    inv1 = (1.0 / 1000000.0 ** (np.arange(HD1 // 2, dtype=np.float32) / np.float32(HD1 // 2))).astype(np.float32)
    ang = np.outer(np.arange(S, dtype=np.float32), inv1).astype(np.float32)
    c, sn = np.cos(ang).astype(np.float32), np.sin(ang).astype(np.float32)
    rope1 = np.stack([np.concatenate([c, c], 1), np.concatenate([-sn, sn], 1)], 0)
    rope1 = np.ascontiguousarray(rope1.reshape(2, ST, P, HD1).transpose(2, 0, 1, 3))
    tri = np.stack([np.triu(np.ones((P, P), np.float32), 1), np.ones((P, P), np.float32)], 1)
    small = np.concatenate([np.arange(E), np.arange(SLOTS), [-0.5]]).astype(np.float32)
    tok = (np.arange(TT)[None, :] * P + np.arange(P)[:, None]).astype(np.uint32)
    return {"tri": np.ascontiguousarray(tri), "small": np.tile(small, (P, 1)), "tok": tok, "rope1": rope1, "identb": np.eye(P).astype(mybir.dt.np(BF16)), "mult": np.ascontiguousarray(mult), "half": half, "rope0": np.ascontiguousarray(rope0), "mask": mask,
            "ident": np.eye(P, dtype=np.float32)}


def rows_on_partitions(w):
    import numpy as np
    n = w.shape[1]
    return np.ascontiguousarray(w.reshape(-1, P, n).transpose(1, 0, 2).reshape(P, -1))


IN_NAMES = ["dyn", "coef", "mult", "half", "wq0", "wk0", "wv0", "wo0", "rope0", "mask", "ident", "fw", "fb", "wq1",
            "wkv1", "wo1", "bias1", "rope1", "identb", "wexp", "rms", "router", "tri", "small", "tok"]


def program(nc, a, out):
    def scratch(name, shape, dt=F32):
        return nc.dram_tensor(name, shape, dt, kind="Internal").ap()

    h0 = scratch("h0", (P, S, NM))
    h1 = scratch("h1", (B, S, D))
    h3 = scratch("h3", (B, S, D))
    ht = scratch("ht", (T, D))
    token_list = scratch("token_list", (P * NL, 1), mybir.dt.uint32)
    ys = scratch("ys", (SLOTS, P, ROWS, D))
    token_mixer(nc, a["dyn"], a["coef"], a["mult"], a["half"], h0)
    attention0(nc, a["wq0"], a["wk0"], a["wv0"], a["wo0"], a["rope0"], a["mask"], a["ident"], h0, h1)
    block01(nc, a["fw"], a["fb"], a["wq1"], a["wkv1"], a["wo1"], a["bias1"], a["rope1"], a["mask"], a["ident"],
            a["identb"], h1, h3)
    experts(nc, a["wexp"], a["rms"], a["router"], a["tri"], a["small"], a["tok"], a["ident"], h3, ht, token_list, ys,
            out)


def kernel(x, L0_tok_log_dt, L0_tok_log_w_real, L0_tok_w_imag, L0_attn_w_q, L0_attn_w_k, L0_attn_w_v, L0_attn_w_o,
           L0_ffn_weight, L0_ffn_bias, L1_attn_Wq, L1_attn_bq, L1_attn_Wk, L1_attn_bk, L1_attn_Wv, L1_attn_bv,
           L1_attn_Wo, L1_ffn_rms_weight, L1_ffn_router_w, L1_ffn_w_gate, L1_ffn_w_up, L1_ffn_w_down,
           L1_ffn_sw_gate, L1_ffn_sw_up, L1_ffn_sw_down):
    import numpy as np
    import concourse.bacc as bacc
    from concourse.bass_utils import run_bass_kernel_spmd

    arrays = constants()
    arrays["dyn"], arrays["coef"] = host_tok(np.asarray(x), np.asarray(L0_tok_log_dt), np.asarray(L0_tok_log_w_real),
                                             np.asarray(L0_tok_w_imag))
    rows = lambda w: rows_on_partitions(np.asarray(w))
    for name, w in (("wq0", L0_attn_w_q), ("wk0", L0_attn_w_k), ("wv0", L0_attn_w_v), ("wo0", L0_attn_w_o)):
        arrays[name] = rows(w)
    arrays["fw"] = rows(np.asarray(L0_ffn_weight).T)
    arrays["fb"] = np.tile(np.asarray(L0_ffn_bias), (P, 1))
    arrays["wq1"] = rows(L1_attn_Wq).reshape(P, CD, D)
    arrays["wkv1"] = rows(np.concatenate([np.asarray(L1_attn_Wk), np.asarray(L1_attn_Wv)], 1)).reshape(P, CD, 2 * P)
    arrays["wo1"] = rows(L1_attn_Wo).reshape(P, CD, D)
    arrays["bias1"] = np.concatenate([np.asarray(L1_attn_bq), np.asarray(L1_attn_bk), np.asarray(L1_attn_bv)])[None]
    arrays["wexp"] = host_experts(*[np.asarray(w) for w in (L1_ffn_w_gate, L1_ffn_w_up, L1_ffn_w_down, L1_ffn_sw_gate,
                                                            L1_ffn_sw_up, L1_ffn_sw_down)])
    arrays["rms"] = np.tile(np.asarray(L1_ffn_rms_weight), (P, 1))
    arrays["router"] = rows(L1_ffn_router_w).reshape(P, CD, E)

    nc = bacc.Bacc("TRN2", target_bir_lowering=False, num_devices=1)
    in_map, aps = {}, {}
    for name in IN_NAMES:
        a = np.ascontiguousarray(arrays[name])
        in_map[f"in_{name}"] = a
        aps[name] = nc.dram_tensor(f"in_{name}", a.shape, mybir.dt.from_np(a.dtype), kind="ExternalInput").ap()
    out = nc.dram_tensor("out", (B, S, D), F32, kind="ExternalOutput").ap()
    program(nc, aps, out)
    return run_bass_kernel_spmd(nc, [in_map], core_ids=[0]).results[0]["out"]
```

```python
from contextlib import ExitStack

import concourse.bass as bass
from concourse import mybir

ALU = mybir.AluOpType
ACT = mybir.ActivationFunctionType
AX_X = mybir.AxisListType.X
F32 = mybir.dt.float32
F32R = mybir.dt.float32r
BF16 = mybir.dt.bfloat16
I32 = mybir.dt.int32

P = 128
B, S, D = 16, 256, 512
NST = 64
CD = D // P
ST = S // P
ROUND = 12582912.0
PI = 3.141592653589793
LN_EPS = 1e-5


class Memory:

    def __init__(self, nc, ctx):
        self.nc, self.ctx = nc, ctx

    def sb(self, name, shape, dt=F32):
        return self.ctx.enter_context(self.nc.sbuf_tensor(name, shape, dt))

    def ps(self, name, shape, dt=F32):
        return self.ctx.enter_context(self.nc.psum_tensor(name, shape, dt))

    def sem(self, name):
        return self.ctx.enter_context(self.nc.semaphore(name))


class Chain:

    def __init__(self, eng, sem, base=0):
        self.eng, self.sem, self.base, self.n = eng, sem, base, 0

    def __call__(self, ins):
        self.n += 1
        ins.then_inc(self.sem, 1)
        self.eng.wait_ge(self.sem, self.base + self.n)


def carry_wait(eng, passed):
    eng.sem_inc(passed, 1)


HC = 8
HS = 2 * HC
STEPS = S // HS
NA, NM = 8, 64
NM1 = 8
TWO_PI_1 = 6.28125
TWO_PI_2 = 0.0019350051879882812
TWO_PI_3 = 3.0199161274e-07
LN2_1 = 0.693359375
LN2_2 = -2.12194440e-4


def token_mixer(nc, dyn_in, c_in, mult_in, half_in, h0):
    with ExitStack() as ctx:
        m = Memory(nc, ctx)
        dyn = m.sb("dyn", [P, 3, S])
        mult = m.sb("mult", [P, 3, NM1])
        half = m.sb("half", [P, 8])
        ex = m.sb("ex", [P, 2, S])
        ek = m.sb("ek", [P, 2, S])
        ep = m.sb("ep", [P, 2, S])
        ei = m.sb("ei", [P, 2, S], I32)
        wr = m.sb("wr", [P, S])
        al = m.sb("al", [P, S])
        th = m.sb("th", [P, S])
        g = [m.sb(f"g{n}", [P, S]) for n in range(7)]
        qq = m.sb("qq", [P, 3, S])
        craw = m.sb("craw", [P, 2, HS, 2, B])
        cm = m.sb("cm", [P, 2, HS, B])
        cm2 = m.sb("cm2", [P, 2, HS, B])
        ang = m.sb("ang", [P, 3, HS, NM1])
        turn = m.sb("turn", [P, 3, HS, NM1])
        ra = m.sb("ra", [P, 3, HS, NM1])
        rb = m.sb("rb", [P, 3, HS, NM1])
        mag = m.sb("mag", [P, 3, HS, NM1])
        tr = m.sb("tr", [P, 2, 3, HS, NM1])
        vv = [m.sb(f"vv{n}", [P, HC, NM]) for n in range(2)]
        v2 = m.sb("v2", [P, HC, NM])
        s1 = [m.sb(f"s1{n}", [P, HC, NA, B]) for n in range(2)]
        s2 = [m.sb(f"s2{n}", [P, HC, NA, B]) for n in range(2)]
        kout = m.sb("kout", [P, HS, NM])
        kps = [m.ps(f"kps{n}", [P, HC, NM]) for n in range(2)]

        ld = m.sem("ld")
        c_landed = [m.sem(f"c_landed{n}") for n in range(2)]
        c_free = m.sem("c_free")
        dve_chain = m.sem("dve_chain")
        exps = m.sem("exps")
        alpha_ready = m.sem("alpha_ready")
        pre_act = m.sem("pre_act")
        q_ready = m.sem("q_ready")
        cm_chain = m.sem("cm_chain")
        cm_ready = m.sem("cm_ready")
        angles_ready = m.sem("angles_ready")
        trig_ready = m.sem("trig_ready")
        tables_ready = m.sem("tables_ready")
        tables_free = m.sem("tables_free")
        vs_ready = m.sem("vs_ready")
        s2_ready = m.sem("s2_ready")
        k_ready = m.sem("k_ready")
        kout_ready = m.sem("kout_ready")
        k_stored = m.sem("k_stored")

        block = ctx.enter_context(nc.Block())

        @block.sync
        def _(sp):
            sp.sem_inc(k_stored, 1)
            sp.dma_start(dyn[:, :, :], dyn_in).then_inc(ld, 16)
            sp.dma_start(mult[:, :, :], mult_in).then_inc(ld, 16)
            sp.dma_start(half[:, :], half_in).then_inc(ld, 16)
            with sp.Fori(0, STEPS) as i:
                sp.wait_ge(c_free, i + 1)
                sp.dma_start(craw[:, 0], c_in[:, bass.ds(i * HS, HS), :, :]).then_inc(c_landed[0], 16)
                sp.wait_ge(kout_ready, 2 * i + 3)
                sp.dma_start(h0[:, bass.ds(i * HS, HS), :], kout[:, :, :]).then_inc(k_stored, 16)
            sp.wait_ge(k_stored, 16 * STEPS + 1)

        @block.gpsimd
        def _(pool):
            pool.sem_inc(c_free, 1)
            pool.sem_inc(s2_ready, 1)
            pool.wait_ge(q_ready, 1)
            with pool.Fori(0, STEPS) as i:
                chain = Chain(pool, cm_chain, i * 2)
                hs = bass.ds(i * HS, HS)
                pool.wait_ge(c_landed[0], 16 * i + 16)
                pool.wait_ge(s2_ready, 2 * i + 1)
                pool.wait_ge(vs_ready, 2 * i + 1)
                cr = craw[:, 0, :, 0, :].unsqueeze(1).broadcast_to([P, 2, HS, B])
                ci = craw[:, 0, :, 1, :].unsqueeze(1).broadcast_to([P, 2, HS, B])
                pool.tensor_tensor(cm2[:, :, :, :], ci, qq[:, 1:3, hs].unsqueeze(3).broadcast_to([P, 2, HS, B]),
                                   ALU.mult)
                chain(pool.tensor_tensor(cm[:, :, :, :], cr,
                                         qq[:, 0:2, hs].unsqueeze(3).broadcast_to([P, 2, HS, B]), ALU.mult))
                chain(pool.tensor_tensor(cm[:, :, :, :], cm[:, :, :, :], cm2[:, :, :, :], ALU.add))
                pool.sem_inc(cm_ready, 1)
                pool.sem_inc(c_free, 1)
                for j in range(2):
                    if j == 0:
                        pool.wait_ge(tables_ready, i + 1)
                    pool.wait_ge(k_ready, 2 * i + 1 + j)
                    js = slice(j * HC, (j + 1) * HC)
                    pool.tensor_tensor(s2[j][:, :, :, :],
                                       cm[:, 1, js, :].unsqueeze(2).broadcast_to([P, HC, NA, B]),
                                       tr[:, 1, 2, js, :].unsqueeze(3).broadcast_to([P, HC, NA, B]),
                                       ALU.mult).then_inc(s2_ready, 1)

        @block.vector
        def _(dve):
            dve.sem_inc(vs_ready, 1)
            c = Chain(dve, dve_chain)
            dve.wait_ge(ld, 48)
            c(dve.tensor_scalar(ex[:, :, :], dyn[:, 0:2, :], -87.0, 88.0, ALU.max, ALU.min))
            c(dve.tensor_scalar(ek[:, :, :], ex[:, :, :], 1.4426950408889634, ROUND, ALU.mult, ALU.add))
            c(dve.tensor_scalar(ek[:, :, :], ek[:, :, :], ROUND, None, ALU.subtract))
            c(dve.scalar_tensor_tensor(ex[:, :, :], ek[:, :, :], -LN2_1, ex[:, :, :], ALU.mult, ALU.add))
            c(dve.scalar_tensor_tensor(ex[:, :, :], ek[:, :, :], -LN2_2, ex[:, :, :], ALU.mult, ALU.add))
            c(dve.tensor_scalar(ep[:, :, :], ex[:, :, :], 1.0 / 5040, None, ALU.mult))
            for f in (720.0, 120.0, 24.0, 6.0, 2.0, 1.0):
                c(dve.scalar_tensor_tensor(ep[:, :, :], ep[:, :, :], 1.0 / f, ex[:, :, :], ALU.add, ALU.mult))
            c(dve.tensor_scalar(ei[:, :, :], ek[:, :, :], 127.0, None, ALU.add))
            c(dve.tensor_scalar(ei[:, :, :], ei[:, :, :], 23, None, ALU.logical_shift_left))
            c(dve.scalar_tensor_tensor(ep[:, :, :], ep[:, :, :], 1.0, ei[:, :, :].bitcast(F32), ALU.add, ALU.mult))
            dt, wabs, wi = ep[:, 0, :], ep[:, 1, :], dyn[:, 2, :]
            c(dve.tensor_scalar(wr[:, :], wabs, -1.0, None, ALU.mult))
            c(dve.tensor_tensor(al[:, :], wr[:, :], dt, ALU.mult))
            c(dve.tensor_tensor(th[:, :], wi, dt, ALU.mult))
            k, r, a = g[0], g[1], g[2]
            c(dve.tensor_scalar(k[:, :], th[:, :], 1.0 / (2 * PI), ROUND, ALU.mult, ALU.add))
            c(dve.tensor_scalar(k[:, :], k[:, :], ROUND, None, ALU.subtract))
            c(dve.scalar_tensor_tensor(r[:, :], k[:, :], -TWO_PI_1, th[:, :], ALU.mult, ALU.add))
            c(dve.scalar_tensor_tensor(r[:, :], k[:, :], -TWO_PI_2, r[:, :], ALU.mult, ALU.add))
            c(dve.scalar_tensor_tensor(r[:, :], k[:, :], -TWO_PI_3, r[:, :], ALU.mult, ALU.add))
            c(dve.tensor_scalar(r[:, :], r[:, :], PI, -PI, ALU.min, ALU.max))
            dve.scalar_tensor_tensor(a[:, :], r[:, :], -1.0, r[:, :], ALU.mult, ALU.max).then_inc(alpha_ready, 1)
            sn, cs, t = g[3], g[4], g[5]
            em1, nr, ni, den = g[0], g[1], g[2], g[6]
            dve.wait_ge(pre_act, 3)
            c(dve.tensor_scalar(den[:, :], t[:, :], -1.0, 1.0, ALU.mult, ALU.add))
            c(dve.reciprocal(den[:, :], den[:, :]))
            c(dve.scalar_tensor_tensor(em1[:, :], t[:, :], 2.0, den[:, :], ALU.mult, ALU.mult))
            c(dve.tensor_tensor(cs[:, :], cs[:, :], sn[:, :], ALU.mult))
            c(dve.scalar_tensor_tensor(sn[:, :], sn[:, :], -2.0, sn[:, :], ALU.mult, ALU.mult))
            c(dve.tensor_scalar(t[:, :], em1[:, :], 1.0, None, ALU.add))
            c(dve.tensor_tensor(nr[:, :], sn[:, :], t[:, :], ALU.mult))
            c(dve.tensor_tensor(nr[:, :], nr[:, :], em1[:, :], ALU.add))
            c(dve.scalar_tensor_tensor(ni[:, :], cs[:, :], 2.0, t[:, :], ALU.mult, ALU.mult))
            c(dve.tensor_tensor(sn[:, :], wr[:, :], wr[:, :], ALU.mult))
            c(dve.tensor_tensor(cs[:, :], wi, wi, ALU.mult))
            c(dve.tensor_tensor(den[:, :], sn[:, :], cs[:, :], ALU.add))
            c(dve.reciprocal(den[:, :], den[:, :]))
            c(dve.tensor_tensor(sn[:, :], nr[:, :], wr[:, :], ALU.mult))
            c(dve.tensor_tensor(cs[:, :], ni[:, :], wi, ALU.mult))
            c(dve.tensor_tensor(sn[:, :], sn[:, :], cs[:, :], ALU.add))
            c(dve.tensor_tensor(qq[:, 0, :], sn[:, :], den[:, :], ALU.mult))
            c(dve.tensor_tensor(sn[:, :], nr[:, :], wi, ALU.mult))
            c(dve.tensor_tensor(cs[:, :], ni[:, :], wr[:, :], ALU.mult))
            c(dve.tensor_tensor(sn[:, :], sn[:, :], cs[:, :], ALU.subtract))
            c(dve.tensor_tensor(qq[:, 1, :], sn[:, :], den[:, :], ALU.mult))
            dve.tensor_scalar(qq[:, 2, :], qq[:, 0, :], -1.0, None, ALU.mult).then_inc(q_ready, 1)

            used = c.n
            with dve.Fori(0, STEPS) as i:
                per = 13
                c = Chain(dve, dve_chain, i * per + used)
                hs = bass.ds(i * HS, HS)
                full = [P, 3, HS, NM1]
                mt = mult[:, :, :].unsqueeze(2).broadcast_to(full)
                dve.wait_ge(trig_ready, i + 1)
                dve.tensor_tensor(mag[:, :, :, :], al[:, hs].unsqueeze(1).unsqueeze(3).broadcast_to(full), mt, ALU.mult)
                c(dve.tensor_tensor(ang[:, :, :, :], th[:, hs].unsqueeze(1).unsqueeze(3).broadcast_to(full), mt,
                                    ALU.mult))
                c(dve.tensor_scalar(turn[:, :, :, :], ang[:, :, :, :], 1.0 / (2 * PI), ROUND, ALU.mult, ALU.add))
                c(dve.tensor_scalar(turn[:, :, :, :], turn[:, :, :, :], ROUND, None, ALU.subtract))
                for part in (TWO_PI_1, TWO_PI_2, TWO_PI_3):
                    c(dve.scalar_tensor_tensor(ang[:, :, :, :], turn[:, :, :, :], -part, ang[:, :, :, :], ALU.mult,
                                               ALU.add))
                c(dve.tensor_scalar(ang[:, :, :, :], ang[:, :, :, :], PI, -PI, ALU.min, ALU.max))
                c(dve.scalar_tensor_tensor(ra[:, :, :, :], ang[:, :, :, :], half[:, 0:1], ang[:, :, :, :], ALU.mult,
                                           ALU.max))
                dve.scalar_tensor_tensor(rb[:, :, :, :], ang[:, :, :, :], half[:, 1:2], ang[:, :, :, :], ALU.mult,
                                         ALU.max).then_inc(angles_ready, 1)
                dve.wait_ge(trig_ready, i + 2)
                c(dve.tensor_tensor(tr[:, :, :, :, :].rearrange("p t g h m -> p t (g h m)"),
                                    tr[:, :, :, :, :].rearrange("p t g h m -> p t (g h m)"),
                                    mag[:, :, :, :].rearrange("p g h m -> p (g h m)").unsqueeze(1).broadcast_to(
                                        [P, 2, 3 * HS * NM1]), ALU.mult))
                dve.sem_inc(tables_ready, 1)
                dve.wait_ge(cm_ready, i + 1)
                for j in range(2):
                    js = slice(j * HC, (j + 1) * HC)
                    out4 = [P, HC, NM1, NM1]
                    dve.wait_ge(k_ready, 2 * i + 1 + j)
                    dve.tensor_tensor(v2[:, :, :].rearrange("p h (a b) -> p h a b", b=NM1),
                                      tr[:, 1, 1, js, :].unsqueeze(3).broadcast_to(out4),
                                      tr[:, 1, 0, js, :].unsqueeze(2).broadcast_to(out4), ALU.mult)
                    c(dve.tensor_tensor(vv[j][:, :, :].rearrange("p h (a b) -> p h a b", b=NM1),
                                        tr[:, 0, 1, js, :].unsqueeze(3).broadcast_to(out4),
                                        tr[:, 0, 0, js, :].unsqueeze(2).broadcast_to(out4), ALU.mult))
                    c(dve.tensor_tensor(vv[j][:, :, :], vv[j][:, :, :], v2[:, :, :], ALU.add))
                    dve.tensor_tensor(s1[j][:, :, :, :],
                                      cm[:, 0, js, :].unsqueeze(2).broadcast_to([P, HC, NA, B]),
                                      tr[:, 0, 2, js, :].unsqueeze(3).broadcast_to([P, HC, NA, B]),
                                      ALU.mult).then_inc(vs_ready, 1)
                assert c.n == per, c.n

        @block.scalar
        def _(act):
            act.sem_inc(trig_ready, 1)
            act.sem_inc(kout_ready, 1)
            act.wait_ge(alpha_ready, 1)
            act.activation(g[3][:, :], g[1][:, :], ACT.Sin, scale=0.5).then_inc(pre_act, 1)
            act.activation(g[4][:, :], g[2][:, :], ACT.Sin, bias=half[:, 6:7], scale=-0.5).then_inc(pre_act, 1)
            act.activation(g[5][:, :], al[:, :], ACT.Tanh, scale=0.5).then_inc(pre_act, 1)
            with act.Fori(0, STEPS) as i:
                act.wait_ge(angles_ready, i + 1)
                act.wait_ge(vs_ready, 2 * i + 1)
                act.wait_ge(s2_ready, 2 * i + 1)
                sin = ACT.Sin
                act.activation(tr[0:64, 0, 0], ra[0:64, 0], sin, bias=half[0:64, 6:7], scale=-1.0)
                act.activation(tr[64:128, 0, 0], rb[64:128, 0], sin, bias=half[64:128, 6:7], scale=-1.0)
                act.activation(tr[0:64, 1, 0], rb[0:64, 0], sin)
                act.activation(tr[64:128, 1, 0], ra[64:128, 0], sin)
                act.activation(tr[:, 0, 1], ra[:, 1], sin, bias=half[:, 2:3], scale=half[:, 0:1])
                act.activation(tr[:, 1, 1], rb[:, 1], sin, bias=half[:, 3:4], scale=-1.0)
                act.activation(tr[:, 0, 2], ra[:, 2], sin, bias=half[:, 2:3], scale=-1.0)
                act.activation(tr[:, 1, 2], rb[:, 2], sin, bias=half[:, 3:4], scale=half[:, 1:2])
                act.activation(mag[:, :, :, :], mag[:, :, :, :], ACT.Exp).then_inc(trig_ready, 1)
                for j in range(2):
                    act.wait_ge(k_ready, 2 * i + j + 3)
                    if j == 0:
                        act.wait_ge(k_stored, 16 * i + 1)
                    act.activation(kout[:, j * HC:(j + 1) * HC, :], kps[j][:, :, :], ACT.Copy,
                                   scale=2.0).then_inc(kout_ready, 1)

        @block.tensor
        def _(pe):
            pe.sem_inc(k_ready, 2)
            with pe.Fori(0, STEPS) as i:
                for j in range(2):
                    pe.wait_ge(vs_ready, 2 * i + j + 2)
                    pe.wait_ge(s2_ready, 2 * i + j + 2)
                    pe.wait_ge(kout_ready, 2 * i + 1)
                    for h in range(HC):
                        pe.matmul(kps[j][:, h, :], s1[j][:, h], vv[j][:, h, :], start=True, stop=False)
                        mm = pe.matmul(kps[j][:, h, :], s2[j][:, h], vv[j][:, h, :], start=False, stop=True)
                    mm.then_inc(k_ready, 1)




def mm3(pe, out, lhs, rhs, start, stop):
    pe.matmul(out, lhs[0], rhs[0], start=start, stop=False)
    pe.matmul(out, lhs[0], rhs[1], start=False, stop=False)
    return pe.matmul(out, lhs[1], rhs[0], start=False, stop=stop)


def split_weights(nc, parts):
    with ExitStack() as ctx:
        m = Memory(nc, ctx)
        width = 2048
        tiles = []
        for dram, hi, lo in parts:
            n = dram.shape[1]
            for a in range(0, n, width):
                b = min(a + width, n)
                tiles.append((dram[:, a:b], hi[:, a:b], lo[:, a:b], b - a))
        bufs = 4
        raw = [m.sb(f"wraw{n}", [P, width]) for n in range(bufs)]
        landed = [m.sem(f"w_landed{n}") for n in range(bufs)]
        hi_done = m.sem("w_hi_done")
        lo_done = m.sem("w_lo_done")
        block = ctx.enter_context(nc.Block())

        @block.sync
        def _(sp):
            for t, (dram, _, _, w) in enumerate(tiles):
                if t >= bufs:
                    sp.wait_ge(lo_done, t - bufs + 1)
                sp.dma_start(raw[t % bufs][:, 0:w], dram).then_inc(landed[t % bufs], 16)

        @block.scalar
        def _(act):
            for t, (_, hi, _, w) in enumerate(tiles):
                act.wait_ge(landed[t % bufs], 16 * (t // bufs + 1))
                act.activation(hi, raw[t % bufs][:, 0:w], ACT.Copy).then_inc(hi_done, 1)

        @block.vector
        def _(dve):
            for t, (_, hi, lo, w) in enumerate(tiles):
                dve.wait_ge(hi_done, t + 1)
                dve.tensor_tensor(lo, raw[t % bufs][:, 0:w], hi.bitcast(F32), ALU.subtract).then_inc(lo_done, 1)


NH, NKV, HD = 16, 4, 128
REP = NH // NKV
NEG = -1e37
BIG = 3e38


def attention0(nc, wq_in, wk_in, wv_in, wo_in, rope_in, mask_in, ident_in, h0, h1):
    with ExitStack() as wctx:
        w = Memory(nc, wctx)
        wq = [w.sb(f"wq{p}", [P, CD, NH * HD], F32R) for p in ("h", "l")]
        wk = [w.sb(f"wk{p}", [P, CD, NKV * HD], F32R) for p in ("h", "l")]
        wv = [w.sb(f"wv{p}", [P, CD, NKV * HD], F32R) for p in ("h", "l")]
        wo = [w.sb(f"wo{p}", [P, NH, D], F32R) for p in ("h", "l")]
        flat = lambda t: t[:, :, :].rearrange("p a n -> p (a n)")
        split_weights(nc, [(wk_in, flat(wk[0]), flat(wk[1])), (wv_in, flat(wv[0]), flat(wv[1])),
                           (wq_in, flat(wq[0]), flat(wq[1])), (wo_in, flat(wo[0]), flat(wo[1]))])
        with ExitStack() as ctx:
            attention0_loop(nc, Memory(nc, ctx), wq, wk, wv, wo, rope_in, mask_in, ident_in, h0, h1)


class Image:

    def __init__(self, i):
        self.i, self.n, self.u, self.r = i, i * NH, i * UNITS, i * ROPES


UNITS, ROPES = 2 + NKV + ST + NH, NKV + NH
K_UNIT = [ST + g for g in range(NKV)]
V_UNIT = [ST + NKV + 1 + t for t in range(ST)]
Q_UNIT = [ST + NKV] + [2 * ST + NKV + h for h in range(1, NH)]


def all_images(eng, start, step, finish=None):

    def image(i, first=False, last=False):
        for s in range(NH + 2):
            step(Image(i), s, None if last else Image(i + 1), None if first else Image(i - 1))

    start(Image(0))
    image(0, first=True)
    with eng.Fori(0, B - 2) as i:
        image(i + 1)
    image(B - 1, last=True)
    if finish:
        finish(Image(B - 1))


def attention0_loop(nc, m, wq, wk, wv, wo, rope_in, mask_in, ident_in, h0, h1):
    SCALE = float(HD) ** -0.5
    ident = m.sb("ident", [P, P])
    cos = m.sb("cos", [P, S])
    sin = m.sb("sin", [P, S])
    mask = m.sb("mask", [P, 2 * P])
    xs = m.sb("xs", [P, D])
    res = m.sb("res", [P, ST, D])
    xT = [m.sb(f"xT{p}", [P, CD, S], F32R) for p in "hl"]
    kT = [m.sb(f"kT{p}", [P, NKV, S], F32R) for p in "hl"]
    v = [m.sb(f"v{p}", [P, ST, NKV * HD], F32R) for p in "hl"]
    turn = [[m.sb(f"turn{n}", [P, S])[:, :] for n in range(2)], [xs[:, 0:S], xs[:, S:2 * S]]]
    q = [[m.sb(f"q{p}{n}", [P, S], F32R) for p in "hl"] for n in range(2)]
    prob = [m.sb(f"prob{n}", [P, 3 * P]) for n in range(2)]
    pT = [m.sb(f"pT{p}", [P, 3 * P], F32R) for p in "hl"]
    oT = [m.sb(f"oT{p}", [P, S], F32R) for p in "hl"]
    mx = m.sb("mx", [P, 2, ST])
    sums = m.sb("sums", [P, 2, ST])
    inv = m.sb("inv", [P, 2, ST])
    st = m.sb("st", [P, ST, 6])
    mv = m.sb("mv", [P, ST, 2])
    nhalf = m.sb("nhalf", [P, ST])
    proj = [m.ps(f"proj{n}", [P, 512]) for n in range(3)]
    sc = m.ps("sc", [P, 512])
    pTp = m.ps("pTp", [P, 512])
    oTp = m.ps("oTp", [P, 512])
    acc = [m.ps(f"acc{t}", [P, D]) for t in range(ST)]

    consts = m.sem("consts")
    dve_passed = m.sem("a_dve_passed")
    x_landed = m.sem("x_landed")
    res_landed = m.sem("res_landed")
    proj_ready = m.sem("proj_ready")
    proj_used = m.sem("proj_used")
    split_hi = m.sem("split_hi")
    rope_sum = m.sem("rope_sum")
    rope_hi = m.sem("rope_hi")
    rope_lo = m.sem("rope_lo")
    sc_ready = m.sem("sc_ready")
    mx_ready = m.sem("mx_ready")
    ex_ready = m.sem("ex_ready")
    inv_ready = m.sem("inv_ready")
    p_ready = m.sem("p_ready")
    pt_ready = m.sem("pt_ready")
    pt_hi = m.sem("pt_hi")
    pt_lo = m.sem("pt_lo")
    pv_ready = m.sem("pv_ready")
    ot_hi = m.sem("ot_hi")
    ot_lo = m.sem("ot_lo")
    o_done = m.sem("o_done")
    ln_chain = m.sem("ln_chain")
    ln_var = m.sem("ln_var")
    ln_rstd = m.sem("ln_rstd")
    ln_done = m.sem("ln_done")
    stored = m.sem("stored")

    head = lambda h: 0 <= h < NH
    LN_STEPS = 3
    PAIRED = NKV + 2
    products = lambda r: turn[r % 2 if r < PAIRED else 0]
    block = m.ctx.enter_context(nc.Block())

    @block.sync
    def _(sp):
        sp.sem_inc(stored, 1)
        sp.dma_start(ident[:, :], ident_in).then_inc(consts, 16)
        sp.dma_start(cos[:, :], rope_in[:, 0, :]).then_inc(consts, 16)
        sp.dma_start(sin[:, :], rope_in[:, 1, :]).then_inc(consts, 16)
        sp.dma_start(mask[:, :], mask_in).then_inc(consts, 16)
        h0_v = h0.rearrange("(a b) s m -> b s a m", b=B)
        h1_v = h1.rearrange("b (t p) d -> b p t d", p=P)

        def load(i, t, dst, sem):
            src = h0_v[bass.ds(i, 1), t * P:(t + 1) * P, :, :].rearrange("o s a m -> (o s) a m")
            sp.dma_start(dst.rearrange("p (a m) -> p a m", m=NM), src).then_inc(sem, 16)

        def load_res(i):
            for t in range(ST):
                load(i, t, res[:, t, :], res_landed)

        def store(i):
            sp.wait_ge(ln_done, i + 1)
            sp.dma_start(h1_v[bass.ds(i, 1), :, :, :].rearrange("o p t d -> (o p) t d"), res[:, :, :])\
              .then_inc(stored, 16)

        load(0, 0, xs[:, :], x_landed)
        sp.wait_ge(proj_ready, 2)
        load(0, 1, xs[:, :], x_landed)
        load_res(0)
        with sp.Fori(0, B - 1) as i:
            sp.wait_ge(rope_lo, i * ROPES + (PAIRED + 2))
            load(i + 1, 0, xs[:, :], x_landed)
            sp.wait_ge(proj_ready, i * UNITS + (UNITS + 2))
            load(i + 1, 1, xs[:, :], x_landed)
            store(i)
            sp.wait_ge(stored, 16 * i + 17)
            load_res(i + 1)
        store(B - 1)
        sp.wait_ge(stored, 16 * B + 1)

    @block.tensor
    def _(pe):
        pe.sem_inc(sc_ready, 2)
        pe.sem_inc(pt_ready, 2)
        for first in (proj_ready, pv_ready, o_done):
            pe.sem_inc(first, 1)
        pe.wait_ge(consts, 64)

        def bank(im, u):
            pe.wait_ge(proj_used, im.u + (u + 1))
            return proj[u % 3]

        def x_transpose(im, t):
            pe.wait_ge(x_landed, im.i * (16 * ST) + 16 * (t + 1))
            b = bank(im, t)
            for c in range(CD):
                mm = pe.transpose(b[:, c * P:(c + 1) * P], xs[:, c * P:(c + 1) * P], ident[:, :])
            mm.then_inc(proj_ready, 1)

        def keys(im, g):
            b = bank(im, K_UNIT[g])
            if g == 0:
                pe.wait_ge(proj_used, im.u + (3 + ST))
            for c in range(CD):
                mm = mm3(pe, b[:, 0:S], [x[:, c, g * HD:(g + 1) * HD] for x in wk], [x[:, c, :] for x in xT],
                         c == 0, c == CD - 1)
            mm.then_inc(proj_ready, 1)

        def values(im, t):
            b = bank(im, V_UNIT[t])
            for c in range(CD):
                mm = mm3(pe, b[:, :], [x[:, c, t * P:(t + 1) * P] for x in xT], [x[:, c, :] for x in wv],
                         c == 0, c == CD - 1)
            mm.then_inc(proj_ready, 1)

        def queries(im, h):
            b = bank(im, Q_UNIT[h])
            for c in range(CD):
                mm = mm3(pe, b[:, 0:S], [x[:, c, h * HD:(h + 1) * HD] for x in wq],
                         [x[:, c, :] for x in xT], c == 0, c == CD - 1)
            mm.then_inc(proj_ready, 1)

        def output(im, h):
            pe.wait_ge(ot_lo, im.n + (h + 2))
            if h == 0:
                pe.wait_ge(ln_var, im.i + 1)
            for t in range(ST):
                mm = mm3(pe, acc[t][:, :], [x[:, t * P:(t + 1) * P] for x in oT], [x[:, h, :] for x in wo],
                         h == 0, h == NH - 1)
            mm.then_inc(o_done, 1)

        def start(im):
            x_transpose(im, 0)
            x_transpose(im, 1)
            for g in range(2):
                keys(im, g)
            rest(im)

        def rest(im):
            keys(im, 2)
            keys(im, 3)
            queries(im, 0)
            values(im, 0)
            values(im, 1)
            queries(im, 1)

        def step(im, s, after, before):
            n = im.n
            if head(s):
                h, g = s, s // REP
                pe.wait_ge(rope_lo, im.r + (NKV + h + 3))
                pe.wait_ge(mx_ready, n + (h + 1))
                qh = q[h % 2]
                mm3(pe, sc[:, 0:P], [x[:, 0:P] for x in qh], [x[:, g, 0:P] for x in kT], True, True)
                mm3(pe, sc[:, P:3 * P], [x[:, P:S] for x in qh], [x[:, g, :] for x in kT], True, True)\
                    .then_inc(sc_ready, 1)
            if s == 0 and before:
                output(before, NH - 1)
            if head(s - 2):
                h, g = s - 2, (s - 2) // REP
                pe.wait_ge(pt_lo, n + (h + 2))
                pe.wait_ge(ot_lo, n + (h + 1))
                if h == 0:
                    pe.wait_ge(proj_used, im.u + (4 + V_UNIT[1]))
                mm3(pe, oTp[:, 0:S], [x[:, 0, g * HD:(g + 1) * HD] for x in v], [x[:, 0:S] for x in pT], True,
                    False)
                mm3(pe, oTp[:, P:S], [x[:, 1, g * HD:(g + 1) * HD] for x in v], [x[:, S:3 * P] for x in pT],
                    False, True).then_inc(pv_ready, 1)
            if head(s + 2):
                queries(im, s + 2)
            elif after and s < NH:
                x_transpose(after, s - (NH - 2))
            elif after and s == NH:
                keys(after, 0)
                keys(after, 1)
            if head(s - 1):
                h = s - 1
                pe.wait_ge(p_ready, n + (h + 1))
                pe.wait_ge(pt_lo, n + (h + 1))
                pr = prob[h % 2]
                pe.transpose(pTp[:, 0:P], pr[:, 0:P], ident[:, :])
                pe.transpose(pTp[:, P:2 * P], pr[:, P:2 * P], ident[:, :])
                pe.transpose(pTp[:, 2 * P:3 * P], pr[:, 2 * P:3 * P], ident[:, :]).then_inc(pt_ready, 1)

            if head(s - 2) and not (after and s == NH + 1):
                output(im, s - 2)
            elif after and s == NH + 1:
                rest(after)

        all_images(pe, start, step)

    @block.scalar
    def _(act):
        def x_split(im, t):
            act.wait_ge(proj_ready, im.u + (t + 2))
            act.activation(xT[0][:, :, t * P:(t + 1) * P], proj[t][:, :].rearrange("p (c s) -> p c s", c=CD),
                           ACT.Copy).then_inc(split_hi, 1)

        def k_split(im, g):
            act.wait_ge(rope_sum, im.r + (g + 1))
            act.activation(kT[0][:, g, :], products(g)[0], ACT.Copy).then_inc(rope_hi, 1)

        def v_split(im, t):
            act.wait_ge(proj_ready, im.u + (V_UNIT[t] + 2))
            act.activation(v[0][:, t, :], proj[V_UNIT[t] % 3][:, :], ACT.Copy).then_inc(split_hi, 1)

        def q_split(im, h):
            act.wait_ge(rope_sum, im.r + (NKV + h + 1))
            act.wait_ge(sc_ready, im.n + (h + 1))
            act.activation(q[h % 2][0][:, :], products(NKV + h)[0], ACT.Copy).then_inc(rope_hi, 1)

        def start(im):
            x_split(im, 0)
            x_split(im, 1)
            k_split(im, 0)
            k_split(im, 1)
            rest(im)

        def rest(im):
            k_split(im, 2)
            k_split(im, 3)
            q_split(im, 0)
            v_split(im, 0)
            v_split(im, 1)

        def step(im, s, after, before):
            n = im.n
            if head(s + 1):
                q_split(im, s + 1)
            if head(s - 2):
                h = s - 2
                act.wait_ge(pv_ready, n + (h + 2))
                act.wait_ge(o_done, n + (h + 1))
                act.activation(oT[0][:, :], oTp[:, 0:S], ACT.Copy).then_inc(ot_hi, 1)
            if head(s):
                h = s
                act.wait_ge(mx_ready, n + (h + 2))
                for t, (a, b) in enumerate(((0, P), (P, 3 * P))):
                    ins = act.activation(prob[h % 2][:, a:b], prob[h % 2][:, a:b], ACT.Exp,
                                         bias=mx[:, h % 2, t:t + 1], scale=-1.0,
                                         accum_out=sums[:, h % 2, t:t + 1])
                ins.then_inc(ex_ready, 1)
            if head(s - 1):
                h = s - 1
                act.wait_ge(pt_ready, n + (h + 3))
                act.wait_ge(pv_ready, n + (h + 1))
                act.activation(pT[0][:, :], pTp[:, 0:3 * P], ACT.Copy).then_inc(pt_hi, 1)
            if after and s in (NH - 2, NH - 1):
                x_split(after, s - (NH - 2))
            elif after and s == NH:
                act.wait_ge(sc_ready, after.n + 2)
                k_split(after, 0)
                k_split(after, 1)
            elif after and s == NH + 1:
                act.wait_ge(pv_ready, after.n + 1)
                rest(after)

        all_images(act, start, step)

    @block.gpsimd
    def _(pool):
        pool.sem_inc(rope_lo, 2)
        pool.memset(nhalf[:, :], -0.5)

        def parts(r):
            return (kT[0][:, r, :], kT[1][:, r, :]) if r < NKV else (q[r % 2][0][:, :], q[r % 2][1][:, :])

        def add(im, r):
            u = K_UNIT[r] if r < NKV else Q_UNIT[r - NKV]
            a, b = products(r)
            pool.wait_ge(proj_used, im.u + (3 + u + 1))
            pool.tensor_tensor(a, a, b, ALU.add).then_inc(rope_sum, 1)

        def rest_of(im, r):
            hi, lo = parts(r)
            pool.wait_ge(rope_hi, im.r + (r + 1))
            pool.tensor_tensor(lo, products(r)[0], hi.bitcast(F32), ALU.subtract).then_inc(rope_lo, 1)

        def start(im):
            add(im, 0)
            add(im, 1)
            rest_of(im, 0)
            rest_of(im, 1)
            rest(im)

        def rest(im):
            add(im, 2)
            add(im, 3)
            rest_of(im, 2)
            add(im, NKV)
            rest_of(im, 3)
            rest_of(im, NKV)
            add(im, NKV + 1)

        def step(im, s, after, before):
            if s == 0:
                rest_of(im, NKV + 1)
            if head(s + 2):
                add(im, NKV + s + 2)
                rest_of(im, NKV + s + 2)
            if s == 1 and before:
                power(before)
            if after and s == NH:
                add(after, 0)
                add(after, 1)
                rest_of(after, 0)
                rest_of(after, 1)
            elif after and s == NH + 1:
                rest(after)

        def power(im):
            pool.wait_ge(ln_var, im.i + 2)
            pool.tensor_tensor(mv[:, :, 1], mv[:, :, 1], nhalf[:, :], ALU.pow).then_inc(ln_rstd, 1)

        all_images(pool, start, step, power)

    @block.vector
    def _(dve):
        dve.sem_inc(proj_used, 3)
        for first in (mx_ready, ot_lo, pt_lo, ln_var):
            dve.sem_inc(first, 1)
        dve.wait_ge(consts, 64)

        def rope(im, u, r):
            b, (p, p_turned) = proj[u % 3], products(r)
            dve.wait_ge(proj_ready, im.u + (u + 2))
            dve.wait_ge(rope_lo, im.r + (r + (1 if 0 < r <= PAIRED else 2)))
            dve.tensor_tensor(p_turned[0:64, :], b[64:P, 0:S], sin[0:64, :], ALU.mult)
            dve.tensor_tensor(p_turned[64:P, :], b[0:64, 0:S], sin[64:P, :], ALU.mult)
            dve.tensor_tensor(p, b[:, 0:S], cos[:, :], ALU.mult).then_inc(proj_used, 1)

        def x_split(im, t):
            dve.wait_ge(split_hi, im.i * (2 * ST) + (t + 1))
            sl = slice(t * P, (t + 1) * P)
            dve.tensor_tensor(xT[1][:, :, sl], proj[t][:, :].rearrange("p (c s) -> p c s", c=CD),
                              xT[0][:, :, sl].bitcast(F32), ALU.subtract).then_inc(proj_used, 1)

        def keys(im, g):
            rope(im, K_UNIT[g], g)

        def v_split(im, t):
            dve.wait_ge(split_hi, im.i * (2 * ST) + (ST + t + 1))
            dve.tensor_tensor(v[1][:, t, :], proj[V_UNIT[t] % 3][:, :], v[0][:, t, :].bitcast(F32),
                              ALU.subtract).then_inc(proj_used, 1)

        def queries(im, h):
            rope(im, Q_UNIT[h], NKV + h)

        def start(im):
            x_split(im, 0)
            x_split(im, 1)
            keys(im, 0)
            keys(im, 1)
            rest(im)

        def rest(im):
            keys(im, 2)
            keys(im, 3)
            queries(im, 0)
            v_split(im, 0)
            v_split(im, 1)
            queries(im, 1)

        def variance(im):
            ch = Chain(dve, ln_chain, im.i * LN_STEPS)
            dve.wait_ge(o_done, im.n + (NH + 1))
            dve.wait_ge(res_landed, im.i * (16 * ST) + 16 * ST)
            for t in range(ST):
                ins = dve.tensor_tensor(res[:, t, :], res[:, t, :], acc[t][:, :], ALU.add)
            ch(ins)
            for t in range(ST):
                ins = dve.bn_stats(st[:, t, :], res[:, t, :])
            ch(ins)
            carry_wait(dve, dve_passed)
            for t in range(ST):
                ins = dve.bn_aggr(mv[:, t, :], st[:, t, :])
            ch(ins)
            dve.tensor_scalar(mv[:, :, 1], mv[:, :, 1], LN_EPS, None, ALU.add).then_inc(ln_var, 1)

        def normalise(im):
            dve.wait_ge(ln_rstd, im.i + 1)
            for t in range(ST):
                ins = dve.tensor_scalar(res[:, t, :], res[:, t, :], mv[:, t, 0:1], mv[:, t, 1:2], ALU.subtract,
                                        ALU.mult)
            ins.then_inc(ln_done, 1)

        def step(im, s, after, before):
            n = im.n
            if head(s):
                h = s
                dve.wait_ge(sc_ready, n + (h + 3))
                dve.wait_ge(pt_ready, n + (h + 1))
                carry_wait(dve, dve_passed)
                for t, (a, b) in enumerate(((0, P), (P, 3 * P))):
                    ins = dve.tensor_tensor_reduce(out=prob[h % 2][:, a:b], in0=sc[:, a:b],
                                                   in1=mask[:, 2 * P - (b - a):2 * P], scale=-SCALE, scalar=BIG,
                                                   op0=ALU.add, op1=ALU.min, accum_out=mx[:, h % 2, t:t + 1])
                ins.then_inc(mx_ready, 1)
            if head(s - 2):
                h = s - 2
                dve.wait_ge(ot_hi, n + (h + 1))
                dve.tensor_tensor(oT[1][:, :], oTp[:, 0:S], oT[0][:, :].bitcast(F32), ALU.subtract)\
                   .then_inc(ot_lo, 1)
            if head(s):
                h = s
                dve.wait_ge(ex_ready, n + (h + 1))
                dve.reciprocal(inv[:, h % 2, :], sums[:, h % 2, :]).then_inc(inv_ready, 1)
                dve.wait_ge(inv_ready, n + (h + 1))
                for t, (a, b) in enumerate(((0, P), (P, 3 * P))):
                    ins = dve.tensor_scalar(prob[h % 2][:, a:b], prob[h % 2][:, a:b], inv[:, h % 2, t:t + 1],
                                            None, ALU.mult)
                ins.then_inc(p_ready, 1)
            if head(s + 2):
                queries(im, s + 2)
            if head(s - 1):
                h = s - 1
                dve.wait_ge(pt_hi, n + (h + 1))
                dve.tensor_tensor(pT[1][:, :], pTp[:, 0:3 * P], pT[0][:, :].bitcast(F32), ALU.subtract)\
                   .then_inc(pt_lo, 1)
            if s == 1 and before:
                variance(before)
            if s == 2 and before:
                normalise(before)
            if after and s in (NH - 2, NH - 1):
                x_split(after, s - (NH - 2))
            elif after and s == NH:
                keys(after, 0)
                keys(after, 1)
            elif after and s == NH + 1:
                rest(after)

        def finish(im):
            variance(im)
            normalise(im)

        all_images(dve, start, step, finish)


NH1, HD1 = 16, 32
G1 = 4
QEPS = 1e-5
F_UNITS = ["qT", "ffn0", "ffn1", "x0", "x1", "q0", "kv0", "q1", "kv1", "tq0", "tk0", "tq1", "tk1"]
G_UNITS = ["out0", "out1"]
ALL_UNITS = G_UNITS + F_UNITS
HIS = ["x0", "x1", "v0", "v1", "tq0", "tk0", "tq1", "tk1"]
BETWEEN = {0: ["f_quant"], 1: ["g_out0"], 2: ["g_out1"], 3: ["f_qT"], 4: ["g_norm", "f_ffn"], 6: ["f_norm"], 8: ["f_xT"],
           10: ["f_q0"], 12: ["f_kv0"], 14: ["f_q1"], 15: ["f_kv1"], 16: ["f_hT0"], 17: ["f_hT1"]}
LAG = 4


class Segment:

    def __init__(self, b, kind, parity):
        self.b, self.kind, self.parity = b, kind, parity
        self.units = {"front": F_UNITS, "all": ALL_UNITS, "back": G_UNITS}[kind]
        self.hi0 = len(HIS) * (b + 1)
        before = 2 * len(F_UNITS) - len(ALL_UNITS)
        if kind == "front":
            self.unit0 = len(F_UNITS) * (b + 1)
            self.mod = self.unit0 % 3
        elif kind == "all" or b == B - 1:
            self.unit0 = b * len(ALL_UNITS) + before
            self.mod = before % 3
        else:
            self.unit0 = (B - 1) * len(ALL_UNITS) + before + len(G_UNITS)
            self.mod = self.unit0 % 3

    def unit(self, name):
        return self.unit0 + (self.units.index(name) + 1)

    def bank(self, name):
        return (self.mod + self.units.index(name)) % 3

    def hi(self, name):
        return self.hi0 + (HIS.index(name) + 1)


def run_segment(seg, h):
    heads = 0 <= seg.b < B if isinstance(seg.b, int) else True
    for s in range(NH1 + LAG + 1):
        for name, k in (("read", s - LAG), ("sc", s), ("mx", s), ("ex", s - 1), ("pt", s - 2), ("pv", s - 3)):
            if heads and name in h and 0 <= k < NH1:
                h[name](seg, k)
        if heads and "divide" in h and s >= LAG and (s - LAG) % 4 == 3:
            h["divide"](seg, (s - LAG) // 4)
        if heads and "split" in h and s > LAG and (s - LAG) % 4 == 0:
            h["split"](seg, (s - LAG) // 4 - 1)
        for name in BETWEEN.get(s, []):
            if name[0] == "g" and seg.kind == "front" or name[0] == "f" and seg.kind == "back":
                continue
            stage = name.rstrip("01")
            if stage in h:
                h[stage](seg) if stage == name else h[stage](seg, int(name[-1]))


def all_segments(eng, h):
    run_segment(Segment(-1, "front", 1), h)
    run_segment(Segment(0, "front", 0), h)
    with eng.Fori(0, (B - 2) // 2) as i:
        run_segment(Segment(i * 2 + 1, "all", 1), h)
        run_segment(Segment(i * 2 + 2, "all", 0), h)
    run_segment(Segment(B - 1, "back", 1), h)
    run_segment(Segment(B, "back", 0), h)


def block01(nc, fw_in, fb_in, wq_in, wkv_in, wo_in, bias_in, rope_in, mask_in, ident_in, identb_in, h1, h3):
    SCALE = float(HD1) ** -0.5
    with ExitStack() as ctx:
        m = Memory(nc, ctx)
        ident = m.sb("b_ident", [P, P])
        identb = m.sb("b_identb", [P, P], BF16)
        rope = m.sb("b_rope", [P, 2, ST, HD1])
        mask = m.sb("b_mask", [P, 2 * P])
        fraw = m.sb("b_fraw", [P, CD * D])
        ftmp = m.sb("b_ftmp", [P, CD * D])
        fw = m.sb("b_fw", [P, CD, D], BF16)
        fbias = m.sb("b_fbias", [P, D])
        asum = m.sb("b_asum", [P, 1])
        alpha = m.sb("b_alpha", [P, 2])
        ones = m.sb("b_ones", [P, P])
        onesr = m.sb("b_onesr", [1, P], F32R)
        wraw = m.sb("b_wraw", [P, CD, D + 2 * P + D], BF16)
        wq = m.sb("b_wq", [P, CD, D], F32R)
        wkv = m.sb("b_wkv", [P, CD, 2 * P], F32R)
        wo = m.sb("b_wo", [P, CD, D], F32R)
        braw = m.sb("b_braw", [1, D + 2 * P], BF16)
        bqkv = m.sb("b_bqkv", [1, D + 2 * P], F32R)
        x1 = m.sb("b_x1", [P, ST, D])
        am = m.sb("b_am", [P, ST])
        rs = m.sb("b_rs", [P, ST])
        sa = m.sb("b_sa", [P, ST])
        qf = m.sb("b_qf", [P, ST, D])
        qb = m.sb("b_qb", [P, ST, D], BF16)
        xb = m.sb("b_xb", [P, ST, D])
        qTb = m.sb("b_qTb", [P, ST, CD, P], BF16)
        x2 = [m.sb(f"b_x2{n}", [P, ST, D]) for n in range(2)]
        xT = [m.sb(f"b_xT{p}", [P, CD, S], F32R) for p in "hl"]
        tq = [m.sb(f"b_tq{n}", [P, D]) for n in range(2)]
        tk = [m.sb(f"b_tk{n}", [P, P]) for n in range(2)]
        qr = m.sb("b_qr", [P, ST, D])
        kr = m.sb("b_kr", [P, ST, D])
        qT = [[m.sb(f"b_qT{p}{n}", [P, G1, S], F32R) for p in "hl"] for n in range(2)]
        kT = [[m.sb(f"b_kT{p}{n}", [P, G1, S], F32R) for p in "hl"] for n in range(2)]
        v = [[m.sb(f"b_v{p}{n}", [P, ST, G1, 2 * HD1], F32R) for p in "hl"] for n in range(2)]
        prob = [m.sb(f"b_prob{n}", [P, 3 * P]) for n in range(4)]
        pT = [[m.sb(f"b_pT{p}{n}", [P, 3 * P], F32R) for p in "hl"] for n in range(2)]
        mx = m.sb("b_mx", [P, 4, ST])
        sums = m.sb("b_sums", [P, 2, S])
        on = m.sb("b_on", [P, CD, S])
        oT = [m.sb(f"b_oT{p}", [P, CD, S], F32R) for p in "hl"]
        y = m.sb("b_y", [P, ST, D])
        st = m.sb("b_st", [P, 2, ST, 6])
        mv = m.sb("b_mv", [P, 2, ST, 2])
        nhalf = m.sb("b_nhalf", [P, ST])
        misc = [m.ps(f"b_misc{n}", [P, D]) for n in range(3)]
        sc = [m.ps(f"b_sc{n}", [P, 512]) for n in range(2)]
        pTp = m.ps("b_pTp", [P, 512])
        oTp = [m.ps(f"b_oTp{n}", [P, 512]) for n in range(2)]

        consts = m.sem("b_consts")
        dve_passed = m.sem("b_dve_passed")
        prep_act = m.sem("b_prep_act")
        prep_dve = m.sem("b_prep_dve")
        prep_pe = m.sem("b_prep_pe")
        x1_landed = m.sem("b_x1_landed")
        xb_done = m.sem("b_xb_done")
        fq_chain = m.sem("b_fq_chain")
        q_done = m.sem("b_q_done")
        misc_ready = m.sem("b_misc_ready")
        misc_used = m.sem("b_misc_used")
        hi_done = m.sem("b_hi_done")
        ln_chain = [m.sem(f"b_ln_chain{n}") for n in range(2)]
        ln_var = [m.sem(f"b_ln_var{n}") for n in range(2)]
        ln_rstd = [m.sem(f"b_ln_rstd{n}") for n in range(2)]
        x2_done = m.sem("b_x2_done")
        rope_done = m.sem("b_rope_done")
        sc_ready = m.sem("b_sc_ready")
        mx_ready = m.sem("b_mx_ready")
        ex_ready = m.sem("b_ex_ready")
        pt_ready = m.sem("b_pt_ready")
        pt_hi = m.sem("b_pt_hi")
        pt_lo = m.sem("b_pt_lo")
        pv_ready = m.sem("b_pv_ready")
        o_read = m.sem("b_o_read")
        inverted = m.sem("b_inverted")
        divided = m.sem("b_divided")
        ot_hi = m.sem("b_ot_hi")
        ot_lo = m.sem("b_ot_lo")
        y_done = m.sem("b_y_done")
        stored = m.sem("b_stored")
        NLN, NFQ = 2, 4
        block = ctx.enter_context(nc.Block())

        @block.sync
        def _(sp):
            sp.sem_inc(stored, 1)
            for dst, src in ((fraw[:, :], fw_in), (fbias[:, :], fb_in), (wraw[:, :, 0:D], wq_in),
                             (wraw[:, :, D:D + 2 * P], wkv_in), (wraw[:, :, D + 2 * P:], wo_in), (braw[:, :], bias_in),
                             (rope[:, :, :, :], rope_in), (mask[:, :], mask_in), (ident[:, :], ident_in),
                             (identb[:, :], identb_in)):
                sp.dma_start(dst, src).then_inc(consts, 16)
            h1_v = h1.rearrange("b (t p) d -> b p t d", p=P)
            h3_v = h3.rearrange("b (t p) d -> b p t d", p=P)

            def load(b):
                sp.wait_ge(q_done, b)
                sp.wait_ge(xb_done, b)
                sp.dma_start(x1[:, :, :], h1_v[bass.ds(b, 1)].rearrange("o p t d -> (o p) t d"))\
                  .then_inc(x1_landed, 16)

            def store(b):
                sp.wait_ge(y_done, b + 1)
                sp.dma_start(h3_v[bass.ds(b, 1)].rearrange("o p t d -> (o p) t d"), y[:, :, :]).then_inc(stored, 16)

            for b in range(3):
                load(b)
            with sp.Fori(0, B - 3) as i:
                store(i)
                load(i + 3)
            for b in range(B - 3, B):
                store(b)
            sp.wait_ge(stored, 16 * B + 1)

        @block.tensor
        def _(pe):
            pe.sem_inc(pt_ready, 4)
            pe.sem_inc(pv_ready, 1)
            pe.wait_ge(prep_act, 8)
            pe.wait_ge(prep_dve, 1)
            pe.matmul(misc[0][:, 0:1], ones[:, :], asum[:, :], start=True, stop=True).then_inc(prep_pe, 1)
            pe.wait_ge(prep_dve, 6)

            def bank(seg, name):
                pe.wait_ge(misc_used, seg.unit(name))
                return misc[seg.bank(name)]

            def f_qT(seg):
                pe.wait_ge(q_done, seg.b + 2)
                b = bank(seg, "qT")[:, :].bitcast(BF16)
                for t in range(ST):
                    for c in range(CD):
                        a = (t * CD + c) * P
                        mm = pe.transpose(b[:, a:a + P], qb[:, t, c * P:(c + 1) * P], identb[:, :])
                mm.then_inc(misc_ready, 1)

            def f_ffn(seg):
                for t in range(ST):
                    b = bank(seg, f"ffn{t}")
                    pe.wait_ge(misc_used, seg.unit("qT") + 3)
                    for c in range(CD):
                        mm = pe.matmul(b[:, :], qTb[:, t, c, :], fw[:, c, :], start=c == 0, stop=c == CD - 1)
                    mm.then_inc(misc_ready, 1)

            def f_xT(seg):
                pe.wait_ge(x2_done, seg.b + 2)
                for t in range(ST):
                    b = bank(seg, f"x{t}")
                    for c in range(CD):
                        mm = pe.transpose(b[:, c * P:(c + 1) * P], x2[1 - seg.parity][:, t, c * P:(c + 1) * P],
                                          ident[:, :])
                    mm.then_inc(misc_ready, 1)

            def project(seg, t, name, w, a, n):
                b = bank(seg, f"{name}{t}")
                pe.wait_ge(misc_used, seg.unit("x1") + 3)
                pe.matmul(b[:, 0:n], onesr[:, :], bqkv[:, a:a + n], start=True, stop=False)
                for c in range(CD):
                    for x in xT:
                        mm = pe.matmul(b[:, 0:n], x[:, c, t * P:(t + 1) * P], w[:, c, :], start=False,
                                       stop=c == CD - 1 and x is xT[1])
                mm.then_inc(misc_ready, 1)

            def f_q(seg, t):
                project(seg, t, "q", wq, 0, D)

            def f_kv(seg, t):
                project(seg, t, "kv", wkv, D, 2 * P)

            def f_hT(seg, t):
                pe.wait_ge(rope_done, seg.b * ST + (ST + t + 1))
                for name, src in (("tq", qr), ("tk", kr)):
                    b = bank(seg, f"{name}{t}")
                    for c in range(CD):
                        mm = pe.transpose(b[:, c * P:(c + 1) * P], src[:, t, c * P:(c + 1) * P], ident[:, :])
                    mm.then_inc(misc_ready, 1)

            def score(seg, s):
                if s == 0:
                    pe.wait_ge(misc_used, seg.unit0 + 3)
                pe.wait_ge(mx_ready, seg.b * NH1 + (s + 1))
                g, r = s // 4, slice(32 * (s % 4), 32 * (s % 4) + 32)
                qs, ks = qT[seg.parity], kT[seg.parity]
                mm3(pe, sc[s % 2][:, 0:P], [x[r, g, 0:P] for x in qs], [x[r, g, 0:P] for x in ks], True, True)
                mm3(pe, sc[s % 2][:, P:3 * P], [x[r, g, P:S] for x in qs], [x[r, g, :] for x in ks], True, True)\
                    .then_inc(sc_ready, 1)

            def pt(seg, s):
                pe.wait_ge(ex_ready, seg.b * NH1 + (s + 1))
                pe.wait_ge(pt_lo, seg.b * NH1 + s)
                for c in range(3):
                    mm = pe.transpose(pTp[:, c * P:(c + 1) * P], prob[s % 4][:, c * P:(c + 1) * P], ident[:, :])
                mm.then_inc(pt_ready, 1)

            def pv(seg, s):
                pe.wait_ge(pt_lo, seg.b * NH1 + (s + 1))
                pe.wait_ge(o_read, seg.b * NH1 + (s + 1))
                p, vs, g, o = pT[s % 2], v[seg.parity], s // 4, oTp[s % 2]
                mm3(pe, o[0:2 * HD1, 0:S], [x[:, 0, g, :] for x in vs], [x[:, 0:S] for x in p], True, False)
                mm3(pe, o[0:2 * HD1, P:S], [x[:, 1, g, :] for x in vs], [x[:, S:3 * P] for x in p], False, True)\
                    .then_inc(pv_ready, 1)

            def g_out(seg, t):
                pe.wait_ge(ot_lo, seg.b * G1)
                b = bank(seg, f"out{t}")
                for c in range(CD):
                    for x in oT:
                        mm = pe.matmul(b[:, :], x[:, c, t * P:(t + 1) * P], wo[:, c, :],
                                       start=c == 0 and x is oT[0], stop=c == CD - 1 and x is oT[1])
                mm.then_inc(misc_ready, 1)

            all_segments(pe, {"f_qT": f_qT, "f_ffn": f_ffn, "f_xT": f_xT, "f_q": f_q, "f_kv": f_kv, "f_hT": f_hT,
                              "sc": score, "pt": pt, "pv": pv, "g_out": g_out})

        @block.scalar
        def _(act):
            act.sem_inc(o_read, 2)
            act.wait_ge(consts, 160)
            act.activation(ftmp[:, :], fraw[:, :], ACT.Abs, accum_out=asum[:, :]).then_inc(prep_act, 1)
            act.activation(wq[:, :, :], wraw[:, :, 0:D], ACT.Copy).then_inc(prep_act, 1)
            act.activation(wkv[:, :, :], wraw[:, :, D:D + 2 * P], ACT.Copy).then_inc(prep_act, 1)
            act.activation(wo[:, :, :], wraw[:, :, D + 2 * P:], ACT.Copy).then_inc(prep_act, 1)
            act.activation(bqkv[:, :], braw[:, :], ACT.Copy).then_inc(prep_act, 1)
            act.wait_ge(prep_dve, 1)
            act.activation(onesr[:, :], ones[0:1, :], ACT.Copy).then_inc(prep_act, 2)
            for n in range(2):
                for t in range(ST):
                    block_of_ones = ones[:, :].rearrange("p (g d) -> p g d", g=G1)
                    act.activation(v[n][0][:, t, :, HD1:], block_of_ones, ACT.Copy)
                    ins = act.activation(v[n][1][:, t, :, HD1:], block_of_ones, ACT.Copy, scale=0.0)
            ins.then_inc(prep_act, 1)

            def f_xT(seg):
                for t in range(ST):
                    act.wait_ge(misc_ready, seg.unit(f"x{t}"))
                    act.activation(xT[0][:, :, t * P:(t + 1) * P],
                                   misc[seg.bank(f"x{t}")][:, :].rearrange("p (c s) -> p c s", c=CD),
                                   ACT.Copy).then_inc(hi_done, 1)

            def f_kv(seg, t):
                act.wait_ge(misc_ready, seg.unit(f"kv{t}"))
                act.activation(v[1 - seg.parity][0][:, t, :, 0:HD1],
                               misc[seg.bank(f"kv{t}")][:, P:2 * P].rearrange("p (g d) -> p g d", g=G1),
                               ACT.Copy).then_inc(hi_done, 1)

            def f_hT(seg, t):
                for name, dst in (("tq", qT), ("tk", kT)):
                    act.wait_ge(misc_ready, seg.unit(f"{name}{t}"))
                    act.activation(dst[1 - seg.parity][0][:, :, t * P:(t + 1) * P],
                                   misc[seg.bank(f"{name}{t}")][:, :].rearrange("p (c s) -> p c s", c=G1),
                                   ACT.Copy).then_inc(hi_done, 1)

            def ex(seg, s):
                act.wait_ge(mx_ready, seg.b * NH1 + (s + 3))
                for t, (a, b) in enumerate(((0, P), (P, 3 * P))):
                    ins = act.activation(prob[s % 4][:, a:b], prob[s % 4][:, a:b], ACT.Exp,
                                         bias=mx[:, s % 4, t:t + 1], scale=-1.0)
                ins.then_inc(ex_ready, 1)

            def pt(seg, s):
                act.wait_ge(pt_ready, seg.b * NH1 + (s + 5))
                act.wait_ge(pv_ready, seg.b * NH1 + s)
                act.activation(pT[s % 2][0][:, :], pTp[:, 0:3 * P], ACT.Copy).then_inc(pt_hi, 1)

            def read(seg, s):
                g, r = s // 4, slice(HD1 * (s % 4), HD1 * (s % 4 + 1))
                act.wait_ge(pv_ready, seg.b * NH1 + (s + 2))
                if s % 4 == 0 and seg.kind != "front":
                    act.wait_ge(ot_lo, seg.b * G1 + (g + 1 - G1))
                act.activation(on[r, g, :], oTp[s % 2][0:HD1, 0:S], ACT.Copy)
                act.activation(sums[r, g % 2, :], oTp[s % 2][HD1:2 * HD1, 0:S], ACT.Copy).then_inc(o_read, 1)

            def split(seg, g):
                act.wait_ge(divided, seg.b * G1 + (g + 1))
                if g == 0 and seg.kind != "front":
                    act.wait_ge(misc_ready, seg.unit("out1"))
                act.activation(oT[0][:, g, :], on[:, g, :], ACT.Copy).then_inc(ot_hi, 1)

            all_segments(act, {"f_xT": f_xT, "f_kv": f_kv, "f_hT": f_hT, "ex": ex, "pt": pt, "read": read,
                               "split": split})

        @block.gpsimd
        def _(pool):
            pool.memset(nhalf[:, :], -0.5)
            pool.wait_ge(consts, 160)

            def f_quant(seg):
                pool.wait_ge(x1_landed, seg.b * 16 + 32)
                pool.wait_ge(x2_done, seg.b + 1)
                pool.tensor_tensor(xb[:, :, :], x1[:, :, :], fbias[:, :].unsqueeze(1).broadcast_to([P, ST, D]),
                                   ALU.add).then_inc(xb_done, 1)

            def rstd(n, images):
                pool.wait_ge(ln_var[n], images)
                pool.tensor_tensor(mv[:, n, :, 1], mv[:, n, :, 1], nhalf[:, :], ALU.pow).then_inc(ln_rstd[n], 1)

            def f_q(seg, t):
                pool.wait_ge(misc_used, seg.unit(f"q{t}") + 3)
                pool.tensor_tensor(qr[:, t, :], tq[0][:, :], tq[1][:, :], ALU.add)

            def f_kv(seg, t):
                pool.wait_ge(misc_used, seg.unit(f"kv{t}") + 3)
                shape = [P, G1, 4, HD1]
                a, b = [x[:, :].rearrange("p (g d) -> p g d", g=G1).unsqueeze(2).broadcast_to(shape) for x in tk]
                pool.tensor_tensor(kr[:, t, :].rearrange("p (g r d) -> p g r d", g=G1, r=4), a, b,
                                   ALU.add).then_inc(rope_done, 1)

            def divide(seg, g):
                pool.wait_ge(inverted, seg.b * G1 + (g + 1))
                pool.tensor_tensor(on[:, g, :], on[:, g, :], sums[:, g % 2, :], ALU.mult).then_inc(divided, 1)

            def split(seg, g):
                pool.wait_ge(ot_hi, seg.b * G1 + (g + 1))
                pool.tensor_tensor(oT[1][:, g, :], on[:, g, :], oT[0][:, g, :].bitcast(F32),
                                   ALU.subtract).then_inc(ot_lo, 1)

            all_segments(pool, {"f_quant": f_quant, "f_norm": lambda seg: rstd(0, seg.b + 2), "f_q": f_q,
                                "f_kv": f_kv, "g_norm": lambda seg: rstd(1, seg.b), "divide": divide,
                                "split": split})

        @block.vector
        def _(dve):
            dve.sem_inc(misc_used, 3)
            dve.sem_inc(mx_ready, 2)
            dve.memset(ones[:, :], 1.0).then_inc(prep_dve, 1)
            dve.wait_ge(prep_pe, 1)
            c = Chain(dve, prep_dve, 1)
            c(dve.tensor_scalar(alpha[:, 0:1], misc[0][:, 0:1], 1.0 / (D * D), QEPS, ALU.mult, ALU.max))
            c(dve.reciprocal(alpha[:, 1:2], alpha[:, 0:1]))
            c(dve.tensor_scalar(ftmp[:, :], fraw[:, :], alpha[:, 1:2], ROUND, ALU.mult, ALU.add))
            c(dve.tensor_scalar(ftmp[:, :], ftmp[:, :], ROUND, 1.0, ALU.subtract, ALU.min))
            c(dve.tensor_scalar(fw[:, :, :].rearrange("p c n -> p (c n)"), ftmp[:, :], -1.0, None, ALU.max))

            def f_quant(seg):
                c = Chain(dve, fq_chain, seg.b * NFQ + NFQ)
                dve.wait_ge(x1_landed, seg.b * 16 + 32)
                c(dve.tensor_reduce(am[:, :], x1[:, :, :], AX_X, ALU.max, apply_absolute_value=True))
                c(dve.tensor_scalar(am[:, :], am[:, :], QEPS, 1.0 / 127.0, ALU.max, ALU.mult))
                c(dve.reciprocal(rs[:, :], am[:, :]))
                dve.tensor_scalar(sa[:, :], am[:, :], alpha[:, 0:1], None, ALU.mult)
                for t in range(ST):
                    ins = dve.tensor_scalar(qf[:, t, :], x1[:, t, :], rs[:, t:t + 1], ROUND, ALU.mult, ALU.add)
                c(ins)
                dve.tensor_scalar(qb[:, :, :], qf[:, :, :], ROUND, 127.0, ALU.subtract, ALU.min).then_inc(q_done, 1)

            def f_qT(seg):
                dve.wait_ge(misc_ready, seg.unit("qT"))
                dve.tensor_copy(qTb[:, :, :, :].rearrange("p t c s -> p (t c s)"),
                                misc[seg.bank("qT")][:, :].bitcast(BF16)).then_inc(misc_used, 1)

            def stats(n, images, out):
                c = Chain(dve, ln_chain[n], images * NLN - NLN)
                for t in range(ST):
                    ins = dve.bn_stats(st[:, n, t, :], out[:, t, :])
                c(ins)
                carry_wait(dve, dve_passed)
                for t in range(ST):
                    ins = dve.bn_aggr(mv[:, n, t, :], st[:, n, t, :])
                c(ins)
                dve.tensor_scalar(mv[:, n, :, 1], mv[:, n, :, 1], LN_EPS, None, ALU.add).then_inc(ln_var[n], 1)

            def norm(n, images, out, done):
                dve.wait_ge(ln_rstd[n], images)
                for t in range(ST):
                    ins = dve.tensor_scalar(out[:, t, :], out[:, t, :], mv[:, n, t, 0:1], mv[:, n, t, 1:2],
                                            ALU.subtract, ALU.mult)
                ins.then_inc(done, 1)

            def f_ffn(seg):
                x = x2[1 - seg.parity]
                dve.wait_ge(xb_done, seg.b + 2)
                for t in range(ST):
                    dve.wait_ge(misc_ready, seg.unit(f"ffn{t}"))
                    dve.scalar_tensor_tensor(x[:, t, :], misc[seg.bank(f"ffn{t}")][:, :], sa[:, t:t + 1],
                                             xb[:, t, :], ALU.mult, ALU.add).then_inc(misc_used, 1)
                dve.wait_ge(misc_used, seg.unit("ffn1") + 3)
                stats(0, seg.b + 2, x)

            def lo(seg, name, hi_name, out, hi, a=0, n=D):
                dve.wait_ge(hi_done, seg.hi(hi_name))
                b = misc[seg.bank(name)][:, a:a + n]
                if len(out.shape) == 3:
                    b = b.rearrange("p (c s) -> p c s", c=CD)
                dve.tensor_tensor(out, b, hi.bitcast(F32), ALU.subtract).then_inc(misc_used, 1)

            def f_xT(seg):
                for t in range(ST):
                    sl = slice(t * P, (t + 1) * P)
                    lo(seg, f"x{t}", f"x{t}", xT[1][:, :, sl], xT[0][:, :, sl])

            def turn(b, t, out, heads):
                x = b.rearrange("p (h two d) -> p h two d", two=2, d=HD1 // 2)
                t1, t2 = out
                r1 = t1[:, :].rearrange("p (h d) -> p h d", d=HD1)
                r2 = t2[:, :].rearrange("p (h two d) -> p h two d", two=2, d=HD1 // 2)
                cs = rope[:, 0, t, :].unsqueeze(1).broadcast_to([P, heads, HD1])
                half = [P, heads, HD1 // 2]
                dve.tensor_tensor(r2[:, :, 0, :], x[:, :, 1, :],
                                  rope[:, 1, t, 0:HD1 // 2].unsqueeze(1).broadcast_to(half), ALU.mult)
                dve.tensor_tensor(r2[:, :, 1, :], x[:, :, 0, :],
                                  rope[:, 1, t, HD1 // 2:].unsqueeze(1).broadcast_to(half), ALU.mult)
                return dve.tensor_tensor(r1, b.rearrange("p (h d) -> p h d", d=HD1), cs, ALU.mult)

            def f_q(seg, t):
                dve.wait_ge(rope_done, seg.b * ST + (ST + t))
                dve.wait_ge(misc_ready, seg.unit(f"q{t}"))
                turn(misc[seg.bank(f"q{t}")][:, :], t, tq, NH1).then_inc(misc_used, 1)

            def f_kv(seg, t):
                dve.wait_ge(hi_done, seg.hi(f"v{t}"))
                turn(misc[seg.bank(f"kv{t}")][:, 0:P], t, tk, G1)
                vv = [x[:, t, :, 0:HD1] for x in v[1 - seg.parity]]
                lo(seg, f"kv{t}", f"v{t}", vv[1], vv[0], P, P)

            def f_hT(seg, t):
                sl = slice(t * P, (t + 1) * P)
                for name, dst in (("tq", qT), ("tk", kT)):
                    d = dst[1 - seg.parity]
                    lo(seg, f"{name}{t}", f"{name}{t}", d[1][:, :, sl], d[0][:, :, sl])

            def maxima(seg, s):
                dve.wait_ge(sc_ready, seg.b * NH1 + (s + 1))
                dve.wait_ge(pt_ready, seg.b * NH1 + (s + 1))
                carry_wait(dve, dve_passed)
                for t, (a, b) in enumerate(((0, P), (P, 3 * P))):
                    ins = dve.tensor_tensor_reduce(out=prob[s % 4][:, a:b], in0=sc[s % 2][:, a:b],
                                                   in1=mask[:, 2 * P - (b - a):2 * P], scale=-SCALE, scalar=BIG,
                                                   op0=ALU.add, op1=ALU.min, accum_out=mx[:, s % 4, t:t + 1])
                ins.then_inc(mx_ready, 1)

            def pt(seg, s):
                dve.wait_ge(pt_hi, seg.b * NH1 + (s + 1))
                dve.tensor_tensor(pT[s % 2][1][:, :], pTp[:, 0:3 * P], pT[s % 2][0][:, :].bitcast(F32),
                                  ALU.subtract).then_inc(pt_lo, 1)

            def divide(seg, g):
                dve.wait_ge(o_read, seg.b * NH1 + (4 * g + 6))
                dve.reciprocal(sums[:, g % 2, :], sums[:, g % 2, :]).then_inc(inverted, 1)

            def g_out(seg, t):
                if t == 0:
                    dve.wait_ge(stored, seg.b * 16 - 15)
                dve.wait_ge(misc_ready, seg.unit(f"out{t}"))
                dve.tensor_tensor(y[:, t, :], misc[seg.bank(f"out{t}")][:, :], x2[1 - seg.parity][:, t, :],
                                  ALU.add).then_inc(misc_used, 1)
                if t == ST - 1:
                    dve.wait_ge(misc_used, seg.unit("out1") + 3)
                    stats(1, seg.b, y)

            all_segments(dve, {"f_quant": f_quant, "f_qT": f_qT, "f_ffn": f_ffn,
                               "f_norm": lambda seg: norm(0, seg.b + 2, x2[1 - seg.parity], x2_done), "f_xT": f_xT,
                               "f_q": f_q, "f_kv": f_kv, "f_hT": f_hT, "mx": maxima, "pt": pt, "divide": divide,
                               "g_out": g_out, "g_norm": lambda seg: norm(1, seg.b, y, y_done)})


E, F, TOPK = 8, 256, 2
CF = F // P
T = B * S
TT = T // P
ROWS = 4
CHUNK = ROWS * P
SHARED = T // CHUNK
SLOTS = (TOPK * T + E * (CHUNK - 1)) // CHUNK
ITEMS = SHARED + SLOTS
NL = SLOTS * ROWS
WCOLS = 2 * CD * F + CF * D
W_PARTS = ((0, CD * F), (CD * F, 2 * CD * F), (2 * CD * F, WCOLS))
RMS_EPS = 1e-6


def experts(nc, w_in, rms_in, router_in, tri_in, small_in, tok_in, ident_in, h3, ht, token_list, ys, out):
    with ExitStack() as octx:
        om = Memory(nc, octx)
        res = om.sb("e_res", [P, TT, D])
        place = om.sb("e_place", [P, 2, TT], mybir.dt.uint32)
        share = om.sb("e_share", [P, 2, TT])
        with ExitStack() as ctx:
            expert_items(nc, Memory(nc, ctx), res, place, share, w_in, rms_in, router_in, tri_in, small_in, tok_in,
                         ident_in, h3, ht, token_list, ys)
        with ExitStack() as ctx:
            combine(nc, Memory(nc, ctx), res, place, share, ys, out)


class Item:

    def __init__(self, n, slot, parity, n_static=None):
        self.n, self.slot, self.parity = n, slot, parity
        self.j = n - (SHARED - 1) if slot else 0
        self.wbuf = (parity + 1) % 2 if slot else 0


def item_segments(eng, h):

    def call(name, *args):
        if name in h:
            h[name](*args)

    def segment(n, parity, slot, slot_before, slot_next, first=False, last=False):
        it = Item(n, slot, parity)
        call("gu", it, 0)
        if not last:
            call("inputs", Item(n + 1, slot_next, 1 - parity))
        if not first:
            call("down", Item(n - 1, slot_before, 1 - parity))
        if not last and slot_next:
            call("weights", Item(n + 1, True, 1 - parity))
        call("gu", it, 1)

    call("weights", Item(0, False, 0))
    call("inputs", Item(0, False, 0))
    segment(0, 0, False, False, False, first=True)
    segment(1, 1, False, False, False)
    with eng.Fori(0, (SHARED - 4) // 2) as i:
        segment(i * 2 + 2, 0, False, False, False)
        segment(i * 2 + 3, 1, False, False, False)
    segment(SHARED - 2, 0, False, False, False)
    segment(SHARED - 1, 1, False, False, True)
    segment(SHARED, 0, True, False, True)
    segment(SHARED + 1, 1, True, True, True)
    pairs = (SLOTS - 2 - 2) // 2
    with eng.Fori(0, pairs) as i:
        segment(i * 2 + (SHARED + 2), 0, True, True, True)
        segment(i * 2 + (SHARED + 3), 1, True, True, True)
    for n in range(SHARED + 2 + 2 * pairs, ITEMS):
        segment(n, n % 2, True, True, True, last=n == ITEMS - 1)
    call("down", Item(ITEMS - 1, True, (ITEMS - 1) % 2))


def expert_items(nc, m, res, place, share, w_in, rms_in, router_in, tri_in, small_in, tok_in, ident_in, h3, ht,
                 token_list, ys):
    U32 = mybir.dt.uint32
    ident = m.sb("e_ident", [P, P])
    rms = m.sb("e_rms", [P, D])
    rraw = m.sb("e_rraw", [P, CD, E])
    router = [m.sb(f"e_router{p}", [P, CD, E], F32R) for p in "hl"]
    tri = m.sb("e_tri", [P, 2, P])
    small = m.sb("e_small", [P, E + SLOTS + 1])
    tok = m.sb("e_tok", [P, TT], U32)
    xin = m.sb("e_xin", [P, ROWS, D])
    ss = m.sb("e_ss", [P, ROWS])
    xT = [[m.sb(f"e_xT{p}{n}", [P, CD, CHUNK], F32R) for p in "hl"] for n in range(2)]
    aT = [[m.sb(f"e_aT{p}{n}", [P, CF, CHUNK], F32R) for p in "hl"] for n in range(2)]
    sg = [m.sb(f"e_sg{f}", [P, CHUNK]) for f in range(CF)]
    wraw = m.sb("e_wraw", [P, WCOLS])
    wb = [[m.sb(f"e_w{p}{n}", [P, WCOLS], F32R) for p in "hl"] for n in range(2)]
    yb = m.sb("e_yb", [P, ROWS, D])
    lg = m.sb("e_lg", [P, TT, E])
    top = m.sb("e_top", [P, TT, 8])
    topi = m.sb("e_topi", [P, TT, 8], U32)
    oh = m.sb("e_oh", [P, 2, TT, E])
    mm_ = m.sb("e_mm", [P, TT, E])
    cum = m.sb("e_cum", [P, E, TT])
    tot = m.sb("e_tot", [P, E, TT])
    blk = m.sb("e_blk", [P, 4, E])
    fl = m.sb("e_fl", [P, 2, TT])
    fj = m.sb("e_fj", [P, 2, TT])
    addr = m.sb("e_addr", [P, 2, TT], U32)
    own = m.sb("e_own", [1, SLOTS, E])
    ownf = m.sb("e_ownf", [1, SLOTS])
    owner = m.sb("e_owner", [1, SLOTS], I32)
    idx = m.sb("e_idx", [P, NL], U32)
    idx4 = m.sb("e_idx4", [P, ROWS], U32)
    tp = [m.ps(f"e_tp{n}", [P, D]) for n in range(2)]
    gu = [m.ps(f"e_gu{n}", [P, CHUNK]) for n in range(4)]
    dn = [m.ps(f"e_dn{n}", [P, D]) for n in range(2)]

    consts = m.sem("e_consts")
    pool_passed = m.sem("e_pool_passed")
    res_landed = [m.sem(f"e_res_landed{n}") for n in range(2)]
    ss_done = m.sem("e_ss_done")
    ms_done = m.sem("e_ms_done")
    rs_done = m.sem("e_rs_done")
    ht_done = m.sem("e_ht_done")
    ht_stored = m.sem("e_ht_stored")
    r_prep = m.sem("e_r_prep")
    c_t = m.sem("e_c_t")
    c_hi = m.sem("e_c_hi")
    c_lo = m.sem("e_c_lo")
    c_lg = m.sem("e_c_lg")
    c_lgd = m.sem("e_c_lgd")
    rt = m.sem("e_rt")
    rt_mm = m.sem("e_rt_mm")
    rt_pe = m.sem("e_rt_pe")
    rt_exp = m.sem("e_rt_exp")
    rt_done = m.sem("e_rt_done")
    zeroed = m.sem("e_zeroed")
    listed = m.sem("e_listed")
    idx_landed = m.sem("e_idx_landed")
    idx_copied = m.sem("e_idx_copied")
    x_landed = m.sem("e_x_landed")
    g_landed = m.sem("e_g_landed")
    t_ready = m.sem("e_t_ready")
    x_hi = m.sem("e_x_hi")
    x_lo = m.sem("e_x_lo")
    gu_ready = m.sem("e_gu_ready")
    silu_done = m.sem("e_silu_done")
    mul_done = m.sem("e_mul_done")
    a_hi = m.sem("e_a_hi")
    a_lo = m.sem("e_a_lo")
    d_ready = m.sem("e_d_ready")
    d_used = m.sem("e_d_used")
    y_stored = m.sem("e_y_stored")
    raw_landed = m.sem("e_raw_landed")
    w_hi = m.sem("e_w_hi")
    w_lo = m.sem("e_w_lo")
    block = m.ctx.enter_context(nc.Block())

    def gate(w, c, f):
        return w[:, c * F + f * P:c * F + f * P + P]

    def up(w, c, f):
        return w[:, CD * F + c * F + f * P:CD * F + c * F + f * P + P]

    def down_w(w, f):
        return w[:, 2 * CD * F + f * D:2 * CD * F + (f + 1) * D]

    @block.sync
    def _(sp):
        sp.sem_inc(ht_stored, 1)
        for dst, src in ((ident[:, :], ident_in), (rms[:, :], rms_in), (rraw[:, :, :], router_in),
                         (tri[:, :, :], tri_in), (small[:, :], small_in), (tok[:, :], tok_in)):
            sp.dma_start(dst, src).then_inc(consts, 16)
        h3_v = h3.rearrange("b (t p) d -> p (b t) d", p=P)
        ht_v = ht.rearrange("(t p) d -> p t d", p=P)

        def load_res(k, par):
            sp.dma_start(res[:, bass.ds(k * ROWS, ROWS), :], h3_v[:, bass.ds(k * ROWS, ROWS), :])\
              .then_inc(res_landed[par], 16)

        def store_ht(k):
            sp.wait_ge(ht_done, k + 2)
            sp.dma_start(ht_v[:, bass.ds(k * ROWS, ROWS), :], xin[:, :, :]).then_inc(ht_stored, 16)

        load_res(0, 0)
        load_res(1, 1)
        sp.dma_start(wraw[:, :], w_in[E]).then_inc(raw_landed, 16)
        with sp.Fori(0, SHARED // 2 - 1) as i:
            for par in range(2):
                sp.wait_ge(ss_done, i * 2 + (par + 1))
                load_res(i * 2 + (par + 2), par)
                store_ht(i * 2 + par)
        store_ht(SHARED - 2)
        store_ht(SHARED - 1)
        sp.wait_ge(ht_stored, 16 * SHARED + 1)

        def load_x(n):
            sp.dma_start(xin[:, :, :], ht_v[:, bass.ds(n * ROWS, ROWS), :]).then_inc(x_landed, 16)

        sp.wait_ge(c_t, 4 * SHARED + 2)
        load_x(0)

        def load_w(j, s):
            sp.wait_ge(w_lo, j * 3)
            e = sp.value_load(owner[0:1, bass.ds(s, 1)], min_val=0, max_val=E - 1)
            sp.dma_start(wraw[:, :], w_in[bass.ds(e, 1)].rearrange("o p n -> (o p) n")).then_inc(raw_landed, 16)

        def after_inputs(it):
            if not it.slot and not (isinstance(it.n, int) and it.n >= SHARED - 1):
                sp.wait_ge(t_ready, it.n * 4 + 4)
                load_x(it.n + 1)

        def after_down(it):
            if it.slot:
                sp.wait_ge(d_used, it.n * 4 + 6)
                s = it.n - SHARED
                sp.dma_start(ys[bass.ds(s, 1)].rearrange("o p r d -> (o p) r d"), yb[:, :, :]).then_inc(y_stored, 16)

        def after_weights(it):
            if isinstance(it.n, int) and (it.n == 0 or it.n == ITEMS - 1):
                if it.n == 0:
                    sp.wait_ge(rt_done, 1)
                    load_w(1, 0)
                return
            load_w(it.j + 1, it.n + 1 - SHARED)

        item_segments(sp, {"inputs": after_inputs, "down": after_down, "weights": after_weights})
        sp.wait_ge(y_stored, 16 * SLOTS)

    @block.tensor
    def _(pe):
        pe.sem_inc(c_t, 2)
        pe.wait_ge(consts, 96)
        pe.wait_ge(r_prep, 2)
        with pe.Fori(0, SHARED // 2) as i:
            for par in range(2):
                k = i * 2 + par
                pe.wait_ge(ht_done, k + 2)
                for t in range(ROWS):
                    pe.wait_ge(c_lo, k * ROWS + t + 1)
                    for c in range(CD):
                        mm = pe.transpose(tp[t % 2][:, c * P:(c + 1) * P], xin[:, t, c * P:(c + 1) * P], ident[:, :])
                    mm.then_inc(c_t, 1)
                pe.wait_ge(c_lo, k * ROWS + (ROWS + 2))
                pe.wait_ge(c_lgd, k + 1)
                for t in range(ROWS):
                    for c in range(CD):
                        mm = mm3(pe, dn[0][:, t * E:(t + 1) * E], [x[:, c, t * P:(t + 1) * P] for x in xT[par]],
                                 [x[:, c, :] for x in router], c == 0, c == CD - 1)
                mm.then_inc(c_lg, 1)
        pe.wait_ge(rt_mm, 1)
        flat = mm_[:, :, :].rearrange("p t e -> p (t e)")
        pe.matmul(dn[0][:, 0:TT * E], tri[:, 0, :], flat, start=True, stop=True)
        pe.matmul(dn[1][:, 0:TT * E], tri[:, 1, :], flat, start=True, stop=True).then_inc(rt_pe, 1)

        def inputs(it):
            if it.slot:
                pe.wait_ge(g_landed, it.n * (16 * ROWS) - (SHARED - 1) * (16 * ROWS))
            else:
                pe.wait_ge(x_landed, it.n * 16 + 16)
            for t in range(ROWS):
                pe.wait_ge(x_lo, it.n * 4 + (t + 1))
                for c in range(CD):
                    mm = pe.transpose(tp[t % 2][:, c * P:(c + 1) * P], xin[:, t, c * P:(c + 1) * P], ident[:, :])
                mm.then_inc(t_ready, 1)

        def gate_up(it, f):
            if f == 0:
                pe.wait_ge(x_lo, it.n * 4 + 6)
                pe.wait_ge(w_lo, it.j * 3 + 2)
            pe.wait_ge(mul_done, it.n * 2 + (f + 1))
            x, w = xT[it.parity], wb[it.wbuf]
            for k, part in enumerate((gate, up)):
                for c in range(CD):
                    mm = mm3(pe, gu[2 * f + k][:, :], [part(y, c, f) for y in w], [y[:, c, :] for y in x], c == 0,
                             c == CD - 1)
                mm.then_inc(gu_ready, 1)

        def down(it):
            pe.wait_ge(a_lo, it.n * 2 + 2)
            pe.wait_ge(w_lo, it.j * 3 + 3)
            a, w = aT[it.parity], wb[it.wbuf]
            for t in range(ROWS):
                pe.wait_ge(d_used, it.n * 4 + (t + 1))
                for f in range(CF):
                    mm = mm3(pe, dn[t % 2][:, :], [y[:, f, t * P:(t + 1) * P] for y in a], [down_w(y, f) for y in w],
                             f == 0, f == CF - 1)
                mm.then_inc(d_ready, 1)

        pe.wait_ge(rt_done, 1)
        item_segments(pe, {"inputs": inputs, "gu": gate_up, "down": down})

    @block.scalar
    def _(act):
        act.wait_ge(consts, 96)
        act.activation(router[0][:, :, :], rraw[:, :, :], ACT.Copy).then_inc(r_prep, 1)
        with act.Fori(0, SHARED // 2) as i:
            for par in range(2):
                k = i * 2 + par
                act.wait_ge(res_landed[par], i * 16 + 16)
                act.wait_ge(ht_done, k + 1)
                for t in range(ROWS):
                    ins = act.activation(yb[:, t, :], res[:, bass.ds(k * ROWS + t, 1), :].rearrange(
                        "p o d -> p (o d)"), ACT.Square, accum_out=ss[:, t:t + 1])
                ins.then_inc(ss_done, 1)
                for t in range(ROWS):
                    act.wait_ge(c_t, k * ROWS + (t + 3))
                    act.activation(xT[par][0][:, :, t * P:(t + 1) * P],
                                   tp[t % 2][:, :].rearrange("p (c s) -> p c s", c=CD), ACT.Copy).then_inc(c_hi, 1)
        act.wait_ge(rt, 2)
        act.activation(share[:, 1, :], fl[:, 0, :], ACT.Exp).then_inc(rt_exp, 1)

        def inputs(it):
            for t in range(ROWS):
                act.wait_ge(t_ready, it.n * 4 + (t + 1))
                if t == 0 and not (isinstance(it.n, int) and it.n < 1):
                    act.wait_ge(gu_ready, it.n * 4 - 4)
                act.activation(xT[it.parity][0][:, :, t * P:(t + 1) * P],
                               tp[t % 2][:, :].rearrange("p (c s) -> p c s", c=CD), ACT.Copy).then_inc(x_hi, 1)

        def gate_up(it, f):
            act.wait_ge(gu_ready, it.n * 4 + (2 * f + 1))
            if not (isinstance(it.n, int) and it.n < 1):
                act.wait_ge(a_lo, it.n * 2 + (f - 1))
            act.activation(sg[f][:, :], gu[2 * f][:, :], ACT.Silu).then_inc(silu_done, 1)
            act.wait_ge(mul_done, it.n * 2 + (f + 3))
            if f == 0 and not (isinstance(it.n, int) and it.n < 1):
                act.wait_ge(d_ready, it.n * 4 - 4)
            act.activation(aT[it.parity][0][:, f, :], sg[f][:, :], ACT.Copy).then_inc(a_hi, 1)

        def weights(it):
            act.wait_ge(raw_landed, it.j * 16 + 16)
            if it.slot:
                act.wait_ge(d_ready, it.n * 4 - 4)
            for a, b in W_PARTS:
                act.activation(wb[it.wbuf][0][:, a:b], wraw[:, a:b], ACT.Copy).then_inc(w_hi, 1)

        item_segments(act, {"inputs": inputs, "gu": gate_up, "weights": weights})

    @block.gpsimd
    def _(pool):
        pool.wait_ge(consts, 96)
        pool.memset(idx[:, :], 0)  .then_inc(zeroed, 1)
        pool.wait_ge(zeroed, 1)
        list_v = token_list.rearrange("(p n) o -> p (n o)", p=P)
        pool.dma_start(list_v, idx[:, :]).then_inc(listed, 16)
        nh = small[:, E + SLOTS:E + SLOTS + 1].broadcast_to([P, ROWS])
        with pool.Fori(0, SHARED) as k:
            pool.wait_ge(ss_done, k + 1)
            pool.wait_ge(ht_done, k + 1)
            carry_wait(pool, pool_passed)
            pool.tensor_scalar(ss[:, :], ss[:, :], 1.0 / D, RMS_EPS, ALU.mult, ALU.add).then_inc(ms_done, 1)
            pool.wait_ge(ms_done, k + 1)
            pool.tensor_tensor(ss[:, :], ss[:, :], nh, ALU.pow).then_inc(rs_done, 1)
        pool.wait_ge(rt_done, 1)
        pool.wait_ge(listed, 16)
        for t in range(TT):
            for k in range(2):
                pool.indirect_dma_start(token_list, bass.IndirectOffsetOnAxis(addr[:, k, t:t + 1], 0),
                                        tok[:, t:t + 1], None).then_inc(listed, 16)
        pool.wait_ge(listed, 16 + 16 * 2 * TT)
        pool.dma_start(idx[:, :], list_v).then_inc(idx_landed, 16)
        pool.wait_ge(idx_landed, 16)

        def gather(n):
            s = n - SHARED
            pool.tensor_copy(idx4[:, :], idx[:, bass.ds(s * ROWS, ROWS)]).then_inc(idx_copied, 1)
            pool.wait_ge(idx_copied, s + 1)
            carry_wait(pool, pool_passed)
            for r in range(ROWS):
                pool.indirect_dma_start(xin[:, r, :], None, ht, bass.IndirectOffsetOnAxis(idx4[:, r:r + 1], 0))\
                    .then_inc(g_landed, 16)

        def after_inputs(it):
            if isinstance(it.n, int) and (it.n < SHARED - 1 or it.n == ITEMS - 1) or not it.slot and not isinstance(
                    it.n, int):
                return
            pool.wait_ge(t_ready, it.n * 4 + 4)
            gather(it.n + 1)

        item_segments(pool, {"inputs": after_inputs})

    @block.vector
    def _(dve):
        dve.sem_inc(c_lo, 2)
        dve.sem_inc(c_lgd, 1)
        dve.sem_inc(ht_done, 1)
        dve.sem_inc(x_lo, 2)
        dve.sem_inc(mul_done, 2)
        dve.sem_inc(d_used, 2)
        dve.wait_ge(consts, 96)
        dve.wait_ge(r_prep, 1)
        dve.tensor_tensor(router[1][:, :, :], rraw[:, :, :], router[0][:, :, :].bitcast(F32), ALU.subtract)\
           .then_inc(r_prep, 1)
        with dve.Fori(0, SHARED // 2) as i:
            for par in range(2):
                k = i * 2 + par
                dve.wait_ge(rs_done, k + 1)
                dve.wait_ge(c_t, k * ROWS + 2)
                dve.wait_ge(ht_stored, k * 16 + 1)
                for t in range(ROWS):
                    ins = dve.scalar_tensor_tensor(xin[:, t, :], res[:, bass.ds(k * ROWS + t, 1), :].rearrange(
                        "p o d -> p (o d)"), ss[:, t:t + 1], rms[:, :], ALU.mult, ALU.mult)
                ins.then_inc(ht_done, 1)
                for t in range(ROWS):
                    sl = slice(t * P, (t + 1) * P)
                    dve.wait_ge(c_hi, k * ROWS + (t + 1))
                    dve.tensor_tensor(xT[par][1][:, :, sl], tp[t % 2][:, :].rearrange("p (c s) -> p c s", c=CD),
                                      xT[par][0][:, :, sl].bitcast(F32), ALU.subtract).then_inc(c_lo, 1)
                dve.wait_ge(c_lg, k + 1)
                dve.tensor_copy(lg[:, bass.ds(k * ROWS, ROWS), :],
                                dn[0][:, 0:ROWS * E].rearrange("p (t e) -> p t e", e=E)).then_inc(c_lgd, 1)
        dve.wait_ge(c_lgd, SHARED + 1)
        for t in range(TT):
            ins = dve.max(top[:, t, :], lg[:, t, :])
        c = Chain(dve, rt)
        c(ins)
        for t in range(TT):
            dve.max_index(topi[:, t, :], top[:, t, :], lg[:, t, :])
        c(dve.tensor_tensor(fl[:, 0, :], top[:, :, 1], top[:, :, 0], ALU.subtract))
        iota = small[:, 0:E].unsqueeze(1).broadcast_to([P, TT, E])
        for k in range(2):
            ins = dve.tensor_copy(fj[:, k, :], topi[:, :, k])
        c(ins)
        for k in range(2):
            ins = dve.tensor_tensor(oh[:, k, :, :], fj[:, k, :].unsqueeze(2).broadcast_to([P, TT, E]), iota,
                                    ALU.is_equal)
        c(ins)
        dve.tensor_tensor(mm_[:, :, :], oh[:, 0, :, :], oh[:, 1, :, :], ALU.add).then_inc(rt_mm, 1)
        dve.wait_ge(rt_exp, 1)
        c(dve.tensor_scalar(share[:, 0, :], share[:, 1, :], 1.0, None, ALU.add))
        c(dve.reciprocal(share[:, 0, :], share[:, 0, :]))
        c(dve.tensor_tensor(share[:, 1, :], share[:, 1, :], share[:, 0, :], ALU.mult))
        dve.wait_ge(rt_pe, 1)
        c(dve.tensor_copy(tot[:, :, :], dn[1][:, 0:TT * E].rearrange("p (t e) -> p e t", e=E)))
        for e in range(E):
            ins = dve.tensor_tensor_scan(cum[:, e, :], tri[:, 1, 0:TT], tot[:, e, :], 0.0, ALU.mult, ALU.add)
        c(ins)
        c(dve.tensor_copy(blk[:, 0, :], cum[:, :, TT - 1]))
        c(dve.tensor_tensor(cum[:, :, :], cum[:, :, :], tot[:, :, :], ALU.subtract))
        c(dve.tensor_scalar(blk[:, 1, :], blk[:, 0, :], 1.0 / CHUNK, (CHUNK - 1.0) / (2 * CHUNK), ALU.mult, ALU.add))
        c(dve.tensor_scalar(blk[:, 1, :], blk[:, 1, :], ROUND, None, ALU.add))
        c(dve.tensor_scalar(blk[:, 1, :], blk[:, 1, :], ROUND, None, ALU.subtract))
        c(dve.tensor_tensor_scan(blk[:, 2, :], tri[:, 1, 0:E], blk[:, 1, :], 0.0, ALU.mult, ALU.add))
        c(dve.tensor_tensor(blk[:, 3, :], blk[:, 2, :], blk[:, 1, :], ALU.subtract))
        c(dve.tensor_scalar(blk[:, 3, :], blk[:, 3, :], float(CHUNK), None, ALU.mult))
        pos = lg
        c(dve.tensor_tensor(pos[:, :, :], dn[0][:, 0:TT * E].rearrange("p (t e) -> p t e", e=E),
                            cum[:, :, :].rearrange("p e t -> p t e"), ALU.add))
        c(dve.tensor_tensor(pos[:, :, :], pos[:, :, :], blk[:, 3, :].unsqueeze(1).broadcast_to([P, TT, E]), ALU.add))
        for k in range(2):
            ins = dve.tensor_tensor(oh[:, k, :, :], oh[:, k, :, :], pos[:, :, :], ALU.mult)
        c(ins)
        c(dve.tensor_reduce(fl[:, :, :], oh[:, :, :, :], AX_X, ALU.add))
        c(dve.tensor_scalar(fj[:, :, :], fl[:, :, :], 1.0 / P, -(P - 1.0) / (2 * P), ALU.mult, ALU.add))
        c(dve.tensor_scalar(fj[:, :, :], fj[:, :, :], ROUND, None, ALU.add))
        c(dve.tensor_scalar(fj[:, :, :], fj[:, :, :], ROUND, None, ALU.subtract))
        fk = tot[:, 0:2, :]
        c(dve.scalar_tensor_tensor(fk, fj[:, :, :], -float(P), fl[:, :, :], ALU.mult, ALU.add))
        c(dve.scalar_tensor_tensor(addr[:, :, :], fk, float(NL), fj[:, :, :], ALU.mult, ALU.add))
        fs = tot[:, 2:4, :]
        c(dve.tensor_scalar(fs, fj[:, :, :], 1.0 / ROWS, -(ROWS - 1.0) / (2 * ROWS), ALU.mult, ALU.add))
        c(dve.tensor_scalar(fs, fs, ROUND, None, ALU.add))
        c(dve.tensor_scalar(fs, fs, ROUND, None, ALU.subtract))
        c(dve.scalar_tensor_tensor(fj[:, :, :], fs, float(P * ROWS - ROWS), fj[:, :, :], ALU.mult, ALU.add))
        c(dve.scalar_tensor_tensor(place[:, :, :], fk, float(ROWS), fj[:, :, :], ALU.mult, ALU.add))
        sl = small[0:1, E:E + SLOTS].unsqueeze(2).broadcast_to([1, SLOTS, E])
        c(dve.tensor_tensor(own[:, :, :], blk[0:1, 2, :].unsqueeze(1).broadcast_to([1, SLOTS, E]), sl, ALU.is_le))
        c(dve.tensor_reduce(ownf[:, :], own[:, :, :], AX_X, ALU.add))
        dve.tensor_scalar(owner[:, :], ownf[:, :], E - 1.0, None, ALU.min).then_inc(rt_done, 1)

        def inputs(it):
            for t in range(ROWS):
                sl = slice(t * P, (t + 1) * P)
                dve.wait_ge(x_hi, it.n * 4 + (t + 1))
                x = xT[it.parity]
                dve.tensor_tensor(x[1][:, :, sl], tp[t % 2][:, :].rearrange("p (c s) -> p c s", c=CD),
                                  x[0][:, :, sl].bitcast(F32), ALU.subtract).then_inc(x_lo, 1)

        def gate_up(it, f):
            dve.wait_ge(silu_done, it.n * 2 + (f + 1))
            dve.wait_ge(gu_ready, it.n * 4 + (2 * f + 2))
            dve.tensor_tensor(sg[f][:, :], sg[f][:, :], gu[2 * f + 1][:, :], ALU.mult).then_inc(mul_done, 1)
            dve.wait_ge(a_hi, it.n * 2 + (f + 1))
            a = aT[it.parity]
            dve.tensor_tensor(a[1][:, f, :], sg[f][:, :], a[0][:, f, :].bitcast(F32), ALU.subtract).then_inc(a_lo, 1)

        def down(it):
            if it.slot:
                dve.wait_ge(y_stored, it.n * 16 - 16 * SHARED)
            for t in range(ROWS):
                dve.wait_ge(d_ready, it.n * 4 + (t + 1))
                if it.slot:
                    dve.tensor_copy(yb[:, t, :], dn[t % 2][:, :]).then_inc(d_used, 1)
                else:
                    r = res[:, bass.ds(it.n * ROWS + t, 1), :].rearrange("p o d -> p (o d)")
                    dve.tensor_tensor(r, r, dn[t % 2][:, :], ALU.add).then_inc(d_used, 1)

        def weights(it):
            for k, (a, b) in enumerate(W_PARTS):
                dve.wait_ge(w_hi, it.j * 3 + (k + 1))
                w = wb[it.wbuf]
                dve.tensor_tensor(w[1][:, a:b], wraw[:, a:b], w[0][:, a:b].bitcast(F32), ALU.subtract)\
                   .then_inc(w_lo, 1)

        item_segments(dve, {"inputs": inputs, "gu": gate_up, "down": down, "weights": weights})


def combine(nc, m, res, place, share, ys, out):
    NB = 4
    g = [[m.sb(f"f_g{k}{n}", [P, D]) for k in range(2)] for n in range(NB)]
    pl = [m.sb(f"f_pl{n}", [P, 2], mybir.dt.uint32) for n in range(NB)]
    st = m.sb("f_st", [P, NB, 6])
    mv = m.sb("f_mv", [P, NB, 2])
    nhalf = m.sb("f_nhalf", [P, 1])
    nmr = m.sb("f_nmr", [P, NB])
    o = [m.sb(f"f_o{n}", [P, D]) for n in range(NB)]
    copied = m.sem("f_copied")
    dve_passed = m.sem("f_dve_passed")
    pool_passed = m.sem("f_pool_passed")
    landed = [m.sem(f"f_landed{n}") for n in range(NB)]
    chain = m.sem("f_chain")
    var = m.sem("f_var")
    rstd = m.sem("f_rstd")
    shift = m.sem("f_shift")
    normed = m.sem("f_normed")
    stored = [m.sem(f"f_stored{n}") for n in range(NB)]
    rows = ys.rearrange("s p r d -> (s p r) d")
    out_v = out.rearrange("b (t p) d -> p (b t) d", p=P)
    block = m.ctx.enter_context(nc.Block())

    def tiles(eng, body):
        with eng.Fori(0, TT // NB - 1) as i:
            for b in range(NB):
                body(i * NB + b, b, i, True)
        for b in range(NB):
            body(TT - NB + b, b, TT // NB - 1, False)

    @block.gpsimd
    def _(pool):
        pool.memset(nhalf[:, :], -0.5).then_inc(copied, 1)
        pool.wait_ge(copied, 1)

        def gather(t, b):
            pool.tensor_copy(pl[b][:, :], place[:, :, bass.ds(t, 1)].rearrange("p k o -> p (k o)")).then_inc(copied, 1)
            pool.wait_ge(copied, t + 2)
            carry_wait(pool, pool_passed)
            for k in range(2):
                pool.indirect_dma_start(g[b][k][:, :], None, rows, bass.IndirectOffsetOnAxis(pl[b][:, k:k + 1], 0))\
                    .then_inc(landed[b], 16)

        def body(t, b, i, more):
            pool.wait_ge(var, t + 1)
            pool.tensor_tensor(mv[:, b, 1:2], mv[:, b, 1:2], nhalf[:, :], ALU.pow).then_inc(rstd, 1)
            pool.wait_ge(rstd, t + 1)
            carry_wait(pool, pool_passed)
            pool.tensor_scalar(nmr[:, b:b + 1], mv[:, b, 0:1], -1.0, mv[:, b, 1:2], ALU.mult, ALU.mult)\
                .then_inc(shift, 1)
            if more:
                gather(t + NB, b)

        for b in range(NB):
            gather(b, b)
        tiles(pool, body)

    @block.vector
    def _(dve):
        def body(t, b, i, more):
            c = Chain(dve, chain, t * 4)
            dve.wait_ge(landed[b], i * 32 + 32)
            c(dve.scalar_tensor_tensor(g[b][0][:, :], g[b][0][:, :], share[:, 0, bass.ds(t, 1)],
                                       res[:, bass.ds(t, 1), :].rearrange("p o d -> p (o d)"), ALU.mult, ALU.add))
            dve.wait_ge(stored[b], i * 16 + 1)
            c(dve.scalar_tensor_tensor(o[b][:, :], g[b][1][:, :], share[:, 1, bass.ds(t, 1)], g[b][0][:, :],
                                       ALU.mult, ALU.add))
            c(dve.bn_stats(st[:, b, :], o[b][:, :]))
            carry_wait(dve, dve_passed)
            c(dve.bn_aggr(mv[:, b, :], st[:, b, :]))
            dve.tensor_scalar(mv[:, b, 1:2], mv[:, b, 1:2], LN_EPS, None, ALU.add).then_inc(var, 1)

        tiles(dve, body)

    @block.scalar
    def _(act):
        def body(t, b, i, more):
            act.wait_ge(shift, t + 1)
            act.activation(o[b][:, :], o[b][:, :], ACT.Identity, bias=nmr[:, b:b + 1], scale=mv[:, b, 1:2])\
               .then_inc(normed, 1)

        tiles(act, body)

    @block.sync
    def _(sp):
        for b in range(NB):
            sp.sem_inc(stored[b], 1)

        def body(t, b, i, more):
            sp.wait_ge(normed, t + 1)
            sp.dma_start(out_v[:, bass.ds(t, 1), :].rearrange("p o d -> p (o d)"), o[b][:, :]).then_inc(stored[b], 16)

        tiles(sp, body)
        for b in range(NB):
            sp.wait_ge(stored[b], 16 * (TT // NB) + 1)


def host_tok(x, log_dt, log_w_real, w_imag):
    import numpy as np
    dyn = np.stack([np.broadcast_to(log_dt[None, :], (NST, S)), log_w_real.T, w_imag.T], 1)
    dyn = np.ascontiguousarray(np.concatenate([dyn, dyn], 0))
    c = x.transpose(2, 1, 3, 0)
    c = np.ascontiguousarray(np.concatenate([c, c], 0))
    return dyn, c


def host_experts(w_gate, w_up, w_down, sw_gate, sw_up, sw_down):
    import numpy as np
    one = lambda a, b, c: np.concatenate([rows_on_partitions(a), rows_on_partitions(b), rows_on_partitions(c)], 1)
    parts = [one(w_gate[e], w_up[e], w_down[e]) for e in range(E)] + [one(sw_gate, sw_up, sw_down)]
    return np.ascontiguousarray(np.stack(parts))


def constants():
    import numpy as np
    mult = np.broadcast_to(np.arange(NM1, dtype=np.float32) * np.array([[1], [NM1], [NM]], np.float32), (P, 3, NM1))
    half = np.zeros((P, 8), np.float32)
    half[:64, 0], half[64:, 0] = -1, 1
    half[:64, 1], half[64:, 1] = 1, -1
    half[:64, 2] = PI / 2
    half[64:, 3] = PI / 2
    half[:, 6] = PI / 2
    inv_freq = 1.0 / 10000.0 ** (np.arange(0, HD, 2, dtype=np.float32) / np.float32(HD))
    ang = np.outer(np.arange(S, dtype=np.float32), inv_freq.astype(np.float32)).astype(np.float32)
    c, sn = np.cos(ang).T.astype(np.float32), np.sin(ang).T.astype(np.float32)
    rope0 = np.stack([np.concatenate([c, c], 0), np.concatenate([-sn, sn], 0)], 1)
    mask = np.zeros((P, 2 * P), np.float32)
    mask[:, P:] = np.triu(np.full((P, P), NEG, np.float32), 1)
    inv1 = (1.0 / 1000000.0 ** (np.arange(HD1 // 2, dtype=np.float32) / np.float32(HD1 // 2))).astype(np.float32)
    ang = np.outer(np.arange(S, dtype=np.float32), inv1).astype(np.float32)
    c, sn = np.cos(ang).astype(np.float32), np.sin(ang).astype(np.float32)
    rope1 = np.stack([np.concatenate([c, c], 1), np.concatenate([-sn, sn], 1)], 0)
    rope1 = np.ascontiguousarray(rope1.reshape(2, ST, P, HD1).transpose(2, 0, 1, 3))
    tri = np.stack([np.triu(np.ones((P, P), np.float32), 1), np.ones((P, P), np.float32)], 1)
    small = np.concatenate([np.arange(E), np.arange(SLOTS), [-0.5]]).astype(np.float32)
    tok = (np.arange(TT)[None, :] * P + np.arange(P)[:, None]).astype(np.uint32)
    return {"tri": np.ascontiguousarray(tri), "small": np.tile(small, (P, 1)), "tok": tok, "rope1": rope1, "identb": np.eye(P).astype(mybir.dt.np(BF16)), "mult": np.ascontiguousarray(mult), "half": half, "rope0": np.ascontiguousarray(rope0), "mask": mask,
            "ident": np.eye(P, dtype=np.float32)}


def rows_on_partitions(w):
    import numpy as np
    n = w.shape[1]
    return np.ascontiguousarray(w.reshape(-1, P, n).transpose(1, 0, 2).reshape(P, -1))


IN_NAMES = ["dyn", "coef", "mult", "half", "wq0", "wk0", "wv0", "wo0", "rope0", "mask", "ident", "fw", "fb", "wq1",
            "wkv1", "wo1", "bias1", "rope1", "identb", "wexp", "rms", "router", "tri", "small", "tok"]


def program(nc, a, out):
    def scratch(name, shape, dt=F32):
        return nc.dram_tensor(name, shape, dt, kind="Internal").ap()

    h0 = scratch("h0", (P, S, NM))
    h1 = scratch("h1", (B, S, D))
    h3 = scratch("h3", (B, S, D))
    ht = scratch("ht", (T, D))
    token_list = scratch("token_list", (P * NL, 1), mybir.dt.uint32)
    ys = scratch("ys", (SLOTS, P, ROWS, D))
    token_mixer(nc, a["dyn"], a["coef"], a["mult"], a["half"], h0)
    attention0(nc, a["wq0"], a["wk0"], a["wv0"], a["wo0"], a["rope0"], a["mask"], a["ident"], h0, h1)
    block01(nc, a["fw"], a["fb"], a["wq1"], a["wkv1"], a["wo1"], a["bias1"], a["rope1"], a["mask"], a["ident"],
            a["identb"], h1, h3)
    experts(nc, a["wexp"], a["rms"], a["router"], a["tri"], a["small"], a["tok"], a["ident"], h3, ht, token_list, ys,
            out)


def kernel(x, L0_tok_log_dt, L0_tok_log_w_real, L0_tok_w_imag, L0_attn_w_q, L0_attn_w_k, L0_attn_w_v, L0_attn_w_o,
           L0_ffn_weight, L0_ffn_bias, L1_attn_Wq, L1_attn_bq, L1_attn_Wk, L1_attn_bk, L1_attn_Wv, L1_attn_bv,
           L1_attn_Wo, L1_ffn_rms_weight, L1_ffn_router_w, L1_ffn_w_gate, L1_ffn_w_up, L1_ffn_w_down,
           L1_ffn_sw_gate, L1_ffn_sw_up, L1_ffn_sw_down):
    import numpy as np
    import concourse.bacc as bacc
    from concourse.bass_utils import run_bass_kernel_spmd

    arrays = constants()
    arrays["dyn"], arrays["coef"] = host_tok(np.asarray(x), np.asarray(L0_tok_log_dt), np.asarray(L0_tok_log_w_real),
                                             np.asarray(L0_tok_w_imag))
    rows = lambda w: rows_on_partitions(np.asarray(w))
    for name, w in (("wq0", L0_attn_w_q), ("wk0", L0_attn_w_k), ("wv0", L0_attn_w_v), ("wo0", L0_attn_w_o)):
        arrays[name] = rows(w)
    arrays["fw"] = rows(np.asarray(L0_ffn_weight).T)
    arrays["fb"] = np.tile(np.asarray(L0_ffn_bias), (P, 1))
    arrays["wq1"] = rows(L1_attn_Wq).reshape(P, CD, D)
    arrays["wkv1"] = rows(np.concatenate([np.asarray(L1_attn_Wk), np.asarray(L1_attn_Wv)], 1)).reshape(P, CD, 2 * P)
    arrays["wo1"] = rows(L1_attn_Wo).reshape(P, CD, D)
    arrays["bias1"] = np.concatenate([np.asarray(L1_attn_bq), np.asarray(L1_attn_bk), np.asarray(L1_attn_bv)])[None]
    arrays["wexp"] = host_experts(*[np.asarray(w) for w in (L1_ffn_w_gate, L1_ffn_w_up, L1_ffn_w_down, L1_ffn_sw_gate,
                                                            L1_ffn_sw_up, L1_ffn_sw_down)])
    arrays["rms"] = np.tile(np.asarray(L1_ffn_rms_weight), (P, 1))
    arrays["router"] = rows(L1_ffn_router_w).reshape(P, CD, E)

    nc = bacc.Bacc("TRN2", target_bir_lowering=False, num_devices=1)
    in_map, aps = {}, {}
    for name in IN_NAMES:
        a = np.ascontiguousarray(arrays[name])
        in_map[f"in_{name}"] = a
        aps[name] = nc.dram_tensor(f"in_{name}", a.shape, mybir.dt.from_np(a.dtype), kind="ExternalInput").ap()
    out = nc.dram_tensor("out", (B, S, D), F32, kind="ExternalOutput").ap()
    program(nc, aps, out)
    return run_bass_kernel_spmd(nc, [in_map], core_ids=[0]).results[0]["out"]
```

```python
from contextlib import ExitStack

import concourse.bass as bass
from concourse import mybir

ALU = mybir.AluOpType
ACT = mybir.ActivationFunctionType
AX_X = mybir.AxisListType.X
F32 = mybir.dt.float32
F32R = mybir.dt.float32r
BF16 = mybir.dt.bfloat16
I32 = mybir.dt.int32

P = 128
B, S, D = 16, 256, 512
NST = 64
CD = D // P
ST = S // P
ROUND = 12582912.0
PI = 3.141592653589793
LN_EPS = 1e-5


class Memory:

    def __init__(self, nc, ctx):
        self.nc, self.ctx = nc, ctx

    def sb(self, name, shape, dt=F32):
        return self.ctx.enter_context(self.nc.sbuf_tensor(name, shape, dt))

    def ps(self, name, shape, dt=F32):
        return self.ctx.enter_context(self.nc.psum_tensor(name, shape, dt))

    def sem(self, name):
        return self.ctx.enter_context(self.nc.semaphore(name))


class Chain:

    def __init__(self, eng, sem, base=0):
        self.eng, self.sem, self.base, self.n = eng, sem, base, 0

    def __call__(self, ins):
        self.n += 1
        ins.then_inc(self.sem, 1)
        self.eng.wait_ge(self.sem, self.base + self.n)


def carry_wait(eng, passed):
    eng.sem_inc(passed, 1)


HC = 8
HS = 2 * HC
STEPS = S // HS
NA, NM = 8, 64
NM1 = 8
TWO_PI_1 = 6.28125
TWO_PI_2 = 0.0019350051879882812
TWO_PI_3 = 3.0199161274e-07
LN2_1 = 0.693359375
LN2_2 = -2.12194440e-4


def all_steps(eng, step):
    with eng.Fori(0, STEPS // 2 - 1) as i:
        step(i * 2, 0, False, i)
        step(i * 2 + 1, 1, False, i)
    step(STEPS - 2, 0, False, STEPS // 2 - 1)
    step(STEPS - 1, 1, True, STEPS // 2 - 1)


def token_mixer(nc, dyn_in, c_in, mult_in, half_in, h0, weights):
    tiles = weight_tiles(weights, 1024)
    with ExitStack() as ctx:
        m = Memory(nc, ctx)
        dyn = m.sb("dyn", [P, 3, S])
        mult = m.sb("mult", [P, 3, NM1])
        half = m.sb("half", [P, 8])
        ex = m.sb("ex", [P, 2, S])
        ek = m.sb("ek", [P, 2, S])
        ep = m.sb("ep", [P, 2, S])
        ei = m.sb("ei", [P, 2, S], I32)
        wr = m.sb("wr", [P, S])
        al = m.sb("al", [P, S])
        th = m.sb("th", [P, S])
        g = [m.sb(f"g{n}", [P, S]) for n in range(7)]
        qq = m.sb("qq", [P, 3, S])
        craw = [m.sb(f"craw{n}", [P, HS, 2, B]) for n in range(2)]
        cm = [m.sb(f"cm{n}", [P, 2, HS, B]) for n in range(2)]
        cm2 = m.sb("cm2", [P, 2, HS, B])
        ang = m.sb("ang", [P, 3, HS, NM1])
        turn = m.sb("turn", [P, 3, HS, NM1])
        ra = m.sb("ra", [P, 3, HS, NM1])
        rb = m.sb("rb", [P, 3, HS, NM1])
        mag = [m.sb(f"mag{n}", [P, 3, HS, NM1]) for n in range(2)]
        tr = [m.sb(f"tr{n}", [P, 2, 3, HS, NM1]) for n in range(2)]
        vv = [m.sb(f"vv{n}", [P, HC, NM]) for n in range(2)]
        v2 = m.sb("v2", [P, HC, NM])
        s1 = [m.sb(f"s1{n}", [P, HC, NA, B]) for n in range(2)]
        s2 = [m.sb(f"s2{n}", [P, HC, NA, B]) for n in range(2)]
        kout = m.sb("kout", [P, HS, NM])
        kps = [m.ps(f"kps{n}", [P, HC, NM]) for n in range(2)]

        W_BUFS = 4
        wraw = [m.sb(f"t_wraw{n}", [P, 1024]) for n in range(W_BUFS)]

        ld = m.sem("ld")
        w_landed = [m.sem(f"t_w_landed{n}") for n in range(W_BUFS)]
        w_hi = m.sem("t_w_hi")
        w_lo = m.sem("t_w_lo")
        c_landed = [m.sem(f"c_landed{n}") for n in range(2)]
        mag_ready = m.sem("mag_ready")
        c_free = m.sem("c_free")
        dve_chain = m.sem("dve_chain")
        exps = m.sem("exps")
        alpha_ready = m.sem("alpha_ready")
        pre_act = m.sem("pre_act")
        q_ready = m.sem("q_ready")
        cm_chain = m.sem("cm_chain")
        cm_ready = m.sem("cm_ready")
        angles_ready = m.sem("angles_ready")
        trig_ready = m.sem("trig_ready")
        tables_ready = m.sem("tables_ready")
        vs_ready = m.sem("vs_ready")
        s2_done = m.sem("s2_done")
        s_ready = m.sem("s_ready")
        k_ready = m.sem("k_ready")
        kout_ready = m.sem("kout_ready")
        k_stored = m.sem("k_stored")

        block = ctx.enter_context(nc.Block())

        @block.sync
        def _(sp):
            sp.sem_inc(k_stored, 1)
            sp.dma_start(dyn[:, :, :], dyn_in).then_inc(ld, 16)
            sp.dma_start(mult[:, :, :], mult_in).then_inc(ld, 16)
            sp.dma_start(half[:, :], half_in).then_inc(ld, 16)

            def load(n, par):
                if not isinstance(n, int):
                    sp.wait_ge(c_free, n)
                sp.dma_start(craw[par][:, :, :, :], c_in[:, bass.ds(n * HS, HS), :, :]).then_inc(c_landed[par], 16)

            def step(n, par, last, pair):
                if not isinstance(n, int):
                    load(n + 2, par)
                sp.wait_ge(kout_ready, n * 2 + 3)
                sp.dma_start(h0[:, bass.ds(n * HS, HS), :], kout[:, :, :]).then_inc(k_stored, 16)

            load(0, 0)
            load(1, 1)
            for t, (dram, _, _, w) in enumerate(tiles):
                if t >= W_BUFS:
                    sp.wait_ge(w_lo, t - W_BUFS + 1)
                sp.dma_start(wraw[t % W_BUFS][:, 0:w], dram).then_inc(w_landed[t % W_BUFS], 16)
            all_steps(sp, step)
            sp.wait_ge(k_stored, 16 * STEPS + 1)

        @block.gpsimd
        def _(pool):
            pool.sem_inc(c_free, 1)
            pool.sem_inc(s_ready, 1)
            for t, (_, hi, lo, w) in enumerate(tiles):
                pool.wait_ge(w_hi, t + 1)
                pool.tensor_tensor(lo, wraw[t % W_BUFS][:, 0:w], hi.bitcast(F32), ALU.subtract).then_inc(w_lo, 1)
            pool.wait_ge(q_ready, 1)

            def coefficients(n, par, of_pair):
                chain = Chain(pool, cm_chain, n * 2)
                hs = bass.ds(n * HS, HS)
                pool.wait_ge(c_landed[par], of_pair * 16 + 16)
                if not isinstance(n, int):
                    pool.wait_ge(vs_ready, n * 2 - 1)
                cr = craw[par][:, :, 0, :].unsqueeze(1).broadcast_to([P, 2, HS, B])
                ci = craw[par][:, :, 1, :].unsqueeze(1).broadcast_to([P, 2, HS, B])
                pool.tensor_tensor(cm2[:, :, :, :], ci, qq[:, 1:3, hs].unsqueeze(3).broadcast_to([P, 2, HS, B]),
                                   ALU.mult)
                chain(pool.tensor_tensor(cm[par][:, :, :, :], cr,
                                         qq[:, 0:2, hs].unsqueeze(3).broadcast_to([P, 2, HS, B]), ALU.mult))
                chain(pool.tensor_tensor(cm[par][:, :, :, :], cm[par][:, :, :, :], cm2[:, :, :, :], ALU.add))
                pool.sem_inc(cm_ready, 1)
                pool.sem_inc(c_free, 1)

            def step(n, par, last, pair):
                if not last:
                    coefficients(n + 1, 1 - par, pair + par)
                for j in range(2):
                    if j == 0:
                        pool.wait_ge(tables_ready, n + 1)
                    pool.wait_ge(k_ready, n * 2 + (1 + j))
                    js = slice(j * HC, (j + 1) * HC)
                    pool.tensor_tensor(s2[j][:, :, :, :],
                                       cm[par][:, 1, js, :].unsqueeze(2).broadcast_to([P, HC, NA, B]),
                                       tr[par][:, 1, 2, js, :].unsqueeze(3).broadcast_to([P, HC, NA, B]),
                                       ALU.mult).then_inc(s2_done, 1)
                    pool.wait_ge(s2_done, n * 2 + (j + 1))
                    pool.wait_ge(vs_ready, n * 2 + (j + 2))
                    pool.tensor_tensor(s2[j][:, :, :, :], s2[j][:, :, :, :], s1[j][:, :, :, :],
                                       ALU.add).then_inc(s_ready, 1)

            coefficients(0, 0, 0)
            all_steps(pool, step)

        @block.vector
        def _(dve):
            dve.sem_inc(vs_ready, 1)
            c = Chain(dve, dve_chain)
            dve.wait_ge(ld, 48)
            c(dve.tensor_scalar(ex[:, :, :], dyn[:, 0:2, :], -87.0, 88.0, ALU.max, ALU.min))
            c(dve.tensor_scalar(ek[:, :, :], ex[:, :, :], 1.4426950408889634, ROUND, ALU.mult, ALU.add))
            c(dve.tensor_scalar(ek[:, :, :], ek[:, :, :], ROUND, None, ALU.subtract))
            c(dve.scalar_tensor_tensor(ex[:, :, :], ek[:, :, :], -LN2_1, ex[:, :, :], ALU.mult, ALU.add))
            c(dve.scalar_tensor_tensor(ex[:, :, :], ek[:, :, :], -LN2_2, ex[:, :, :], ALU.mult, ALU.add))
            c(dve.tensor_scalar(ep[:, :, :], ex[:, :, :], 1.0 / 5040, None, ALU.mult))
            for f in (720.0, 120.0, 24.0, 6.0, 2.0, 1.0):
                c(dve.scalar_tensor_tensor(ep[:, :, :], ep[:, :, :], 1.0 / f, ex[:, :, :], ALU.add, ALU.mult))
            c(dve.tensor_scalar(ei[:, :, :], ek[:, :, :], 127.0, None, ALU.add))
            c(dve.tensor_scalar(ei[:, :, :], ei[:, :, :], 23, None, ALU.logical_shift_left))
            c(dve.scalar_tensor_tensor(ep[:, :, :], ep[:, :, :], 1.0, ei[:, :, :].bitcast(F32), ALU.add, ALU.mult))
            dt, wabs, wi = ep[:, 0, :], ep[:, 1, :], dyn[:, 2, :]
            c(dve.tensor_scalar(wr[:, :], wabs, -1.0, None, ALU.mult))
            c(dve.tensor_tensor(al[:, :], wr[:, :], dt, ALU.mult))
            c(dve.tensor_tensor(th[:, :], wi, dt, ALU.mult))
            k, r, a = g[0], g[1], g[2]
            c(dve.tensor_scalar(k[:, :], th[:, :], 1.0 / (2 * PI), ROUND, ALU.mult, ALU.add))
            c(dve.tensor_scalar(k[:, :], k[:, :], ROUND, None, ALU.subtract))
            c(dve.scalar_tensor_tensor(r[:, :], k[:, :], -TWO_PI_1, th[:, :], ALU.mult, ALU.add))
            c(dve.scalar_tensor_tensor(r[:, :], k[:, :], -TWO_PI_2, r[:, :], ALU.mult, ALU.add))
            c(dve.scalar_tensor_tensor(r[:, :], k[:, :], -TWO_PI_3, r[:, :], ALU.mult, ALU.add))
            c(dve.tensor_scalar(r[:, :], r[:, :], PI, -PI, ALU.min, ALU.max))
            dve.scalar_tensor_tensor(a[:, :], r[:, :], -1.0, r[:, :], ALU.mult, ALU.max).then_inc(alpha_ready, 1)
            sn, cs, t = g[3], g[4], g[5]
            em1, nr, ni, den = g[0], g[1], g[2], g[6]
            dve.wait_ge(pre_act, 3)
            c(dve.tensor_scalar(den[:, :], t[:, :], -1.0, 1.0, ALU.mult, ALU.add))
            c(dve.reciprocal(den[:, :], den[:, :]))
            c(dve.scalar_tensor_tensor(em1[:, :], t[:, :], 2.0, den[:, :], ALU.mult, ALU.mult))
            c(dve.tensor_tensor(cs[:, :], cs[:, :], sn[:, :], ALU.mult))
            c(dve.scalar_tensor_tensor(sn[:, :], sn[:, :], -2.0, sn[:, :], ALU.mult, ALU.mult))
            c(dve.tensor_scalar(t[:, :], em1[:, :], 1.0, None, ALU.add))
            c(dve.tensor_tensor(nr[:, :], sn[:, :], t[:, :], ALU.mult))
            c(dve.tensor_tensor(nr[:, :], nr[:, :], em1[:, :], ALU.add))
            c(dve.scalar_tensor_tensor(ni[:, :], cs[:, :], 2.0, t[:, :], ALU.mult, ALU.mult))
            c(dve.tensor_tensor(sn[:, :], wr[:, :], wr[:, :], ALU.mult))
            c(dve.tensor_tensor(cs[:, :], wi, wi, ALU.mult))
            c(dve.tensor_tensor(den[:, :], sn[:, :], cs[:, :], ALU.add))
            c(dve.reciprocal(den[:, :], den[:, :]))
            c(dve.tensor_tensor(sn[:, :], nr[:, :], wr[:, :], ALU.mult))
            c(dve.tensor_tensor(cs[:, :], ni[:, :], wi, ALU.mult))
            c(dve.tensor_tensor(sn[:, :], sn[:, :], cs[:, :], ALU.add))
            c(dve.tensor_tensor(qq[:, 0, :], sn[:, :], den[:, :], ALU.mult))
            c(dve.tensor_tensor(sn[:, :], nr[:, :], wi, ALU.mult))
            c(dve.tensor_tensor(cs[:, :], ni[:, :], wr[:, :], ALU.mult))
            c(dve.tensor_tensor(sn[:, :], sn[:, :], cs[:, :], ALU.subtract))
            c(dve.tensor_tensor(qq[:, 1, :], sn[:, :], den[:, :], ALU.mult))
            dve.tensor_scalar(qq[:, 2, :], qq[:, 0, :], -1.0, None, ALU.mult).then_inc(q_ready, 1)

            used = c.n
            N_ANGLES, N_STEP = 8, 13

            def angles(n, par, base):
                c = Chain(dve, dve_chain, base)
                hs = bass.ds(n * HS, HS)
                full = [P, 3, HS, NM1]
                mt = mult[:, :, :].unsqueeze(2).broadcast_to(full)
                dve.tensor_tensor(mag[par][:, :, :, :], al[:, hs].unsqueeze(1).unsqueeze(3).broadcast_to(full), mt,
                                  ALU.mult).then_inc(mag_ready, 1)
                c(dve.tensor_tensor(ang[:, :, :, :], th[:, hs].unsqueeze(1).unsqueeze(3).broadcast_to(full), mt,
                                    ALU.mult))
                c(dve.tensor_scalar(turn[:, :, :, :], ang[:, :, :, :], 1.0 / (2 * PI), ROUND, ALU.mult, ALU.add))
                c(dve.tensor_scalar(turn[:, :, :, :], turn[:, :, :, :], ROUND, None, ALU.subtract))
                for part in (TWO_PI_1, TWO_PI_2, TWO_PI_3):
                    c(dve.scalar_tensor_tensor(ang[:, :, :, :], turn[:, :, :, :], -part, ang[:, :, :, :], ALU.mult,
                                               ALU.add))
                c(dve.tensor_scalar(ang[:, :, :, :], ang[:, :, :, :], PI, -PI, ALU.min, ALU.max))
                c(dve.scalar_tensor_tensor(ra[:, :, :, :], ang[:, :, :, :], half[:, 0:1], ang[:, :, :, :], ALU.mult,
                                           ALU.max))
                dve.scalar_tensor_tensor(rb[:, :, :, :], ang[:, :, :, :], half[:, 1:2], ang[:, :, :, :], ALU.mult,
                                         ALU.max).then_inc(angles_ready, 1)
                assert c.n == N_ANGLES

            def scale(n, par, base):
                dve.wait_ge(trig_ready, n + 2)
                flat = tr[par][:, :, :, :, :].rearrange("p t g h m -> p t (g h m)")
                Chain(dve, dve_chain, base)(dve.tensor_tensor(
                    flat, flat, mag[par][:, :, :, :].rearrange("p g h m -> p (g h m)").unsqueeze(1).broadcast_to(
                        [P, 2, 3 * HS * NM1]), ALU.mult))
                dve.sem_inc(tables_ready, 1)

            def operands(n, par, base):
                c = Chain(dve, dve_chain, base)
                t = tr[par]
                dve.wait_ge(cm_ready, n + 1)
                for j in range(2):
                    js = slice(j * HC, (j + 1) * HC)
                    out4 = [P, HC, NM1, NM1]
                    dve.wait_ge(k_ready, n * 2 + (1 + j))
                    dve.tensor_tensor(v2[:, :, :].rearrange("p h (a b) -> p h a b", b=NM1),
                                      t[:, 1, 1, js, :].unsqueeze(3).broadcast_to(out4),
                                      t[:, 1, 0, js, :].unsqueeze(2).broadcast_to(out4), ALU.mult)
                    c(dve.tensor_tensor(vv[j][:, :, :].rearrange("p h (a b) -> p h a b", b=NM1),
                                        t[:, 0, 1, js, :].unsqueeze(3).broadcast_to(out4),
                                        t[:, 0, 0, js, :].unsqueeze(2).broadcast_to(out4), ALU.mult))
                    c(dve.tensor_tensor(vv[j][:, :, :], vv[j][:, :, :], v2[:, :, :], ALU.add))
                    dve.tensor_tensor(s1[j][:, :, :, :],
                                      cm[par][:, 0, js, :].unsqueeze(2).broadcast_to([P, HC, NA, B]),
                                      t[:, 0, 2, js, :].unsqueeze(3).broadcast_to([P, HC, NA, B]),
                                      ALU.mult).then_inc(vs_ready, 1)
                assert c.n == N_STEP - N_ANGLES - 1

            def step(n, par, last, pair):
                base = n * N_STEP + (used + N_ANGLES + 1)
                if not last:
                    angles(n + 1, 1 - par, base)
                    base = n * N_STEP + (used + 2 * N_ANGLES + 1)
                operands(n, par, base)
                if not last:
                    scale(n + 1, 1 - par, n * N_STEP + (used + N_ANGLES + N_STEP))

            angles(0, 0, used)
            scale(0, 0, used + N_ANGLES)
            all_steps(dve, step)

        @block.scalar
        def _(act):
            act.sem_inc(trig_ready, 1)
            act.sem_inc(kout_ready, 1)

            def leading(first, last):
                for t in range(first, last):
                    _, hi, _, w = tiles[t]
                    act.wait_ge(w_landed[t % W_BUFS], 16 * (t // W_BUFS + 1))
                    act.activation(hi, wraw[t % W_BUFS][:, 0:w], ACT.Copy).then_inc(w_hi, 1)

            leading(0, len(tiles) // 3)
            act.wait_ge(alpha_ready, 1)
            act.activation(g[3][:, :], g[1][:, :], ACT.Sin, scale=0.5).then_inc(pre_act, 1)
            act.activation(g[4][:, :], g[2][:, :], ACT.Sin, bias=half[:, 6:7], scale=-0.5).then_inc(pre_act, 1)
            act.activation(g[5][:, :], al[:, :], ACT.Tanh, scale=0.5).then_inc(pre_act, 1)

            leading(len(tiles) // 3, len(tiles))

            def tables(n, par):
                act.wait_ge(mag_ready, n + 1)
                act.activation(mag[par][:, :, :, :], mag[par][:, :, :, :], ACT.Exp)
                act.wait_ge(angles_ready, n + 1)
                if not isinstance(n, int):
                    act.wait_ge(vs_ready, n * 2 - 1)
                    act.wait_ge(s_ready, n * 2 - 1)
                sin, t = ACT.Sin, tr[par]
                act.activation(t[0:64, 0, 0], ra[0:64, 0], sin, bias=half[0:64, 6:7], scale=-1.0)
                act.activation(t[64:128, 0, 0], rb[64:128, 0], sin, bias=half[64:128, 6:7], scale=-1.0)
                act.activation(t[0:64, 1, 0], rb[0:64, 0], sin)
                act.activation(t[64:128, 1, 0], ra[64:128, 0], sin)
                act.activation(t[:, 0, 1], ra[:, 1], sin, bias=half[:, 2:3], scale=half[:, 0:1])
                act.activation(t[:, 1, 1], rb[:, 1], sin, bias=half[:, 3:4], scale=-1.0)
                act.activation(t[:, 0, 2], ra[:, 2], sin, bias=half[:, 2:3], scale=-1.0)
                act.activation(t[:, 1, 2], rb[:, 2], sin, bias=half[:, 3:4],
                               scale=half[:, 1:2]).then_inc(trig_ready, 1)

            def step(n, par, last, pair):
                if not last:
                    tables(n + 1, 1 - par)
                for j in range(2):
                    act.wait_ge(k_ready, n * 2 + (j + 3))
                    if j == 0:
                        act.wait_ge(k_stored, n * 16 + 1)
                    act.activation(kout[:, j * HC:(j + 1) * HC, :], kps[j][:, :, :], ACT.Copy,
                                   scale=2.0).then_inc(kout_ready, 1)

            tables(0, 0)
            all_steps(act, step)

        @block.tensor
        def _(pe):
            pe.sem_inc(k_ready, 2)

            def step(n, par, last, pair):
                for j in range(2):
                    pe.wait_ge(vs_ready, n * 2 + (j + 2))
                    pe.wait_ge(s_ready, n * 2 + (j + 2))
                    pe.wait_ge(kout_ready, n * 2 + 1)
                    for h in range(HC):
                        mm = pe.matmul(kps[j][:, h, :], s2[j][:, h], vv[j][:, h, :], start=True, stop=True)
                    mm.then_inc(k_ready, 1)

            all_steps(pe, step)




def mm3(pe, out, lhs, rhs, start, stop):
    pe.matmul(out, lhs[0], rhs[0], start=start, stop=False)
    pe.matmul(out, lhs[0], rhs[1], start=False, stop=False)
    return pe.matmul(out, lhs[1], rhs[0], start=False, stop=stop)


def weight_tiles(parts, width):
    return [(dram[:, a:a + width], hi[:, a:a + width], lo[:, a:a + width], min(width, dram.shape[1] - a))
            for dram, hi, lo in parts for a in range(0, dram.shape[1], width)]


def split_weights(nc, parts):
    with ExitStack() as ctx:
        m = Memory(nc, ctx)
        width = 1024
        tiles = weight_tiles(parts, width)
        bufs = 4
        raw = [m.sb(f"wraw{n}", [P, width]) for n in range(bufs)]
        landed = [m.sem(f"w_landed{n}") for n in range(bufs)]
        hi_done = m.sem("w_hi_done")
        lo_done = m.sem("w_lo_done")
        block = ctx.enter_context(nc.Block())

        @block.sync
        def _(sp):
            for t, (dram, _, _, w) in enumerate(tiles):
                if t >= bufs:
                    sp.wait_ge(lo_done, t - bufs + 1)
                sp.dma_start(raw[t % bufs][:, 0:w], dram).then_inc(landed[t % bufs], 16)

        @block.scalar
        def _(act):
            for t, (_, hi, _, w) in enumerate(tiles):
                act.wait_ge(landed[t % bufs], 16 * (t // bufs + 1))
                act.activation(hi, raw[t % bufs][:, 0:w], ACT.Copy).then_inc(hi_done, 1)

        @block.vector
        def _(dve):
            for t, (_, hi, lo, w) in enumerate(tiles):
                dve.wait_ge(hi_done, t + 1)
                dve.tensor_tensor(lo, raw[t % bufs][:, 0:w], hi.bitcast(F32), ALU.subtract).then_inc(lo_done, 1)


NH, NKV, HD = 16, 4, 128
REP = NH // NKV
NEG = -1e37
BIG = 3e38


def flat(t):
    return t[:, :, :].rearrange("p a n -> p (a n)")


def attention0(nc, wq, wk, wv, wo_in, rope_in, mask_in, ident_in, h0, h1):
    with ExitStack() as wctx:
        wo = [Memory(nc, wctx).sb(f"wo{p}", [P, NH, D], F32R) for p in ("h", "l")]
        split_weights(nc, [(wo_in, flat(wo[0]), flat(wo[1]))])
        with ExitStack() as ctx:
            attention0_loop(nc, Memory(nc, ctx), wq, wk, wv, wo, rope_in, mask_in, ident_in, h0, h1)


def stages_1_and_2(nc, dyn, coef, mult, half, wq_in, wk_in, wv_in, wo_in, rope_in, mask_in, ident_in, h0, h1):
    with ExitStack() as ctx:
        m = Memory(nc, ctx)
        wq = [m.sb(f"wq{p}", [P, CD, NH * HD], F32R) for p in ("h", "l")]
        wk = [m.sb(f"wk{p}", [P, CD, NKV * HD], F32R) for p in ("h", "l")]
        wv = [m.sb(f"wv{p}", [P, CD, NKV * HD], F32R) for p in ("h", "l")]
        token_mixer(nc, dyn, coef, mult, half, h0,
                    [(x, flat(w[0]), flat(w[1])) for x, w in ((wk_in, wk), (wv_in, wv), (wq_in, wq))])
        attention0(nc, wq, wk, wv, wo_in, rope_in, mask_in, ident_in, h0, h1)


class Image:

    def __init__(self, i):
        self.i, self.n, self.u, self.r = i, i * NH, i * UNITS, i * ROPES


UNITS, ROPES = 2 + NKV + ST + NH, NKV + NH
K_UNIT = [ST + g for g in range(NKV)]
V_UNIT = [ST + NKV + 1 + t for t in range(ST)]
Q_UNIT = [ST + NKV] + [2 * ST + NKV + h for h in range(1, NH)]


def all_images(eng, start, step, finish=None):

    def image(i, first=False, last=False):
        for s in range(NH + 2):
            step(Image(i), s, None if last else Image(i + 1), None if first else Image(i - 1))

    start(Image(0))
    image(0, first=True)
    with eng.Fori(0, B - 2) as i:
        image(i + 1)
    image(B - 1, last=True)
    if finish:
        finish(Image(B - 1))


def attention0_loop(nc, m, wq, wk, wv, wo, rope_in, mask_in, ident_in, h0, h1):
    SCALE = float(HD) ** -0.5
    ident = m.sb("ident", [P, P])
    cos = m.sb("cos", [P, S])
    sin = m.sb("sin", [P, S])
    mask = m.sb("mask", [P, 2 * P])
    xs = m.sb("xs", [P, D])
    res = m.sb("res", [P, ST, D])
    xT = [m.sb(f"xT{p}", [P, CD, S], F32R) for p in "hl"]
    kT = [m.sb(f"kT{p}", [P, NKV, S], F32R) for p in "hl"]
    v = [m.sb(f"v{p}", [P, ST, NKV * HD], F32R) for p in "hl"]
    turn = [[m.sb(f"turn{n}", [P, S])[:, :] for n in range(2)], [xs[:, 0:S], xs[:, S:2 * S]]]
    q = [[m.sb(f"q{p}{n}", [P, S], F32R) for p in "hl"] for n in range(2)]
    prob = [m.sb(f"prob{n}", [P, 3 * P]) for n in range(2)]
    pT = [m.sb(f"pT{p}", [P, 3 * P], F32R) for p in "hl"]
    oT = [m.sb(f"oT{p}", [P, S], F32R) for p in "hl"]
    mx = m.sb("mx", [P, 2, ST])
    sums = m.sb("sums", [P, 2, ST])
    inv = m.sb("inv", [P, 2, ST])
    st = m.sb("st", [P, ST, 6])
    mv = m.sb("mv", [P, ST, 2])
    nhalf = m.sb("nhalf", [P, ST])
    proj = [m.ps(f"proj{n}", [P, 512]) for n in range(3)]
    sc = m.ps("sc", [P, 512])
    pTp = m.ps("pTp", [P, 512])
    oTp = m.ps("oTp", [P, 512])
    acc = [m.ps(f"acc{t}", [P, D]) for t in range(ST)]

    consts = m.sem("consts")
    dve_passed = m.sem("a_dve_passed")
    x_landed = m.sem("x_landed")
    res_landed = m.sem("res_landed")
    proj_ready = m.sem("proj_ready")
    proj_used = m.sem("proj_used")
    split_hi = m.sem("split_hi")
    rope_sum = m.sem("rope_sum")
    rope_hi = m.sem("rope_hi")
    rope_lo = m.sem("rope_lo")
    sc_ready = m.sem("sc_ready")
    mx_ready = m.sem("mx_ready")
    ex_ready = m.sem("ex_ready")
    inv_ready = m.sem("inv_ready")
    p_ready = m.sem("p_ready")
    pt_ready = m.sem("pt_ready")
    pt_hi = m.sem("pt_hi")
    pt_lo = m.sem("pt_lo")
    pv_ready = m.sem("pv_ready")
    ot_hi = m.sem("ot_hi")
    ot_lo = m.sem("ot_lo")
    o_done = m.sem("o_done")
    ln_chain = m.sem("ln_chain")
    ln_var = m.sem("ln_var")
    ln_rstd = m.sem("ln_rstd")
    ln_done = m.sem("ln_done")
    stored = m.sem("stored")

    head = lambda h: 0 <= h < NH
    LN_STEPS = 3
    PAIRED = NKV + 2
    products = lambda r: turn[r % 2 if r < PAIRED else 0]
    block = m.ctx.enter_context(nc.Block())

    @block.sync
    def _(sp):
        sp.sem_inc(stored, 1)
        sp.dma_start(ident[:, :], ident_in).then_inc(consts, 16)
        sp.dma_start(cos[:, :], rope_in[:, 0, :]).then_inc(consts, 16)
        sp.dma_start(sin[:, :], rope_in[:, 1, :]).then_inc(consts, 16)
        sp.dma_start(mask[:, :], mask_in).then_inc(consts, 16)
        h0_v = h0.rearrange("(a b) s m -> b s a m", b=B)
        h1_v = h1.rearrange("b (t p) d -> b p t d", p=P)

        def load(i, t, dst, sem):
            src = h0_v[bass.ds(i, 1), t * P:(t + 1) * P, :, :].rearrange("o s a m -> (o s) a m")
            sp.dma_start(dst.rearrange("p (a m) -> p a m", m=NM), src).then_inc(sem, 16)

        def load_res(i):
            for t in range(ST):
                load(i, t, res[:, t, :], res_landed)

        def store(i):
            sp.wait_ge(ln_done, i + 1)
            sp.dma_start(h1_v[bass.ds(i, 1), :, :, :].rearrange("o p t d -> (o p) t d"), res[:, :, :])\
              .then_inc(stored, 16)

        load(0, 0, xs[:, :], x_landed)
        sp.wait_ge(proj_ready, 2)
        load(0, 1, xs[:, :], x_landed)
        load_res(0)
        with sp.Fori(0, B - 1) as i:
            sp.wait_ge(rope_lo, i * ROPES + (PAIRED + 2))
            load(i + 1, 0, xs[:, :], x_landed)
            sp.wait_ge(proj_ready, i * UNITS + (UNITS + 2))
            load(i + 1, 1, xs[:, :], x_landed)
            store(i)
            sp.wait_ge(stored, 16 * i + 17)
            load_res(i + 1)
        store(B - 1)
        sp.wait_ge(stored, 16 * B + 1)

    @block.tensor
    def _(pe):
        pe.sem_inc(sc_ready, 2)
        pe.sem_inc(pt_ready, 2)
        for first in (proj_ready, pv_ready, o_done):
            pe.sem_inc(first, 1)
        pe.wait_ge(consts, 64)

        def bank(im, u):
            pe.wait_ge(proj_used, im.u + (u + 1))
            return proj[u % 3]

        def x_transpose(im, t):
            pe.wait_ge(x_landed, im.i * (16 * ST) + 16 * (t + 1))
            b = bank(im, t)
            for c in range(CD):
                mm = pe.transpose(b[:, c * P:(c + 1) * P], xs[:, c * P:(c + 1) * P], ident[:, :])
            mm.then_inc(proj_ready, 1)

        def keys(im, g):
            b = bank(im, K_UNIT[g])
            if g == 0:
                pe.wait_ge(proj_used, im.u + (3 + ST))
            for c in range(CD):
                mm = mm3(pe, b[:, 0:S], [x[:, c, g * HD:(g + 1) * HD] for x in wk], [x[:, c, :] for x in xT],
                         c == 0, c == CD - 1)
            mm.then_inc(proj_ready, 1)

        def values(im, t):
            b = bank(im, V_UNIT[t])
            for c in range(CD):
                mm = mm3(pe, b[:, :], [x[:, c, t * P:(t + 1) * P] for x in xT], [x[:, c, :] for x in wv],
                         c == 0, c == CD - 1)
            mm.then_inc(proj_ready, 1)

        def queries(im, h):
            b = bank(im, Q_UNIT[h])
            for c in range(CD):
                mm = mm3(pe, b[:, 0:S], [x[:, c, h * HD:(h + 1) * HD] for x in wq],
                         [x[:, c, :] for x in xT], c == 0, c == CD - 1)
            mm.then_inc(proj_ready, 1)

        def output(im, h):
            pe.wait_ge(ot_lo, im.n + (h + 2))
            if h == 0:
                pe.wait_ge(ln_var, im.i + 1)
            for t in range(ST):
                mm = mm3(pe, acc[t][:, :], [x[:, t * P:(t + 1) * P] for x in oT], [x[:, h, :] for x in wo],
                         h == 0, h == NH - 1)
            mm.then_inc(o_done, 1)

        def start(im):
            x_transpose(im, 0)
            x_transpose(im, 1)
            for g in range(2):
                keys(im, g)
            rest(im)

        def rest(im):
            keys(im, 2)
            keys(im, 3)
            queries(im, 0)
            values(im, 0)
            values(im, 1)
            queries(im, 1)

        def step(im, s, after, before):
            n = im.n
            if head(s):
                h, g = s, s // REP
                pe.wait_ge(rope_lo, im.r + (NKV + h + 3))
                pe.wait_ge(mx_ready, n + (h + 1))
                qh = q[h % 2]
                mm3(pe, sc[:, 0:P], [x[:, 0:P] for x in qh], [x[:, g, 0:P] for x in kT], True, True)
                mm3(pe, sc[:, P:3 * P], [x[:, P:S] for x in qh], [x[:, g, :] for x in kT], True, True)\
                    .then_inc(sc_ready, 1)
            if head(s - 2):
                h, g = s - 2, (s - 2) // REP
                pe.wait_ge(pt_lo, n + (h + 2))
                pe.wait_ge(ot_lo, n + (h + 1))
                if h == 0:
                    pe.wait_ge(proj_used, im.u + (4 + V_UNIT[1]))
                mm3(pe, oTp[:, 0:S], [x[:, 0, g * HD:(g + 1) * HD] for x in v], [x[:, 0:S] for x in pT], True,
                    False)
                mm3(pe, oTp[:, P:S], [x[:, 1, g * HD:(g + 1) * HD] for x in v], [x[:, S:3 * P] for x in pT],
                    False, True).then_inc(pv_ready, 1)
            if head(s + 2):
                queries(im, s + 2)
            elif after and s < NH:
                x_transpose(after, s - (NH - 2))
            elif after and s == NH:
                keys(after, 0)
                keys(after, 1)
            if s == 1 and before:
                output(before, NH - 1)
            if head(s - 1):
                h = s - 1
                pe.wait_ge(p_ready, n + (h + 1))
                pe.wait_ge(pt_lo, n + (h + 1))
                pr = prob[h % 2]
                pe.transpose(pTp[:, 0:P], pr[:, 0:P], ident[:, :])
                pe.transpose(pTp[:, P:2 * P], pr[:, P:2 * P], ident[:, :])
                pe.transpose(pTp[:, 2 * P:3 * P], pr[:, 2 * P:3 * P], ident[:, :]).then_inc(pt_ready, 1)

            if head(s - 2) and not (after and s == NH + 1):
                output(im, s - 2)
            elif after and s == NH + 1:
                rest(after)

        all_images(pe, start, step)

    @block.scalar
    def _(act):
        def x_split(im, t):
            act.wait_ge(proj_ready, im.u + (t + 2))
            act.activation(xT[0][:, :, t * P:(t + 1) * P], proj[t][:, :].rearrange("p (c s) -> p c s", c=CD),
                           ACT.Copy).then_inc(split_hi, 1)

        def k_split(im, g):
            act.wait_ge(rope_sum, im.r + (g + 1))
            act.activation(kT[0][:, g, :], products(g)[0], ACT.Copy).then_inc(rope_hi, 1)

        def v_split(im, t):
            act.wait_ge(proj_ready, im.u + (V_UNIT[t] + 2))
            act.activation(v[0][:, t, :], proj[V_UNIT[t] % 3][:, :], ACT.Copy).then_inc(split_hi, 1)

        def q_split(im, h):
            act.wait_ge(rope_sum, im.r + (NKV + h + 1))
            act.wait_ge(sc_ready, im.n + (h + 1))
            act.activation(q[h % 2][0][:, :], products(NKV + h)[0], ACT.Copy).then_inc(rope_hi, 1)

        def start(im):
            x_split(im, 0)
            x_split(im, 1)
            k_split(im, 0)
            k_split(im, 1)
            rest(im)

        def rest(im):
            k_split(im, 2)
            k_split(im, 3)
            q_split(im, 0)
            v_split(im, 0)
            v_split(im, 1)

        def step(im, s, after, before):
            n = im.n
            if head(s + 1):
                q_split(im, s + 1)
            if head(s - 2):
                h = s - 2
                act.wait_ge(pv_ready, n + (h + 2))
                act.wait_ge(o_done, n + (h + 1))
                act.activation(oT[0][:, :], oTp[:, 0:S], ACT.Copy).then_inc(ot_hi, 1)
            if head(s):
                h = s
                act.wait_ge(mx_ready, n + (h + 2))
                for t, (a, b) in enumerate(((0, P), (P, 3 * P))):
                    ins = act.activation(prob[h % 2][:, a:b], prob[h % 2][:, a:b], ACT.Exp,
                                         bias=mx[:, h % 2, t:t + 1], scale=-1.0,
                                         accum_out=sums[:, h % 2, t:t + 1])
                ins.then_inc(ex_ready, 1)
            if head(s - 1):
                h = s - 1
                act.wait_ge(pt_ready, n + (h + 3))
                act.wait_ge(pv_ready, n + (h + 1))
                act.activation(pT[0][:, :], pTp[:, 0:3 * P], ACT.Copy).then_inc(pt_hi, 1)
            if after and s in (NH - 2, NH - 1):
                x_split(after, s - (NH - 2))
            elif after and s == NH:
                act.wait_ge(sc_ready, after.n + 2)
                k_split(after, 0)
                k_split(after, 1)
            elif after and s == NH + 1:
                act.wait_ge(pv_ready, after.n + 1)
                rest(after)

        all_images(act, start, step)

    @block.gpsimd
    def _(pool):
        pool.sem_inc(rope_lo, 2)
        pool.memset(nhalf[:, :], -0.5)

        def parts(r):
            return (kT[0][:, r, :], kT[1][:, r, :]) if r < NKV else (q[r % 2][0][:, :], q[r % 2][1][:, :])

        def add(im, r):
            u = K_UNIT[r] if r < NKV else Q_UNIT[r - NKV]
            a, b = products(r)
            pool.wait_ge(proj_used, im.u + (3 + u + 1))
            pool.tensor_tensor(a, a, b, ALU.add).then_inc(rope_sum, 1)

        def rest_of(im, r):
            hi, lo = parts(r)
            pool.wait_ge(rope_hi, im.r + (r + 1))
            pool.tensor_tensor(lo, products(r)[0], hi.bitcast(F32), ALU.subtract).then_inc(rope_lo, 1)

        def start(im):
            add(im, 0)
            add(im, 1)
            rest_of(im, 0)
            rest_of(im, 1)
            rest(im)

        def rest(im):
            add(im, 2)
            add(im, 3)
            rest_of(im, 2)
            add(im, NKV)
            rest_of(im, 3)
            rest_of(im, NKV)
            add(im, NKV + 1)

        def step(im, s, after, before):
            if s == 0:
                rest_of(im, NKV + 1)
            if head(s + 2):
                add(im, NKV + s + 2)
                rest_of(im, NKV + s + 2)
            if s == 1 and before:
                power(before)
            if after and s == NH:
                add(after, 0)
                add(after, 1)
                rest_of(after, 0)
                rest_of(after, 1)
            elif after and s == NH + 1:
                rest(after)

        def power(im):
            pool.wait_ge(ln_var, im.i + 2)
            pool.tensor_tensor(mv[:, :, 1], mv[:, :, 1], nhalf[:, :], ALU.pow).then_inc(ln_rstd, 1)

        all_images(pool, start, step, power)

    @block.vector
    def _(dve):
        dve.sem_inc(proj_used, 3)
        for first in (mx_ready, ot_lo, pt_lo, ln_var):
            dve.sem_inc(first, 1)
        dve.wait_ge(consts, 64)

        def rope(im, u, r):
            b, (p, p_turned) = proj[u % 3], products(r)
            dve.wait_ge(proj_ready, im.u + (u + 2))
            dve.wait_ge(rope_lo, im.r + (r + (1 if 0 < r <= PAIRED else 2)))
            dve.tensor_tensor(p_turned[0:64, :], b[64:P, 0:S], sin[0:64, :], ALU.mult)
            dve.tensor_tensor(p_turned[64:P, :], b[0:64, 0:S], sin[64:P, :], ALU.mult)
            dve.tensor_tensor(p, b[:, 0:S], cos[:, :], ALU.mult).then_inc(proj_used, 1)

        def x_split(im, t):
            dve.wait_ge(split_hi, im.i * (2 * ST) + (t + 1))
            sl = slice(t * P, (t + 1) * P)
            dve.tensor_tensor(xT[1][:, :, sl], proj[t][:, :].rearrange("p (c s) -> p c s", c=CD),
                              xT[0][:, :, sl].bitcast(F32), ALU.subtract).then_inc(proj_used, 1)

        def keys(im, g):
            rope(im, K_UNIT[g], g)

        def v_split(im, t):
            dve.wait_ge(split_hi, im.i * (2 * ST) + (ST + t + 1))
            dve.tensor_tensor(v[1][:, t, :], proj[V_UNIT[t] % 3][:, :], v[0][:, t, :].bitcast(F32),
                              ALU.subtract).then_inc(proj_used, 1)

        def queries(im, h):
            rope(im, Q_UNIT[h], NKV + h)

        def start(im):
            x_split(im, 0)
            x_split(im, 1)
            keys(im, 0)
            keys(im, 1)
            rest(im)

        def rest(im):
            keys(im, 2)
            keys(im, 3)
            queries(im, 0)
            v_split(im, 0)
            v_split(im, 1)
            queries(im, 1)

        def variance(im):
            ch = Chain(dve, ln_chain, im.i * LN_STEPS)
            dve.wait_ge(o_done, im.n + (NH + 1))
            dve.wait_ge(res_landed, im.i * (16 * ST) + 16 * ST)
            for t in range(ST):
                ins = dve.tensor_tensor(res[:, t, :], res[:, t, :], acc[t][:, :], ALU.add)
            ch(ins)
            for t in range(ST):
                ins = dve.bn_stats(st[:, t, :], res[:, t, :])
            ch(ins)
            carry_wait(dve, dve_passed)
            for t in range(ST):
                ins = dve.bn_aggr(mv[:, t, :], st[:, t, :])
            ch(ins)
            dve.tensor_scalar(mv[:, :, 1], mv[:, :, 1], LN_EPS, None, ALU.add).then_inc(ln_var, 1)

        def normalise(im):
            dve.wait_ge(ln_rstd, im.i + 1)
            for t in range(ST):
                ins = dve.tensor_scalar(res[:, t, :], res[:, t, :], mv[:, t, 0:1], mv[:, t, 1:2], ALU.subtract,
                                        ALU.mult)
            ins.then_inc(ln_done, 1)

        def step(im, s, after, before):
            n = im.n
            if head(s):
                h = s
                dve.wait_ge(sc_ready, n + (h + 3))
                dve.wait_ge(pt_ready, n + (h + 1))
                carry_wait(dve, dve_passed)
                for t, (a, b) in enumerate(((0, P), (P, 3 * P))):
                    ins = dve.tensor_tensor_reduce(out=prob[h % 2][:, a:b], in0=sc[:, a:b],
                                                   in1=mask[:, 2 * P - (b - a):2 * P], scale=-SCALE, scalar=BIG,
                                                   op0=ALU.add, op1=ALU.min, accum_out=mx[:, h % 2, t:t + 1])
                ins.then_inc(mx_ready, 1)
            if head(s - 2):
                h = s - 2
                dve.wait_ge(ot_hi, n + (h + 1))
                dve.tensor_tensor(oT[1][:, :], oTp[:, 0:S], oT[0][:, :].bitcast(F32), ALU.subtract)\
                   .then_inc(ot_lo, 1)
            if head(s):
                h = s
                dve.wait_ge(ex_ready, n + (h + 1))
                dve.reciprocal(inv[:, h % 2, :], sums[:, h % 2, :]).then_inc(inv_ready, 1)
                dve.wait_ge(inv_ready, n + (h + 1))
                for t, (a, b) in enumerate(((0, P), (P, 3 * P))):
                    ins = dve.tensor_scalar(prob[h % 2][:, a:b], prob[h % 2][:, a:b], inv[:, h % 2, t:t + 1],
                                            None, ALU.mult)
                ins.then_inc(p_ready, 1)
            if head(s + 2):
                queries(im, s + 2)
            if head(s - 1):
                h = s - 1
                dve.wait_ge(pt_hi, n + (h + 1))
                dve.tensor_tensor(pT[1][:, :], pTp[:, 0:3 * P], pT[0][:, :].bitcast(F32), ALU.subtract)\
                   .then_inc(pt_lo, 1)
            if s == 1 and before:
                variance(before)
            if s == 2 and before:
                normalise(before)
            if after and s in (NH - 2, NH - 1):
                x_split(after, s - (NH - 2))
            elif after and s == NH:
                keys(after, 0)
                keys(after, 1)
            elif after and s == NH + 1:
                rest(after)

        def finish(im):
            variance(im)
            normalise(im)

        all_images(dve, start, step, finish)


NH1, HD1 = 16, 32
G1 = 4
QEPS = 1e-5
F_UNITS = ["qT0", "qT1", "ffn0", "ffn1", "x0", "x1", "q0", "kv0", "q1", "kv1", "tq0", "tk0", "tq1", "tk1"]
G_UNITS = ["out0", "out1"]
ALL_UNITS = G_UNITS + F_UNITS
BANKS = 2
HIS = ["x0", "x1", "v0", "v1", "tq0", "tk0", "tq1", "tk1"]
BETWEEN = {1: ["f_quant"], 2: ["g_out0", "g_out1"], 3: ["f_qT"], 4: ["g_norm", "f_ffn"], 6: ["f_norm"],
           7: ["f_xT"], 8: ["f_q0"], 9: ["f_kv0"], 12: ["f_q1"], 13: ["f_kv1"], 15: ["f_hT0"], 17: ["f_hT1"]}
LAG = 4


class Segment:

    def __init__(self, b, kind, parity):
        self.b, self.kind, self.parity = b, kind, parity
        self.units = {"front": F_UNITS, "all": ALL_UNITS, "back": G_UNITS}[kind]
        self.hi0 = len(HIS) * (b + 1)
        before = 2 * len(F_UNITS) - len(ALL_UNITS)
        if kind == "front":
            self.unit0 = len(F_UNITS) * (b + 1)
            self.mod = self.unit0 % BANKS
        elif kind == "all" or b == B - 1:
            self.unit0 = b * len(ALL_UNITS) + before
            self.mod = before % BANKS
        else:
            self.unit0 = (B - 1) * len(ALL_UNITS) + before + len(G_UNITS)
            self.mod = self.unit0 % BANKS

    def unit(self, name):
        return self.unit0 + (self.units.index(name) + 1)

    def bank(self, name):
        return (self.mod + self.units.index(name)) % BANKS

    def hi(self, name):
        return self.hi0 + (HIS.index(name) + 1)


def run_segment(seg, h):
    heads = 0 <= seg.b < B if isinstance(seg.b, int) else True
    for s in range(NH1 + LAG + 1):
        for name, k in (("read", s - LAG), ("sc", s), ("mx", s), ("ex", s - 1), ("pt", s - 2), ("pv", s - 3)):
            if heads and name in h and 0 <= k < NH1:
                h[name](seg, k)
        if heads and "divide" in h and s >= LAG and (s - LAG) % 4 == 3:
            h["divide"](seg, (s - LAG) // 4)
        if heads and "split" in h and s > LAG and (s - LAG) % 4 == 0:
            h["split"](seg, (s - LAG) // 4 - 1)
        for name in BETWEEN.get(s, []):
            if name[0] == "g" and seg.kind == "front" or name[0] == "f" and seg.kind == "back":
                continue
            stage = name.rstrip("01")
            if stage in h:
                h[stage](seg) if stage == name else h[stage](seg, int(name[-1]))


def all_segments(eng, h):
    run_segment(Segment(-1, "front", 1), h)
    run_segment(Segment(0, "front", 0), h)
    with eng.Fori(0, (B - 2) // 2) as i:
        run_segment(Segment(i * 2 + 1, "all", 1), h)
        run_segment(Segment(i * 2 + 2, "all", 0), h)
    run_segment(Segment(B - 1, "back", 1), h)
    run_segment(Segment(B, "back", 0), h)


def block01(nc, fw_in, fb_in, wq_in, wkv_in, wo_in, bias_in, rope_in, mask_in, ident_in, identb_in, h1, h3):
    SCALE = float(HD1) ** -0.5
    with ExitStack() as ctx:
        m = Memory(nc, ctx)
        ident = m.sb("b_ident", [P, P])
        identb = m.sb("b_identb", [P, P], BF16)
        rope = m.sb("b_rope", [P, 2, ST, HD1])
        mask = m.sb("b_mask", [P, 2 * P])
        fraw = m.sb("b_fraw", [P, CD * D])
        ftmp = m.sb("b_ftmp", [P, CD * D])
        fw = m.sb("b_fw", [P, CD, D], BF16)
        fbias = m.sb("b_fbias", [P, D])
        asum = m.sb("b_asum", [P, 1])
        alpha = m.sb("b_alpha", [P, 2])
        ones = m.sb("b_ones", [P, P])
        onesr = m.sb("b_onesr", [1, P], F32R)
        wraw = m.sb("b_wraw", [P, CD, D + 2 * P + D], BF16)
        wq = m.sb("b_wq", [P, CD, D], F32R)
        wkv = m.sb("b_wkv", [P, CD, 2 * P], F32R)
        wo = m.sb("b_wo", [P, CD, D], F32R)
        braw = m.sb("b_braw", [1, D + 2 * P], BF16)
        bqkv = m.sb("b_bqkv", [1, D + 2 * P], F32R)
        x1 = m.sb("b_x1", [P, ST, D])
        am = m.sb("b_am", [P, ST])
        rs = m.sb("b_rs", [P, ST])
        sa = m.sb("b_sa", [P, ST])
        qf = m.sb("b_qf", [P, ST, D])
        qb = m.sb("b_qb", [P, ST, D], BF16)
        xb = m.sb("b_xb", [P, ST, D])
        qTb = m.sb("b_qTb", [P, ST, CD, P], BF16)
        x2 = [m.sb(f"b_x2{n}", [P, ST, D]) for n in range(2)]
        xT = [m.sb(f"b_xT{p}", [P, CD, S], F32R) for p in "hl"]
        tq = [m.sb(f"b_tq{n}", [P, D]) for n in range(2)]
        tk = [m.sb(f"b_tk{n}", [P, P]) for n in range(2)]
        qr = m.sb("b_qr", [P, ST, D])
        kr = m.sb("b_kr", [P, ST, D])
        qT = [[m.sb(f"b_qT{p}{n}", [P, G1, S], F32R) for p in "hl"] for n in range(2)]
        kT = [[m.sb(f"b_kT{p}{n}", [P, G1, S], F32R) for p in "hl"] for n in range(2)]
        v = [[m.sb(f"b_v{p}{n}", [P, ST, G1, 2 * HD1], F32R) for p in "hl"] for n in range(2)]
        prob = [m.sb(f"b_prob{n}", [P, 3 * P]) for n in range(4)]
        pT = [[m.sb(f"b_pT{p}{n}", [P, 3 * P], F32R) for p in "hl"] for n in range(2)]
        mx = m.sb("b_mx", [P, 4, ST])
        sums = m.sb("b_sums", [P, 2, S])
        on = m.sb("b_on", [P, CD, S])
        oT = [m.sb(f"b_oT{p}", [P, CD, S], F32R) for p in "hl"]
        y = m.sb("b_y", [P, ST, D])
        st = m.sb("b_st", [P, 2, ST, 6])
        mv = m.sb("b_mv", [P, 2, ST, 2])
        nhalf = m.sb("b_nhalf", [P, ST])
        misc = [m.ps(f"b_misc{n}", [P, D]) for n in range(BANKS)]
        sc = [m.ps(f"b_sc{n}", [P, 512]) for n in range(2)]
        pTp = [m.ps(f"b_pTp{n}", [P, 512]) for n in range(2)]
        oTp = [m.ps(f"b_oTp{n}", [P, 512]) for n in range(2)]

        fw_landed = m.sem("b_fw_landed")
        consts = m.sem("b_consts")
        dve_passed = m.sem("b_dve_passed")
        prep_act = m.sem("b_prep_act")
        prep_dve = m.sem("b_prep_dve")
        prep_pe = m.sem("b_prep_pe")
        x1_landed = m.sem("b_x1_landed")
        xb_done = m.sem("b_xb_done")
        fq_chain = m.sem("b_fq_chain")
        q_done = m.sem("b_q_done")
        misc_ready = m.sem("b_misc_ready")
        misc_used = m.sem("b_misc_used")
        hi_done = m.sem("b_hi_done")
        ln_chain = [m.sem(f"b_ln_chain{n}") for n in range(2)]
        ln_var = [m.sem(f"b_ln_var{n}") for n in range(2)]
        ln_rstd = [m.sem(f"b_ln_rstd{n}") for n in range(2)]
        x2_done = m.sem("b_x2_done")
        rope_done = m.sem("b_rope_done")
        sc_ready = m.sem("b_sc_ready")
        mx_ready = m.sem("b_mx_ready")
        ex_ready = m.sem("b_ex_ready")
        pt_ready = m.sem("b_pt_ready")
        pt_hi = m.sem("b_pt_hi")
        pt_lo = m.sem("b_pt_lo")
        pv_ready = m.sem("b_pv_ready")
        o_read = m.sem("b_o_read")
        inverted = m.sem("b_inverted")
        divided = m.sem("b_divided")
        ot_hi = m.sem("b_ot_hi")
        ot_lo = m.sem("b_ot_lo")
        y_done = m.sem("b_y_done")
        stored = m.sem("b_stored")
        NLN, NFQ = 2, 4
        block = ctx.enter_context(nc.Block())

        @block.sync
        def _(sp):
            sp.sem_inc(stored, 1)
            sp.dma_start(fraw[:, :], fw_in).then_inc(fw_landed, 16)
            for dst, src in ((fbias[:, :], fb_in), (wraw[:, :, 0:D], wq_in),
                             (wraw[:, :, D:D + 2 * P], wkv_in), (wraw[:, :, D + 2 * P:], wo_in), (braw[:, :], bias_in),
                             (rope[:, :, :, :], rope_in), (mask[:, :], mask_in), (ident[:, :], ident_in),
                             (identb[:, :], identb_in)):
                sp.dma_start(dst, src).then_inc(consts, 16)
            h1_v = h1.rearrange("b (t p) d -> b p t d", p=P)
            h3_v = h3.rearrange("b (t p) d -> b p t d", p=P)

            def load(b):
                sp.wait_ge(q_done, b)
                sp.wait_ge(xb_done, b)
                sp.dma_start(x1[:, :, :], h1_v[bass.ds(b, 1)].rearrange("o p t d -> (o p) t d"))\
                  .then_inc(x1_landed, 16)

            def store(b):
                sp.wait_ge(y_done, b + 1)
                sp.dma_start(h3_v[bass.ds(b, 1)].rearrange("o p t d -> (o p) t d"), y[:, :, :]).then_inc(stored, 16)

            for b in range(3):
                load(b)
            with sp.Fori(0, B - 3) as i:
                store(i)
                load(i + 3)
            for b in range(B - 3, B):
                store(b)
            sp.wait_ge(stored, 16 * B + 1)

        @block.tensor
        def _(pe):
            pe.sem_inc(pt_ready, 4)
            pe.sem_inc(pv_ready, 1)
            pe.wait_ge(prep_act, 1)
            pe.wait_ge(prep_dve, 1)
            pe.matmul(misc[0][:, 0:1], ones[:, :], asum[:, :], start=True, stop=True).then_inc(prep_pe, 1)
            pe.wait_ge(prep_act, 8)
            pe.wait_ge(prep_dve, 6)

            def bank(seg, name):
                pe.wait_ge(misc_used, seg.unit(name))
                return misc[seg.bank(name)]

            def f_qT(seg):
                pe.wait_ge(q_done, seg.b + 2)
                for t in range(ST):
                    b = bank(seg, f"qT{t}")[:, :].bitcast(BF16)
                    for c in range(CD):
                        mm = pe.transpose(b[:, c * P:(c + 1) * P], qb[:, t, c * P:(c + 1) * P], identb[:, :])
                    mm.then_inc(misc_ready, 1)

            def f_ffn(seg):
                for t in range(ST):
                    b = bank(seg, f"ffn{t}")
                    pe.wait_ge(misc_used, seg.unit(f"qT{t}") + BANKS)
                    for c in range(CD):
                        mm = pe.matmul(b[:, :], qTb[:, t, c, :], fw[:, c, :], start=c == 0, stop=c == CD - 1)
                    mm.then_inc(misc_ready, 1)

            def f_xT(seg):
                pe.wait_ge(x2_done, seg.b + 2)
                for t in range(ST):
                    b = bank(seg, f"x{t}")
                    for c in range(CD):
                        mm = pe.transpose(b[:, c * P:(c + 1) * P], x2[1 - seg.parity][:, t, c * P:(c + 1) * P],
                                          ident[:, :])
                    mm.then_inc(misc_ready, 1)

            def project(seg, t, name, w, a, n):
                b = bank(seg, f"{name}{t}")
                pe.wait_ge(misc_used, seg.unit("x1") + BANKS)
                pe.matmul(b[:, 0:n], onesr[:, :], bqkv[:, a:a + n], start=True, stop=False)
                for c in range(CD):
                    for x in xT:
                        mm = pe.matmul(b[:, 0:n], x[:, c, t * P:(t + 1) * P], w[:, c, :], start=False,
                                       stop=c == CD - 1 and x is xT[1])
                mm.then_inc(misc_ready, 1)

            def f_q(seg, t):
                project(seg, t, "q", wq, 0, D)

            def f_kv(seg, t):
                project(seg, t, "kv", wkv, D, 2 * P)

            def f_hT(seg, t):
                pe.wait_ge(rope_done, seg.b * ST + (ST + t + 1))
                for name, src in (("tq", qr), ("tk", kr)):
                    b = bank(seg, f"{name}{t}")
                    for c in range(CD):
                        mm = pe.transpose(b[:, c * P:(c + 1) * P], src[:, t, c * P:(c + 1) * P], ident[:, :])
                    mm.then_inc(misc_ready, 1)

            def score(seg, s):
                if s == 0:
                    pe.wait_ge(misc_used, seg.unit0 + BANKS)
                pe.wait_ge(mx_ready, seg.b * NH1 + (s + 1))
                g, r = s // 4, slice(32 * (s % 4), 32 * (s % 4) + 32)
                qs, ks = qT[seg.parity], kT[seg.parity]
                mm3(pe, sc[s % 2][:, 0:P], [x[r, g, 0:P] for x in qs], [x[r, g, 0:P] for x in ks], True, True)
                mm3(pe, sc[s % 2][:, P:3 * P], [x[r, g, P:S] for x in qs], [x[r, g, :] for x in ks], True, True)\
                    .then_inc(sc_ready, 1)

            def pt(seg, s):
                pe.wait_ge(ex_ready, seg.b * NH1 + (s + 1))
                pe.wait_ge(pt_lo, seg.b * NH1 + (s + 1))
                for c in range(3):
                    mm = pe.transpose(pTp[s % 2][:, c * P:(c + 1) * P], prob[s % 4][:, c * P:(c + 1) * P], ident[:, :])
                mm.then_inc(pt_ready, 1)

            def pv(seg, s):
                pe.wait_ge(pt_lo, seg.b * NH1 + (s + 3))
                pe.wait_ge(o_read, seg.b * NH1 + (s + 1))
                p, vs, g, o = pT[s % 2], v[seg.parity], s // 4, oTp[s % 2]
                mm3(pe, o[0:2 * HD1, 0:S], [x[:, 0, g, :] for x in vs], [x[:, 0:S] for x in p], True, False)
                mm3(pe, o[0:2 * HD1, P:S], [x[:, 1, g, :] for x in vs], [x[:, S:3 * P] for x in p], False, True)\
                    .then_inc(pv_ready, 1)

            def g_out(seg, t):
                pe.wait_ge(ot_lo, seg.b * G1)
                b = bank(seg, f"out{t}")
                for c in range(CD):
                    for x in oT:
                        mm = pe.matmul(b[:, :], x[:, c, t * P:(t + 1) * P], wo[:, c, :],
                                       start=c == 0 and x is oT[0], stop=c == CD - 1 and x is oT[1])
                mm.then_inc(misc_ready, 1)

            all_segments(pe, {"f_qT": f_qT, "f_ffn": f_ffn, "f_xT": f_xT, "f_q": f_q, "f_kv": f_kv, "f_hT": f_hT,
                              "sc": score, "pt": pt, "pv": pv, "g_out": g_out})

        @block.scalar
        def _(act):
            act.sem_inc(o_read, 2)
            act.wait_ge(fw_landed, 16)
            act.activation(ftmp[:, :], fraw[:, :], ACT.Abs, accum_out=asum[:, :]).then_inc(prep_act, 1)
            act.wait_ge(consts, 144)
            act.activation(wq[:, :, :], wraw[:, :, 0:D], ACT.Copy).then_inc(prep_act, 1)
            act.activation(wkv[:, :, :], wraw[:, :, D:D + 2 * P], ACT.Copy).then_inc(prep_act, 1)
            act.activation(wo[:, :, :], wraw[:, :, D + 2 * P:], ACT.Copy).then_inc(prep_act, 1)
            act.activation(bqkv[:, :], braw[:, :], ACT.Copy).then_inc(prep_act, 1)
            act.wait_ge(prep_dve, 1)
            act.activation(onesr[:, :], ones[0:1, :], ACT.Copy).then_inc(prep_act, 2)
            for n in range(2):
                for t in range(ST):
                    block_of_ones = ones[:, :].rearrange("p (g d) -> p g d", g=G1)
                    act.activation(v[n][0][:, t, :, HD1:], block_of_ones, ACT.Copy)
                    ins = act.activation(v[n][1][:, t, :, HD1:], block_of_ones, ACT.Copy, scale=0.0)
            ins.then_inc(prep_act, 1)

            def f_xT(seg):
                for t in range(ST):
                    act.wait_ge(misc_ready, seg.unit(f"x{t}"))
                    act.activation(xT[0][:, :, t * P:(t + 1) * P],
                                   misc[seg.bank(f"x{t}")][:, :].rearrange("p (c s) -> p c s", c=CD),
                                   ACT.Copy).then_inc(hi_done, 1)

            def f_kv(seg, t):
                act.wait_ge(misc_ready, seg.unit(f"kv{t}"))
                act.activation(v[1 - seg.parity][0][:, t, :, 0:HD1],
                               misc[seg.bank(f"kv{t}")][:, P:2 * P].rearrange("p (g d) -> p g d", g=G1),
                               ACT.Copy).then_inc(hi_done, 1)

            def f_hT(seg, t):
                for name, dst in (("tq", qT), ("tk", kT)):
                    act.wait_ge(misc_ready, seg.unit(f"{name}{t}"))
                    act.activation(dst[1 - seg.parity][0][:, :, t * P:(t + 1) * P],
                                   misc[seg.bank(f"{name}{t}")][:, :].rearrange("p (c s) -> p c s", c=G1),
                                   ACT.Copy).then_inc(hi_done, 1)

            def ex(seg, s):
                act.wait_ge(mx_ready, seg.b * NH1 + (s + 3))
                for t, (a, b) in enumerate(((0, P), (P, 3 * P))):
                    ins = act.activation(prob[s % 4][:, a:b], prob[s % 4][:, a:b], ACT.Exp,
                                         bias=mx[:, s % 4, t:t + 1], scale=-1.0)
                ins.then_inc(ex_ready, 1)

            def pt(seg, s):
                act.wait_ge(pt_ready, seg.b * NH1 + (s + 5))
                act.wait_ge(pv_ready, seg.b * NH1 + s)
                act.activation(pT[s % 2][0][:, :], pTp[s % 2][:, 0:3 * P], ACT.Copy).then_inc(pt_hi, 1)

            def read(seg, s):
                g, r = s // 4, slice(HD1 * (s % 4), HD1 * (s % 4 + 1))
                act.wait_ge(pv_ready, seg.b * NH1 + (s + 2))
                if s % 4 == 0 and seg.kind != "front":
                    act.wait_ge(ot_lo, seg.b * G1 + (g + 1 - G1))
                act.activation(on[r, g, :], oTp[s % 2][0:HD1, 0:S], ACT.Copy)
                act.activation(sums[r, g % 2, :], oTp[s % 2][HD1:2 * HD1, 0:S], ACT.Copy).then_inc(o_read, 1)

            def split(seg, g):
                act.wait_ge(divided, seg.b * G1 + (g + 1))
                if g == 0 and seg.kind != "front":
                    act.wait_ge(misc_ready, seg.unit("out1"))
                act.activation(oT[0][:, g, :], on[:, g, :], ACT.Copy).then_inc(ot_hi, 1)

            all_segments(act, {"f_xT": f_xT, "f_kv": f_kv, "f_hT": f_hT, "ex": ex, "pt": pt, "read": read,
                               "split": split})

        @block.gpsimd
        def _(pool):
            pool.memset(nhalf[:, :], -0.5)
            pool.wait_ge(consts, 144)

            def f_quant(seg):
                pool.wait_ge(x1_landed, seg.b * 16 + 32)
                pool.wait_ge(x2_done, seg.b + 1)
                pool.tensor_tensor(xb[:, :, :], x1[:, :, :], fbias[:, :].unsqueeze(1).broadcast_to([P, ST, D]),
                                   ALU.add).then_inc(xb_done, 1)

            def rstd(n, images):
                pool.wait_ge(ln_var[n], images)
                pool.tensor_tensor(mv[:, n, :, 1], mv[:, n, :, 1], nhalf[:, :], ALU.pow).then_inc(ln_rstd[n], 1)

            def f_q(seg, t):
                pool.wait_ge(misc_used, seg.unit(f"q{t}") + BANKS)
                pool.tensor_tensor(qr[:, t, :], tq[0][:, :], tq[1][:, :], ALU.add)

            def f_kv(seg, t):
                pool.wait_ge(misc_used, seg.unit(f"kv{t}") + BANKS)
                shape = [P, G1, 4, HD1]
                a, b = [x[:, :].rearrange("p (g d) -> p g d", g=G1).unsqueeze(2).broadcast_to(shape) for x in tk]
                pool.tensor_tensor(kr[:, t, :].rearrange("p (g r d) -> p g r d", g=G1, r=4), a, b,
                                   ALU.add).then_inc(rope_done, 1)

            def divide(seg, g):
                pool.wait_ge(inverted, seg.b * G1 + (g + 1))
                pool.tensor_tensor(on[:, g, :], on[:, g, :], sums[:, g % 2, :], ALU.mult).then_inc(divided, 1)

            def split(seg, g):
                pool.wait_ge(ot_hi, seg.b * G1 + (g + 1))
                pool.tensor_tensor(oT[1][:, g, :], on[:, g, :], oT[0][:, g, :].bitcast(F32),
                                   ALU.subtract).then_inc(ot_lo, 1)

            all_segments(pool, {"f_quant": f_quant, "f_norm": lambda seg: rstd(0, seg.b + 2), "f_q": f_q,
                                "f_kv": f_kv, "g_norm": lambda seg: rstd(1, seg.b), "divide": divide,
                                "split": split})

        @block.vector
        def _(dve):
            dve.sem_inc(misc_used, BANKS)
            dve.sem_inc(mx_ready, 2)
            dve.sem_inc(pt_lo, 2)
            dve.memset(ones[:, :], 1.0).then_inc(prep_dve, 1)
            dve.wait_ge(prep_pe, 1)
            c = Chain(dve, prep_dve, 1)
            c(dve.tensor_scalar(alpha[:, 0:1], misc[0][:, 0:1], 1.0 / (D * D), QEPS, ALU.mult, ALU.max))
            c(dve.reciprocal(alpha[:, 1:2], alpha[:, 0:1]))
            c(dve.tensor_scalar(ftmp[:, :], fraw[:, :], alpha[:, 1:2], ROUND, ALU.mult, ALU.add))
            c(dve.tensor_scalar(ftmp[:, :], ftmp[:, :], ROUND, 1.0, ALU.subtract, ALU.min))
            c(dve.tensor_scalar(fw[:, :, :].rearrange("p c n -> p (c n)"), ftmp[:, :], -1.0, None, ALU.max))

            def f_quant(seg):
                c = Chain(dve, fq_chain, seg.b * NFQ + NFQ)
                dve.wait_ge(x1_landed, seg.b * 16 + 32)
                c(dve.tensor_reduce(am[:, :], x1[:, :, :], AX_X, ALU.max, apply_absolute_value=True))
                c(dve.tensor_scalar(am[:, :], am[:, :], QEPS, 1.0 / 127.0, ALU.max, ALU.mult))
                c(dve.reciprocal(rs[:, :], am[:, :]))
                dve.tensor_scalar(sa[:, :], am[:, :], alpha[:, 0:1], None, ALU.mult)
                for t in range(ST):
                    ins = dve.tensor_scalar(qf[:, t, :], x1[:, t, :], rs[:, t:t + 1], ROUND, ALU.mult, ALU.add)
                c(ins)
                dve.tensor_scalar(qb[:, :, :], qf[:, :, :], ROUND, 127.0, ALU.subtract, ALU.min).then_inc(q_done, 1)

            def f_qT(seg):
                for t in range(ST):
                    dve.wait_ge(misc_ready, seg.unit(f"qT{t}"))
                    dve.tensor_copy(qTb[:, t, :, :].rearrange("p c s -> p (c s)"),
                                    misc[seg.bank(f"qT{t}")][:, :].bitcast(BF16)[:, 0:D]).then_inc(misc_used, 1)

            def stats(n, images, out):
                c = Chain(dve, ln_chain[n], images * NLN - NLN)
                for t in range(ST):
                    ins = dve.bn_stats(st[:, n, t, :], out[:, t, :])
                c(ins)
                carry_wait(dve, dve_passed)
                for t in range(ST):
                    ins = dve.bn_aggr(mv[:, n, t, :], st[:, n, t, :])
                c(ins)
                dve.tensor_scalar(mv[:, n, :, 1], mv[:, n, :, 1], LN_EPS, None, ALU.add).then_inc(ln_var[n], 1)

            def norm(n, images, out, done):
                dve.wait_ge(ln_rstd[n], images)
                for t in range(ST):
                    ins = dve.tensor_scalar(out[:, t, :], out[:, t, :], mv[:, n, t, 0:1], mv[:, n, t, 1:2],
                                            ALU.subtract, ALU.mult)
                ins.then_inc(done, 1)

            def f_ffn(seg):
                x = x2[1 - seg.parity]
                dve.wait_ge(xb_done, seg.b + 2)
                for t in range(ST):
                    dve.wait_ge(misc_ready, seg.unit(f"ffn{t}"))
                    dve.scalar_tensor_tensor(x[:, t, :], misc[seg.bank(f"ffn{t}")][:, :], sa[:, t:t + 1],
                                             xb[:, t, :], ALU.mult, ALU.add).then_inc(misc_used, 1)
                dve.wait_ge(misc_used, seg.unit("ffn1") + BANKS)
                stats(0, seg.b + 2, x)

            def lo(seg, name, hi_name, out, hi, a=0, n=D):
                dve.wait_ge(hi_done, seg.hi(hi_name))
                b = misc[seg.bank(name)][:, a:a + n]
                if len(out.shape) == 3:
                    b = b.rearrange("p (c s) -> p c s", c=CD)
                dve.tensor_tensor(out, b, hi.bitcast(F32), ALU.subtract).then_inc(misc_used, 1)

            def f_xT(seg):
                for t in range(ST):
                    sl = slice(t * P, (t + 1) * P)
                    lo(seg, f"x{t}", f"x{t}", xT[1][:, :, sl], xT[0][:, :, sl])

            def turn(b, t, out, heads):
                x = b.rearrange("p (h two d) -> p h two d", two=2, d=HD1 // 2)
                t1, t2 = out
                r1 = t1[:, :].rearrange("p (h d) -> p h d", d=HD1)
                r2 = t2[:, :].rearrange("p (h two d) -> p h two d", two=2, d=HD1 // 2)
                cs = rope[:, 0, t, :].unsqueeze(1).broadcast_to([P, heads, HD1])
                half = [P, heads, HD1 // 2]
                dve.tensor_tensor(r2[:, :, 0, :], x[:, :, 1, :],
                                  rope[:, 1, t, 0:HD1 // 2].unsqueeze(1).broadcast_to(half), ALU.mult)
                dve.tensor_tensor(r2[:, :, 1, :], x[:, :, 0, :],
                                  rope[:, 1, t, HD1 // 2:].unsqueeze(1).broadcast_to(half), ALU.mult)
                return dve.tensor_tensor(r1, b.rearrange("p (h d) -> p h d", d=HD1), cs, ALU.mult)

            def f_q(seg, t):
                dve.wait_ge(rope_done, seg.b * ST + (ST + t))
                dve.wait_ge(misc_ready, seg.unit(f"q{t}"))
                turn(misc[seg.bank(f"q{t}")][:, :], t, tq, NH1).then_inc(misc_used, 1)

            def f_kv(seg, t):
                dve.wait_ge(hi_done, seg.hi(f"v{t}"))
                turn(misc[seg.bank(f"kv{t}")][:, 0:P], t, tk, G1)
                vv = [x[:, t, :, 0:HD1] for x in v[1 - seg.parity]]
                lo(seg, f"kv{t}", f"v{t}", vv[1], vv[0], P, P)

            def f_hT(seg, t):
                sl = slice(t * P, (t + 1) * P)
                for name, dst in (("tq", qT), ("tk", kT)):
                    d = dst[1 - seg.parity]
                    lo(seg, f"{name}{t}", f"{name}{t}", d[1][:, :, sl], d[0][:, :, sl])

            def maxima(seg, s):
                dve.wait_ge(sc_ready, seg.b * NH1 + (s + 1))
                dve.wait_ge(pt_ready, seg.b * NH1 + (s + 1))
                carry_wait(dve, dve_passed)
                for t, (a, b) in enumerate(((0, P), (P, 3 * P))):
                    ins = dve.tensor_tensor_reduce(out=prob[s % 4][:, a:b], in0=sc[s % 2][:, a:b],
                                                   in1=mask[:, 2 * P - (b - a):2 * P], scale=-SCALE, scalar=BIG,
                                                   op0=ALU.add, op1=ALU.min, accum_out=mx[:, s % 4, t:t + 1])
                ins.then_inc(mx_ready, 1)

            def pt(seg, s):
                dve.wait_ge(pt_hi, seg.b * NH1 + (s + 1))
                dve.tensor_tensor(pT[s % 2][1][:, :], pTp[s % 2][:, 0:3 * P], pT[s % 2][0][:, :].bitcast(F32),
                                  ALU.subtract).then_inc(pt_lo, 1)

            def divide(seg, g):
                dve.wait_ge(o_read, seg.b * NH1 + (4 * g + 6))
                dve.reciprocal(sums[:, g % 2, :], sums[:, g % 2, :]).then_inc(inverted, 1)

            def g_out(seg, t):
                if t == 0:
                    dve.wait_ge(stored, seg.b * 16 - 15)
                dve.wait_ge(misc_ready, seg.unit(f"out{t}"))
                dve.tensor_tensor(y[:, t, :], misc[seg.bank(f"out{t}")][:, :], x2[1 - seg.parity][:, t, :],
                                  ALU.add).then_inc(misc_used, 1)
                if t == ST - 1:
                    dve.wait_ge(misc_used, seg.unit("out1") + BANKS)
                    stats(1, seg.b, y)

            all_segments(dve, {"f_quant": f_quant, "f_qT": f_qT, "f_ffn": f_ffn,
                               "f_norm": lambda seg: norm(0, seg.b + 2, x2[1 - seg.parity], x2_done), "f_xT": f_xT,
                               "f_q": f_q, "f_kv": f_kv, "f_hT": f_hT, "mx": maxima, "pt": pt, "divide": divide,
                               "g_out": g_out, "g_norm": lambda seg: norm(1, seg.b, y, y_done)})


E, F, TOPK = 8, 256, 2
CF = F // P
T = B * S
TT = T // P
ROWS = 4
CHUNK = ROWS * P
SHARED = T // CHUNK
SLOTS = (TOPK * T + E * (CHUNK - 1)) // CHUNK
ITEMS = SHARED + SLOTS
NL = SLOTS * ROWS
WCOLS = 2 * CD * F + CF * D
W_PARTS = ((0, CD * F), (CD * F, 2 * CD * F), (2 * CD * F, WCOLS))
RMS_EPS = 1e-6


def experts(nc, w_in, rms_in, router_in, tri_in, small_in, tok_in, ident_in, h3, token_list, ys, out):
    with ExitStack() as octx:
        om = Memory(nc, octx)
        res = om.sb("e_res", [P, TT, D])
        place = om.sb("e_place", [P, 2, TT], mybir.dt.uint32)
        share = om.sb("e_share", [P, 2, TT])
        with ExitStack() as ctx:
            expert_items(nc, Memory(nc, ctx), res, place, share, w_in, rms_in, router_in, tri_in, small_in, tok_in,
                         ident_in, h3, token_list, ys)
        with ExitStack() as ctx:
            combine(nc, Memory(nc, ctx), res, place, share, ys, out)


class Item:

    def __init__(self, n, slot, parity, n_static=None):
        self.n, self.slot, self.parity = n, slot, parity
        self.j = n - (SHARED - 1) if slot else 0
        self.wbuf = (parity + 1) % 2 if slot else 0


class Chunk:

    def __init__(self, k, parity, pair):
        self.k, self.parity, self.pair = k, parity, pair


def chunk_steps(eng, h):

    def step(k, parity, pair):
        fixed = isinstance(k, int)
        for name, ahead in (("norm", 1), ("tiles", 0), ("squares", 2), ("logits", -1), ("turned", -2)):
            if name in h and not (fixed and not 0 <= k + ahead < SHARED):
                p = (parity + ahead) % 2
                h[name](Chunk(k + ahead, p, pair + (parity + ahead - p) // 2))

    for name, k in (("squares", 0), ("norm", 0), ("squares", 1)):
        if name in h:
            h[name](Chunk(k, k, 0))
    step(0, 0, 0)
    step(1, 1, 0)
    with eng.Fori(0, (SHARED - 4) // 2) as i:
        step(i * 2 + 2, 0, i + 1)
        step(i * 2 + 3, 1, i + 1)
    for k in range(SHARED - 2, SHARED + 2):
        step(k, k % 2, k // 2)


def item_segments(eng, h):

    def call(name, *args):
        if name in h:
            h[name](*args)

    def segment(n, parity, slots):
        before, this, after, next_but_one = slots
        it = Item(n, this, parity)
        if after is not None:
            call("norm", Item(n + 1, after, 1 - parity))
        call("gu", it, 0)
        if after is not None:
            call("inputs", Item(n + 1, after, 1 - parity))
        if before is not None:
            call("down", Item(n - 1, before, 1 - parity))
        if after:
            call("weights", Item(n + 1, True, 1 - parity))
        if next_but_one:
            call("squares", Item(n + 2, True, parity))
        call("gu", it, 1)

    def fixed(n):
        segment(n, n % 2, [None if not 0 <= k < ITEMS else k >= SHARED for k in range(n - 1, n + 3)])

    call("weights", Item(0, False, 0))
    call("norm", Item(0, False, 0))
    call("inputs", Item(0, False, 0))
    fixed(0)
    fixed(1)
    with eng.Fori(0, (SHARED - 4) // 2) as i:
        segment(i * 2 + 2, 0, [False] * 4)
        segment(i * 2 + 3, 1, [False] * 4)
    for n in range(SHARED - 2, SHARED + 2):
        fixed(n)
    pairs = (SLOTS - 4) // 2
    with eng.Fori(0, pairs) as i:
        segment(i * 2 + (SHARED + 2), 0, [True] * 4)
        segment(i * 2 + (SHARED + 3), 1, [True] * 4)
    for n in range(SHARED + 2 + 2 * pairs, ITEMS):
        fixed(n)
    call("down", Item(ITEMS - 1, True, (ITEMS - 1) % 2))


def expert_items(nc, m, res, place, share, w_in, rms_in, router_in, tri_in, small_in, tok_in, ident_in, h3,
                 token_list, ys):
    U32 = mybir.dt.uint32
    ident = m.sb("e_ident", [P, P])
    rms = m.sb("e_rms", [P, D])
    rraw = m.sb("e_rraw", [P, CD, E])
    router = [m.sb(f"e_router{p}", [P, CD, E], F32R) for p in "hl"]
    tri = m.sb("e_tri", [P, 2, P])
    small = m.sb("e_small", [P, E + SLOTS + 1])
    tok = m.sb("e_tok", [P, TT], U32)
    xin = m.sb("e_xin", [P, ROWS, D])
    ss = [m.sb(f"e_ss{n}", [P, ROWS]) for n in range(3)]
    scale = m.sb("e_scale", [P, TT])
    xT = [[m.sb(f"e_xT{p}{n}", [P, CD, CHUNK], F32R) for p in "hl"] for n in range(2)]
    aT = [[m.sb(f"e_aT{p}{n}", [P, CF, CHUNK], F32R) for p in "hl"] for n in range(2)]
    sg = [m.sb(f"e_sg{f}", [P, CHUNK]) for f in range(CF)]
    lt = sg[0][0:E, :]
    wraw = m.sb("e_wraw", [P, WCOLS])
    wb = [[m.sb(f"e_w{p}{n}", [P, WCOLS], F32R) for p in "hl"] for n in range(2)]
    yb = m.sb("e_yb", [P, ROWS, D])
    xc = [xin, yb]
    lg = m.sb("e_lg", [P, TT, E])
    top = m.sb("e_top", [P, TT, 8])
    topi = m.sb("e_topi", [P, TT, 8], U32)
    oh = m.sb("e_oh", [P, 2, TT, E])
    mm_ = m.sb("e_mm", [P, TT, E])
    cum = m.sb("e_cum", [P, E, TT])
    tot = m.sb("e_tot", [P, E, TT])
    blk = m.sb("e_blk", [P, 4, E])
    fl = m.sb("e_fl", [P, 2, TT])
    fj = m.sb("e_fj", [P, 2, TT])
    addr = m.sb("e_addr", [P, 2, TT], U32)
    own = m.sb("e_own", [1, SLOTS, E])
    ownf = m.sb("e_ownf", [1, SLOTS])
    owner = m.sb("e_owner", [1, SLOTS], I32)
    idx = m.sb("e_idx", [P, NL], U32)
    idx4 = m.sb("e_idx4", [P, ROWS], U32)
    tp = [m.ps(f"e_tp{n}", [P, D]) for n in range(2)]
    gu = [m.ps(f"e_gu{n}", [P, CHUNK]) for n in range(4)]
    dn = [m.ps(f"e_dn{n}", [P, D]) for n in range(2)]

    consts = m.sem("e_consts")
    pool_passed = m.sem("e_pool_passed")
    pe_passed = m.sem("e_pe_passed")
    res_landed = [m.sem(f"e_res_landed{n}") for n in range(2)]
    ss_done = m.sem("e_ss_done")
    ms_done = m.sem("e_ms_done")
    rs_done = m.sem("e_rs_done")
    c_normed = m.sem("e_c_normed")
    r_prep = m.sem("e_r_prep")
    c_t = m.sem("e_c_t")
    c_hi = m.sem("e_c_hi")
    c_lo = m.sem("e_c_lo")
    c_lt = m.sem("e_c_lt")
    lt_read = m.sem("e_lt_read")
    c_lg = m.sem("e_c_lg")
    c_lgd = m.sem("e_c_lgd")
    rt = m.sem("e_rt")
    rt_mm = m.sem("e_rt_mm")
    rt_pe = m.sem("e_rt_pe")
    rt_exp = m.sem("e_rt_exp")
    rt_done = m.sem("e_rt_done")
    zeroed = m.sem("e_zeroed")
    listed = m.sem("e_listed")
    idx_landed = m.sem("e_idx_landed")
    idx_copied = m.sem("e_idx_copied")
    sq_done = m.sem("e_sq_done")
    ms2_done = m.sem("e_ms2_done")
    rs2_done = m.sem("e_rs2_done")
    x_normed = m.sem("e_x_normed")
    g_landed = m.sem("e_g_landed")
    t_ready = m.sem("e_t_ready")
    x_hi = m.sem("e_x_hi")
    x_lo = m.sem("e_x_lo")
    gu_ready = m.sem("e_gu_ready")
    silu_done = m.sem("e_silu_done")
    mul_done = m.sem("e_mul_done")
    a_hi = m.sem("e_a_hi")
    a_lo = m.sem("e_a_lo")
    d_ready = m.sem("e_d_ready")
    d_used = m.sem("e_d_used")
    y_stored = m.sem("e_y_stored")
    raw_landed = m.sem("e_raw_landed")
    w_hi = m.sem("e_w_hi")
    w_lo = m.sem("e_w_lo")
    block = m.ctx.enter_context(nc.Block())

    def gate(w, c, f):
        return w[:, c * F + f * P:c * F + f * P + P]

    def up(w, c, f):
        return w[:, CD * F + c * F + f * P:CD * F + c * F + f * P + P]

    def down_w(w, f):
        return w[:, 2 * CD * F + f * D:2 * CD * F + (f + 1) * D]

    @block.sync
    def _(sp):
        for dst, src in ((ident[:, :], ident_in), (rms[:, :], rms_in), (rraw[:, :, :], router_in),
                         (tri[:, :, :], tri_in), (small[:, :], small_in), (tok[:, :], tok_in)):
            sp.dma_start(dst, src).then_inc(consts, 16)
        h3_v = h3.rearrange("b (t p) d -> p (b t) d", p=P)

        def load_res(k, par):
            sp.dma_start(res[:, bass.ds(k * ROWS, ROWS), :], h3_v[:, bass.ds(k * ROWS, ROWS), :])\
              .then_inc(res_landed[par], 16)

        load_res(0, 0)
        load_res(1, 1)
        sp.dma_start(wraw[:, :], w_in[E]).then_inc(raw_landed, 16)
        with sp.Fori(0, SHARED // 2 - 1) as i:
            for par in range(2):
                sp.wait_ge(ss_done, i * 2 + (par + 1))
                load_res(i * 2 + (par + 2), par)

        def load_w(j, s):
            sp.wait_ge(w_lo, j * 3)
            e = sp.value_load(owner[0:1, bass.ds(s, 1)], min_val=0, max_val=E - 1)
            sp.dma_start(wraw[:, :], w_in[bass.ds(e, 1)].rearrange("o p n -> (o p) n")).then_inc(raw_landed, 16)

        def after_down(it):
            if it.slot:
                sp.wait_ge(d_used, it.n * 4 + 6)
                s = it.n - SHARED
                sp.dma_start(ys[bass.ds(s, 1)].rearrange("o p r d -> (o p) r d"), yb[:, :, :]).then_inc(y_stored, 16)

        def after_weights(it):
            if isinstance(it.n, int) and (it.n == 0 or it.n == ITEMS - 1):
                if it.n == 0:
                    sp.wait_ge(rt_done, 1)
                    load_w(1, 0)
                return
            load_w(it.j + 1, it.n + 1 - SHARED)

        item_segments(sp, {"down": after_down, "weights": after_weights})
        sp.wait_ge(y_stored, 16 * SLOTS)

    @block.tensor
    def _(pe):
        pe.sem_inc(c_t, 2)
        pe.wait_ge(consts, 96)
        pe.wait_ge(r_prep, 2)
        pe.sem_inc(c_lg, 1)

        def tiles(ch):
            pe.wait_ge(c_normed, ch.k + 1)
            for t in range(ROWS):
                pe.wait_ge(c_lo, ch.k * ROWS + (t + 1))
                for c in range(CD):
                    mm = pe.transpose(tp[t % 2][:, c * P:(c + 1) * P], xc[ch.parity][:, t, c * P:(c + 1) * P],
                                      ident[:, :])
                mm.then_inc(c_t, 1)

        def logits(ch):
            pe.wait_ge(c_lo, ch.k * ROWS + (ROWS + 2))
            pe.wait_ge(lt_read, ch.k + 1)
            for c in range(CD):
                mm = mm3(pe, dn[0][0:E, :], [x[:, c, :] for x in router], [x[:, c, :] for x in xT[ch.parity]],
                         c == 0, c == CD - 1)
            mm.then_inc(c_lt, 1)

        def turned(ch):
            pe.wait_ge(lt_read, ch.k + 2)
            pe.wait_ge(c_lgd, ch.k + 1)
            carry_wait(pe, pe_passed)
            for t in range(ROWS):
                mm = pe.transpose(dn[1][:, t * E:(t + 1) * E], lt[:, t * P:(t + 1) * P], ident[0:E, 0:E])
            mm.then_inc(c_lg, 1)

        chunk_steps(pe, {"tiles": tiles, "logits": logits, "turned": turned})
        pe.wait_ge(rt_mm, 1)
        flat = mm_[:, :, :].rearrange("p t e -> p (t e)")
        pe.matmul(dn[0][:, 0:TT * E], tri[:, 0, :], flat, start=True, stop=True)
        pe.matmul(dn[1][:, 0:TT * E], tri[:, 1, :], flat, start=True, stop=True).then_inc(rt_pe, 1)

        def inputs(it):
            pe.wait_ge(x_normed, it.n + 1)
            for t in range(ROWS):
                pe.wait_ge(x_lo, it.n * 4 + (t + 1))
                for c in range(CD):
                    mm = pe.transpose(tp[t % 2][:, c * P:(c + 1) * P], xin[:, t, c * P:(c + 1) * P], ident[:, :])
                mm.then_inc(t_ready, 1)

        def gate_up(it, f):
            if f == 0:
                pe.wait_ge(x_lo, it.n * 4 + 6)
                pe.wait_ge(w_lo, it.j * 3 + 2)
            pe.wait_ge(mul_done, it.n * 2 + (f + 1))
            x, w = xT[it.parity], wb[it.wbuf]
            for k, part in enumerate((gate, up)):
                for c in range(CD):
                    mm = mm3(pe, gu[2 * f + k][:, :], [part(y, c, f) for y in w], [y[:, c, :] for y in x], c == 0,
                             c == CD - 1)
                mm.then_inc(gu_ready, 1)

        def down(it):
            pe.wait_ge(a_lo, it.n * 2 + 2)
            pe.wait_ge(w_lo, it.j * 3 + 3)
            a, w = aT[it.parity], wb[it.wbuf]
            for t in range(ROWS):
                pe.wait_ge(d_used, it.n * 4 + (t + 1))
                for f in range(CF):
                    mm = mm3(pe, dn[t % 2][:, :], [y[:, f, t * P:(t + 1) * P] for y in a], [down_w(y, f) for y in w],
                             f == 0, f == CF - 1)
                mm.then_inc(d_ready, 1)

        pe.wait_ge(rt_done, 1)
        item_segments(pe, {"inputs": inputs, "gu": gate_up, "down": down})

    @block.scalar
    def _(act):
        act.wait_ge(consts, 96)
        act.activation(router[0][:, :, :], rraw[:, :, :], ACT.Copy).then_inc(r_prep, 1)
        act.sem_inc(lt_read, 1)

        def squares(ch):
            act.wait_ge(res_landed[ch.parity], ch.pair * 16 + 16)
            if not isinstance(ch.k, int) or ch.k > 1:
                act.wait_ge(rs_done, ch.k - 1)
            for t in range(ROWS):
                ins = act.activation(aT[ch.parity][t // 2][:, t % 2, :],
                                     res[:, bass.ds(ch.k * ROWS + t, 1), :].rearrange("p o d -> p (o d)"),
                                     ACT.Square, accum_out=ss[ch.parity][:, t:t + 1])
            ins.then_inc(ss_done, 1)

        def tiles(ch):
            if not isinstance(ch.k, int) or ch.k > 1:
                act.wait_ge(c_lt, ch.k - 1)
            for t in range(ROWS):
                act.wait_ge(c_t, ch.k * ROWS + (t + 3))
                act.activation(xT[ch.parity][0][:, :, t * P:(t + 1) * P],
                               tp[t % 2][:, :].rearrange("p (c s) -> p c s", c=CD), ACT.Copy).then_inc(c_hi, 1)

        def logits(ch):
            act.wait_ge(c_lt, ch.k + 1)
            act.wait_ge(c_lg, ch.k + 1)
            act.activation(lt, dn[0][0:E, :], ACT.Copy).then_inc(lt_read, 1)

        chunk_steps(act, {"squares": squares, "tiles": tiles, "logits": logits})
        act.wait_ge(rt, 2)
        act.activation(share[:, 1, :], fl[:, 0, :], ACT.Exp).then_inc(rt_exp, 1)

        def inputs(it):
            for t in range(ROWS):
                act.wait_ge(t_ready, it.n * 4 + (t + 1))
                if t == 0 and not (isinstance(it.n, int) and it.n < 1):
                    act.wait_ge(gu_ready, it.n * 4 - 4)
                act.activation(xT[it.parity][0][:, :, t * P:(t + 1) * P],
                               tp[t % 2][:, :].rearrange("p (c s) -> p c s", c=CD), ACT.Copy).then_inc(x_hi, 1)

        def squares_of_rows(it):
            act.wait_ge(g_landed, it.n * (16 * ROWS) - (SHARED - 1) * (16 * ROWS))
            act.wait_ge(x_normed, it.n)
            act.wait_ge(d_ready, it.n * 4 - 8)
            for t in range(ROWS):
                ins = act.activation(aT[1 - it.parity][t // 2][:, t % 2, :], xin[:, t, :], ACT.Square,
                                     accum_out=ss[2][:, t:t + 1])
            ins.then_inc(sq_done, 1)

        def gate_up(it, f):
            act.wait_ge(gu_ready, it.n * 4 + (2 * f + 1))
            if not (isinstance(it.n, int) and it.n < 1):
                act.wait_ge(a_lo, it.n * 2 + (f - 1))
            act.activation(sg[f][:, :], gu[2 * f][:, :], ACT.Silu).then_inc(silu_done, 1)
            act.wait_ge(mul_done, it.n * 2 + (f + 3))
            if f == 0 and not (isinstance(it.n, int) and it.n < 1):
                act.wait_ge(d_ready, it.n * 4 - 4)
            act.activation(aT[it.parity][0][:, f, :], sg[f][:, :], ACT.Copy).then_inc(a_hi, 1)

        def weights(it):
            act.wait_ge(raw_landed, it.j * 16 + 16)
            if it.slot:
                act.wait_ge(d_ready, it.n * 4 - 4)
            for a, b in W_PARTS:
                act.activation(wb[it.wbuf][0][:, a:b], wraw[:, a:b], ACT.Copy).then_inc(w_hi, 1)

        item_segments(act, {"squares": squares_of_rows, "inputs": inputs, "gu": gate_up, "weights": weights})

    @block.gpsimd
    def _(pool):
        pool.wait_ge(consts, 96)
        pool.memset(idx[:, :], 0).then_inc(zeroed, 1)
        pool.wait_ge(zeroed, 1)
        list_v = token_list.rearrange("(p n) o -> p (n o)", p=P)
        pool.dma_start(list_v, idx[:, :]).then_inc(listed, 16)
        nh = small[:, E + SLOTS:E + SLOTS + 1].broadcast_to([P, ROWS])
        rows = h3.rearrange("b s d -> (b s) d")

        def power(ch):
            x = ss[ch.parity]
            pool.wait_ge(ss_done, ch.k + 1)
            carry_wait(pool, pool_passed)
            pool.tensor_scalar(x[:, :], x[:, :], 1.0 / D, RMS_EPS, ALU.mult, ALU.add).then_inc(ms_done, 1)
            pool.wait_ge(ms_done, ch.k + 1)
            pool.tensor_tensor(scale[:, bass.ds(ch.k * ROWS, ROWS)], x[:, :], nh, ALU.pow).then_inc(rs_done, 1)

        chunk_steps(pool, {"squares": power})
        pool.wait_ge(rt_done, 1)
        pool.wait_ge(listed, 16)
        for t in range(TT):
            for k in range(2):
                pool.indirect_dma_start(token_list, bass.IndirectOffsetOnAxis(addr[:, k, t:t + 1], 0),
                                        tok[:, t:t + 1], None).then_inc(listed, 16)
        pool.wait_ge(listed, 16 + 16 * 2 * TT)
        pool.dma_start(idx[:, :], list_v).then_inc(idx_landed, 16)
        pool.wait_ge(idx_landed, 16)

        def gather(n):
            s = n - SHARED
            pool.tensor_copy(idx4[:, :], idx[:, bass.ds(s * ROWS, ROWS)]).then_inc(idx_copied, 1)
            pool.wait_ge(idx_copied, s + 1)
            carry_wait(pool, pool_passed)
            for r in range(ROWS):
                pool.indirect_dma_start(xin[:, r, :], None, rows, bass.IndirectOffsetOnAxis(idx4[:, r:r + 1], 0))\
                    .then_inc(g_landed, 16)

        def after_inputs(it):
            if isinstance(it.n, int) and (it.n < SHARED - 1 or it.n == ITEMS - 1) or not it.slot and not isinstance(
                    it.n, int):
                return
            pool.wait_ge(t_ready, it.n * 4 + 4)
            gather(it.n + 1)

        def power_of_rows(it):
            x = ss[2]
            pool.wait_ge(sq_done, it.n - (SHARED - 1))
            carry_wait(pool, pool_passed)
            pool.tensor_scalar(x[:, :], x[:, :], 1.0 / D, RMS_EPS, ALU.mult, ALU.add).then_inc(ms2_done, 1)
            pool.wait_ge(ms2_done, it.n - (SHARED - 1))
            pool.tensor_tensor(x[:, :], x[:, :], nh, ALU.pow).then_inc(rs2_done, 1)

        item_segments(pool, {"squares": power_of_rows, "inputs": after_inputs})

    @block.vector
    def _(dve):
        dve.sem_inc(c_lo, 2)
        dve.sem_inc(c_lgd, 1)
        dve.sem_inc(x_lo, 2)
        dve.sem_inc(mul_done, 2)
        dve.sem_inc(d_used, 2)
        dve.wait_ge(consts, 96)
        dve.wait_ge(r_prep, 1)
        dve.tensor_tensor(router[1][:, :, :], rraw[:, :, :], router[0][:, :, :].bitcast(F32), ALU.subtract)\
           .then_inc(r_prep, 1)

        def normalise(k, out):
            for t in range(ROWS):
                ins = dve.scalar_tensor_tensor(out[:, t, :], res[:, bass.ds(k * ROWS + t, 1), :].rearrange(
                    "p o d -> p (o d)"), scale[:, bass.ds(k * ROWS + t, 1)], rms[:, :], ALU.mult, ALU.mult)
            return ins

        def norm(ch):
            dve.wait_ge(rs_done, ch.k + 1)
            if not isinstance(ch.k, int) or ch.k > 0:
                dve.wait_ge(c_t, ch.k * ROWS - (ROWS - 2))
            normalise(ch.k, xc[ch.parity]).then_inc(c_normed, 1)

        def tiles(ch):
            x = xT[ch.parity]
            for t in range(ROWS):
                sl = slice(t * P, (t + 1) * P)
                dve.wait_ge(c_hi, ch.k * ROWS + (t + 1))
                dve.tensor_tensor(x[1][:, :, sl], tp[t % 2][:, :].rearrange("p (c s) -> p c s", c=CD),
                                  x[0][:, :, sl].bitcast(F32), ALU.subtract).then_inc(c_lo, 1)

        def turned(ch):
            dve.wait_ge(c_lg, ch.k + 2)
            dve.tensor_copy(lg[:, bass.ds(ch.k * ROWS, ROWS), :],
                            dn[1][:, 0:ROWS * E].rearrange("p (t e) -> p t e", e=E)).then_inc(c_lgd, 1)

        chunk_steps(dve, {"norm": norm, "tiles": tiles, "turned": turned})
        dve.wait_ge(c_lgd, SHARED + 1)
        for t in range(TT):
            ins = dve.max(top[:, t, :], lg[:, t, :])
        c = Chain(dve, rt)
        c(ins)
        for t in range(TT):
            dve.max_index(topi[:, t, :], top[:, t, :], lg[:, t, :])
        c(dve.tensor_tensor(fl[:, 0, :], top[:, :, 1], top[:, :, 0], ALU.subtract))
        iota = small[:, 0:E].unsqueeze(1).broadcast_to([P, TT, E])
        for k in range(2):
            ins = dve.tensor_copy(fj[:, k, :], topi[:, :, k])
        c(ins)
        for k in range(2):
            ins = dve.tensor_tensor(oh[:, k, :, :], fj[:, k, :].unsqueeze(2).broadcast_to([P, TT, E]), iota,
                                    ALU.is_equal)
        c(ins)
        dve.tensor_tensor(mm_[:, :, :], oh[:, 0, :, :], oh[:, 1, :, :], ALU.add).then_inc(rt_mm, 1)
        dve.wait_ge(rt_exp, 1)
        c(dve.tensor_scalar(share[:, 0, :], share[:, 1, :], 1.0, None, ALU.add))
        c(dve.reciprocal(share[:, 0, :], share[:, 0, :]))
        c(dve.tensor_tensor(share[:, 1, :], share[:, 1, :], share[:, 0, :], ALU.mult))
        dve.wait_ge(rt_pe, 1)
        c(dve.tensor_copy(tot[:, :, :], dn[1][:, 0:TT * E].rearrange("p (t e) -> p e t", e=E)))
        for e in range(E):
            ins = dve.tensor_tensor_scan(cum[:, e, :], tri[:, 1, 0:TT], tot[:, e, :], 0.0, ALU.mult, ALU.add)
        c(ins)
        c(dve.tensor_copy(blk[:, 0, :], cum[:, :, TT - 1]))
        c(dve.tensor_tensor(cum[:, :, :], cum[:, :, :], tot[:, :, :], ALU.subtract))
        c(dve.tensor_scalar(blk[:, 1, :], blk[:, 0, :], 1.0 / CHUNK, (CHUNK - 1.0) / (2 * CHUNK), ALU.mult, ALU.add))
        c(dve.tensor_scalar(blk[:, 1, :], blk[:, 1, :], ROUND, None, ALU.add))
        c(dve.tensor_scalar(blk[:, 1, :], blk[:, 1, :], ROUND, None, ALU.subtract))
        c(dve.tensor_tensor_scan(blk[:, 2, :], tri[:, 1, 0:E], blk[:, 1, :], 0.0, ALU.mult, ALU.add))
        c(dve.tensor_tensor(blk[:, 3, :], blk[:, 2, :], blk[:, 1, :], ALU.subtract))
        c(dve.tensor_scalar(blk[:, 3, :], blk[:, 3, :], float(CHUNK), None, ALU.mult))
        pos = lg
        c(dve.tensor_tensor(pos[:, :, :], dn[0][:, 0:TT * E].rearrange("p (t e) -> p t e", e=E),
                            cum[:, :, :].rearrange("p e t -> p t e"), ALU.add))
        c(dve.tensor_tensor(pos[:, :, :], pos[:, :, :], blk[:, 3, :].unsqueeze(1).broadcast_to([P, TT, E]), ALU.add))
        for k in range(2):
            ins = dve.tensor_tensor(oh[:, k, :, :], oh[:, k, :, :], pos[:, :, :], ALU.mult)
        c(ins)
        c(dve.tensor_reduce(fl[:, :, :], oh[:, :, :, :], AX_X, ALU.add))
        c(dve.tensor_scalar(fj[:, :, :], fl[:, :, :], 1.0 / P, -(P - 1.0) / (2 * P), ALU.mult, ALU.add))
        c(dve.tensor_scalar(fj[:, :, :], fj[:, :, :], ROUND, None, ALU.add))
        c(dve.tensor_scalar(fj[:, :, :], fj[:, :, :], ROUND, None, ALU.subtract))
        fk = tot[:, 0:2, :]
        c(dve.scalar_tensor_tensor(fk, fj[:, :, :], -float(P), fl[:, :, :], ALU.mult, ALU.add))
        c(dve.scalar_tensor_tensor(addr[:, :, :], fk, float(NL), fj[:, :, :], ALU.mult, ALU.add))
        fs = tot[:, 2:4, :]
        c(dve.tensor_scalar(fs, fj[:, :, :], 1.0 / ROWS, -(ROWS - 1.0) / (2 * ROWS), ALU.mult, ALU.add))
        c(dve.tensor_scalar(fs, fs, ROUND, None, ALU.add))
        c(dve.tensor_scalar(fs, fs, ROUND, None, ALU.subtract))
        c(dve.scalar_tensor_tensor(fj[:, :, :], fs, float(P * ROWS - ROWS), fj[:, :, :], ALU.mult, ALU.add))
        c(dve.scalar_tensor_tensor(place[:, :, :], fk, float(ROWS), fj[:, :, :], ALU.mult, ALU.add))
        sl = small[0:1, E:E + SLOTS].unsqueeze(2).broadcast_to([1, SLOTS, E])
        c(dve.tensor_tensor(own[:, :, :], blk[0:1, 2, :].unsqueeze(1).broadcast_to([1, SLOTS, E]), sl, ALU.is_le))
        c(dve.tensor_reduce(ownf[:, :], own[:, :, :], AX_X, ALU.add))
        dve.tensor_scalar(owner[:, :], ownf[:, :], E - 1.0, None, ALU.min).then_inc(rt_done, 1)

        def inputs(it):
            for t in range(ROWS):
                sl = slice(t * P, (t + 1) * P)
                dve.wait_ge(x_hi, it.n * 4 + (t + 1))
                x = xT[it.parity]
                dve.tensor_tensor(x[1][:, :, sl], tp[t % 2][:, :].rearrange("p (c s) -> p c s", c=CD),
                                  x[0][:, :, sl].bitcast(F32), ALU.subtract).then_inc(x_lo, 1)

        def gate_up(it, f):
            dve.wait_ge(silu_done, it.n * 2 + (f + 1))
            dve.wait_ge(gu_ready, it.n * 4 + (2 * f + 2))
            dve.tensor_tensor(sg[f][:, :], sg[f][:, :], gu[2 * f + 1][:, :], ALU.mult).then_inc(mul_done, 1)
            dve.wait_ge(a_hi, it.n * 2 + (f + 1))
            a = aT[it.parity]
            dve.tensor_tensor(a[1][:, f, :], sg[f][:, :], a[0][:, f, :].bitcast(F32), ALU.subtract).then_inc(a_lo, 1)

        def down(it):
            if it.slot:
                dve.wait_ge(y_stored, it.n * 16 - 16 * SHARED)
            for t in range(ROWS):
                dve.wait_ge(d_ready, it.n * 4 + (t + 1))
                if it.slot:
                    dve.tensor_copy(yb[:, t, :], dn[t % 2][:, :]).then_inc(d_used, 1)
                else:
                    r = res[:, bass.ds(it.n * ROWS + t, 1), :].rearrange("p o d -> p (o d)")
                    dve.tensor_tensor(r, r, dn[t % 2][:, :], ALU.add).then_inc(d_used, 1)

        def weights(it):
            for k, (a, b) in enumerate(W_PARTS):
                dve.wait_ge(w_hi, it.j * 3 + (k + 1))
                w = wb[it.wbuf]
                dve.tensor_tensor(w[1][:, a:b], wraw[:, a:b], w[0][:, a:b].bitcast(F32), ALU.subtract)\
                   .then_inc(w_lo, 1)

        def norm_item(it):
            if it.slot:
                dve.wait_ge(rs2_done, it.n - (SHARED - 1))
                for t in range(ROWS):
                    ins = dve.scalar_tensor_tensor(xin[:, t, :], xin[:, t, :], ss[2][:, t:t + 1], rms[:, :],
                                                   ALU.mult, ALU.mult)
            else:
                if isinstance(it.n, int) and it.n == 0:
                    dve.wait_ge(c_t, SHARED * ROWS + 2)
                else:
                    dve.wait_ge(t_ready, it.n * 4)
                ins = normalise(it.n, xin)
            ins.then_inc(x_normed, 1)

        item_segments(dve, {"norm": norm_item, "inputs": inputs, "gu": gate_up, "down": down, "weights": weights})


def combine(nc, m, res, place, share, ys, out):
    GROUP = 4
    NB = 2 * GROUP
    g = [[m.sb(f"f_g{k}{n}", [P, D]) for k in range(2)] for n in range(NB)]
    pl = [m.sb(f"f_pl{n}", [P, 2], mybir.dt.uint32) for n in range(NB)]
    st = m.sb("f_st", [P, NB, 6])
    mv = m.sb("f_mv", [P, NB, 2])
    nhalf = m.sb("f_nhalf", [P, GROUP])
    nmr = m.sb("f_nmr", [P, NB])
    o = m.sb("f_o", [P, NB, D])
    copied = m.sem("f_copied")
    dve_passed = m.sem("f_dve_passed")
    pool_passed = m.sem("f_pool_passed")
    landed = [m.sem(f"f_landed{n}") for n in range(2)]
    chain = m.sem("f_chain")
    var = m.sem("f_var")
    rstd = m.sem("f_rstd")
    shift = m.sem("f_shift")
    normed = m.sem("f_normed")
    stored = [m.sem(f"f_stored{n}") for n in range(2)]
    rows = ys.rearrange("s p r d -> (s p r) d")
    out_v = out.rearrange("b (t p) d -> p (b t) d", p=P)
    block = m.ctx.enter_context(nc.Block())

    def groups(eng, body):
        with eng.Fori(0, TT // NB - 1) as i:
            body(i, 0, True)
            body(i, 1, True)
        body(TT // NB - 1, 0, False)
        body(TT // NB - 1, 1, False)

    @block.gpsimd
    def _(pool):
        pool.memset(nhalf[:, :], -0.5).then_inc(copied, 1)
        pool.wait_ge(copied, 1)

        def gather(t, b):
            pool.tensor_copy(pl[b][:, :], place[:, :, bass.ds(t, 1)].rearrange("p k o -> p (k o)")).then_inc(copied, 1)
            pool.wait_ge(copied, t + 2)
            carry_wait(pool, pool_passed)
            for k in range(2):
                pool.indirect_dma_start(g[b][k][:, :], None, rows, bass.IndirectOffsetOnAxis(pl[b][:, k:k + 1], 0))\
                    .then_inc(landed[b // GROUP], 16)

        def body(i, half, more):
            if more:
                pool.wait_ge(chain, i * 8 + (half * 4 + 2))
                for b in range(half * GROUP, (half + 1) * GROUP):
                    gather(i * NB + (NB + b), b)
            m_, v_ = [mv[:, half * GROUP:(half + 1) * GROUP, k] for k in range(2)]
            pool.wait_ge(var, i * 2 + (half + 1))
            pool.tensor_tensor(v_, v_, nhalf[:, :], ALU.pow).then_inc(rstd, 1)
            pool.wait_ge(rstd, i * 2 + (half + 1))
            pool.tensor_tensor(nmr[:, half * GROUP:(half + 1) * GROUP], m_, v_, ALU.mult).then_inc(shift, 1)

        for b in range(NB):
            gather(b, b)
        groups(pool, body)

    @block.vector
    def _(dve):
        def body(i, half, more):
            c = Chain(dve, chain, i * 8 + half * 4)
            bufs = range(half * GROUP, (half + 1) * GROUP)
            group = slice(half * GROUP, (half + 1) * GROUP)
            dve.wait_ge(landed[half], i * (GROUP * 32) + GROUP * 32)
            for b in bufs:
                t = i * NB + b
                ins = dve.scalar_tensor_tensor(g[b][0][:, :], g[b][0][:, :], share[:, 0, bass.ds(t, 1)],
                                               res[:, bass.ds(t, 1), :].rearrange("p o d -> p (o d)"), ALU.mult,
                                               ALU.add)
            c(ins)
            dve.wait_ge(stored[half], i * 16 + 1)
            for b in bufs:
                ins = dve.scalar_tensor_tensor(o[:, b, :], g[b][1][:, :], share[:, 1, bass.ds(i * NB + b, 1)],
                                               g[b][0][:, :], ALU.mult, ALU.add)
            c(ins)
            for b in bufs:
                ins = dve.bn_stats(st[:, b, :], o[:, b, :])
            c(ins)
            carry_wait(dve, dve_passed)
            for b in bufs:
                ins = dve.bn_aggr(mv[:, b, :], st[:, b, :])
            c(ins)
            dve.tensor_scalar(mv[:, group, 0], mv[:, group, 0], -1.0, None, ALU.mult)
            dve.tensor_scalar(mv[:, group, 1], mv[:, group, 1], LN_EPS, None, ALU.add).then_inc(var, 1)

        groups(dve, body)

    @block.scalar
    def _(act):
        def body(i, half, more):
            act.wait_ge(shift, i * 2 + (half + 1))
            for b in range(half * GROUP, (half + 1) * GROUP):
                act.activation(o[:, b, :], o[:, b, :], ACT.Identity, bias=nmr[:, b:b + 1], scale=mv[:, b, 1:2])\
                   .then_inc(normed, 1)

        groups(act, body)

    @block.sync
    def _(sp):
        for half in range(2):
            sp.sem_inc(stored[half], 1)

        def body(i, half, more):
            sp.wait_ge(normed, i * NB + (half + 1) * GROUP)
            sp.dma_start(out_v[:, bass.ds(i * NB + half * GROUP, GROUP), :], o[:, half * GROUP:(half + 1) * GROUP, :])\
              .then_inc(stored[half], 16)

        groups(sp, body)
        for half in range(2):
            sp.wait_ge(stored[half], 16 * (TT // NB) + 1)


def host_tok(x, log_dt, log_w_real, w_imag):
    import numpy as np
    dyn = np.stack([np.broadcast_to(log_dt[None, :], (NST, S)), log_w_real.T, w_imag.T], 1)
    dyn = np.ascontiguousarray(np.concatenate([dyn, dyn], 0))
    c = x.transpose(2, 1, 3, 0)
    c = np.ascontiguousarray(np.concatenate([c, c], 0))
    return dyn, c


def host_experts(w_gate, w_up, w_down, sw_gate, sw_up, sw_down):
    import numpy as np
    one = lambda a, b, c: np.concatenate([rows_on_partitions(a), rows_on_partitions(b), rows_on_partitions(c)], 1)
    parts = [one(w_gate[e], w_up[e], w_down[e]) for e in range(E)] + [one(sw_gate, sw_up, sw_down)]
    return np.ascontiguousarray(np.stack(parts))


def constants():
    import numpy as np
    mult = np.broadcast_to(np.arange(NM1, dtype=np.float32) * np.array([[1], [NM1], [NM]], np.float32), (P, 3, NM1))
    half = np.zeros((P, 8), np.float32)
    half[:64, 0], half[64:, 0] = -1, 1
    half[:64, 1], half[64:, 1] = 1, -1
    half[:64, 2] = PI / 2
    half[64:, 3] = PI / 2
    half[:, 6] = PI / 2
    inv_freq = 1.0 / 10000.0 ** (np.arange(0, HD, 2, dtype=np.float32) / np.float32(HD))
    ang = np.outer(np.arange(S, dtype=np.float32), inv_freq.astype(np.float32)).astype(np.float32)
    c, sn = np.cos(ang).T.astype(np.float32), np.sin(ang).T.astype(np.float32)
    rope0 = np.stack([np.concatenate([c, c], 0), np.concatenate([-sn, sn], 0)], 1)
    mask = np.zeros((P, 2 * P), np.float32)
    mask[:, P:] = np.triu(np.full((P, P), NEG, np.float32), 1)
    inv1 = (1.0 / 1000000.0 ** (np.arange(HD1 // 2, dtype=np.float32) / np.float32(HD1 // 2))).astype(np.float32)
    ang = np.outer(np.arange(S, dtype=np.float32), inv1).astype(np.float32)
    c, sn = np.cos(ang).astype(np.float32), np.sin(ang).astype(np.float32)
    rope1 = np.stack([np.concatenate([c, c], 1), np.concatenate([-sn, sn], 1)], 0)
    rope1 = np.ascontiguousarray(rope1.reshape(2, ST, P, HD1).transpose(2, 0, 1, 3))
    tri = np.stack([np.triu(np.ones((P, P), np.float32), 1), np.ones((P, P), np.float32)], 1)
    small = np.concatenate([np.arange(E), np.arange(SLOTS), [-0.5]]).astype(np.float32)
    tok = (np.arange(TT)[None, :] * P + np.arange(P)[:, None]).astype(np.uint32)
    return {"tri": np.ascontiguousarray(tri), "small": np.tile(small, (P, 1)), "tok": tok, "rope1": rope1,
            "identb": np.eye(P).astype(mybir.dt.np(BF16)), "mult": np.ascontiguousarray(mult), "half": half,
            "rope0": np.ascontiguousarray(rope0), "mask": mask,
            "ident": np.eye(P, dtype=np.float32)}


def rows_on_partitions(w):
    import numpy as np
    n = w.shape[1]
    return np.ascontiguousarray(w.reshape(-1, P, n).transpose(1, 0, 2).reshape(P, -1))


IN_NAMES = ["dyn", "coef", "mult", "half", "wq0", "wk0", "wv0", "wo0", "rope0", "mask", "ident", "fw", "fb", "wq1",
            "wkv1", "wo1", "bias1", "rope1", "identb", "wexp", "rms", "router", "tri", "small", "tok"]


def program(nc, a, out):
    def scratch(name, shape, dt=F32):
        return nc.dram_tensor(name, shape, dt, kind="Internal").ap()

    h0 = scratch("h0", (P, S, NM))
    h1 = scratch("h1", (B, S, D))
    h3 = scratch("h3", (B, S, D))
    token_list = scratch("token_list", (P * NL, 1), mybir.dt.uint32)
    ys = scratch("ys", (SLOTS, P, ROWS, D))
    stages_1_and_2(nc, a["dyn"], a["coef"], a["mult"], a["half"], a["wq0"], a["wk0"], a["wv0"], a["wo0"], a["rope0"],
                   a["mask"], a["ident"], h0, h1)
    block01(nc, a["fw"], a["fb"], a["wq1"], a["wkv1"], a["wo1"], a["bias1"], a["rope1"], a["mask"], a["ident"],
            a["identb"], h1, h3)
    experts(nc, a["wexp"], a["rms"], a["router"], a["tri"], a["small"], a["tok"], a["ident"], h3, token_list, ys, out)


def kernel(x, L0_tok_log_dt, L0_tok_log_w_real, L0_tok_w_imag, L0_attn_w_q, L0_attn_w_k, L0_attn_w_v, L0_attn_w_o,
           L0_ffn_weight, L0_ffn_bias, L1_attn_Wq, L1_attn_bq, L1_attn_Wk, L1_attn_bk, L1_attn_Wv, L1_attn_bv,
           L1_attn_Wo, L1_ffn_rms_weight, L1_ffn_router_w, L1_ffn_w_gate, L1_ffn_w_up, L1_ffn_w_down,
           L1_ffn_sw_gate, L1_ffn_sw_up, L1_ffn_sw_down):
    import numpy as np
    import concourse.bacc as bacc
    from concourse.bass_utils import run_bass_kernel_spmd

    arrays = constants()
    arrays["dyn"], arrays["coef"] = host_tok(np.asarray(x), np.asarray(L0_tok_log_dt), np.asarray(L0_tok_log_w_real),
                                             np.asarray(L0_tok_w_imag))
    rows = lambda w: rows_on_partitions(np.asarray(w))
    for name, w in (("wq0", L0_attn_w_q), ("wk0", L0_attn_w_k), ("wv0", L0_attn_w_v), ("wo0", L0_attn_w_o)):
        arrays[name] = rows(w)
    arrays["fw"] = rows(np.asarray(L0_ffn_weight).T)
    arrays["fb"] = np.tile(np.asarray(L0_ffn_bias), (P, 1))
    arrays["wq1"] = rows(L1_attn_Wq).reshape(P, CD, D)
    arrays["wkv1"] = rows(np.concatenate([np.asarray(L1_attn_Wk), np.asarray(L1_attn_Wv)], 1)).reshape(P, CD, 2 * P)
    arrays["wo1"] = rows(L1_attn_Wo).reshape(P, CD, D)
    arrays["bias1"] = np.concatenate([np.asarray(L1_attn_bq), np.asarray(L1_attn_bk), np.asarray(L1_attn_bv)])[None]
    arrays["wexp"] = host_experts(*[np.asarray(w) for w in (L1_ffn_w_gate, L1_ffn_w_up, L1_ffn_w_down, L1_ffn_sw_gate,
                                                            L1_ffn_sw_up, L1_ffn_sw_down)])
    arrays["rms"] = np.tile(np.asarray(L1_ffn_rms_weight), (P, 1))
    arrays["router"] = rows(L1_ffn_router_w).reshape(P, CD, E)

    nc = bacc.Bacc("TRN2", target_bir_lowering=False, num_devices=1)
    in_map, aps = {}, {}
    for name in IN_NAMES:
        a = np.ascontiguousarray(arrays[name])
        in_map[f"in_{name}"] = a
        aps[name] = nc.dram_tensor(f"in_{name}", a.shape, mybir.dt.from_np(a.dtype), kind="ExternalInput").ap()
    out = nc.dram_tensor("out", (B, S, D), F32, kind="ExternalOutput").ap()
    program(nc, aps, out)
    return run_bass_kernel_spmd(nc, [in_map], core_ids=[0]).results[0]["out"]
```
